# Optimizing a Trainium2 kernel written in Bass

```python
import numpy as np
import jax
import jax.numpy as jnp

def _softmax(x, axis=-1):
    return jax.nn.softmax(x, axis=axis)

def _gelu(x):
    return jax.nn.gelu(x, approximate=True)

def _silu(x):
    return jax.nn.silu(x)

def _sigmoid(x):
    return jax.nn.sigmoid(x)

def _layernorm(x, axis=-1, eps=1e-05):
    m = jnp.mean(x, axis=axis, keepdims=True)
    v = jnp.var(x, axis=axis, keepdims=True)
    return (x - m) / jnp.sqrt(v + eps)

def _scatter_add(tgt, idx, src, axis=0):
    return tgt.at[idx].add(src)

def _segment_sum(src, seg, n):
    return jax.ops.segment_sum(src, seg, n)
kernel_name = 'mk_gnn_resnorm_d4_gnn_r8_45e8c2'

def setup_inputs(seed: int=0):
    np.random.seed(seed)
    _w = jnp.asarray

    def _rec_inputs():
        import jax
        import jax.numpy as jnp
        _gk = jax.random.key(seed)
        x = -0.000202 + 1 * jax.random.normal(jax.random.fold_in(_gk, 1), (6250, 128), jnp.float32)
        _s = jax.random.randint(jax.random.fold_in(_gk, 2), (100000,), 0, 6250, jnp.int32)
        _d = jax.random.randint(jax.random.fold_in(_gk, 3), (100000,), 0, 6250, jnp.int32)
        _loop = jnp.arange(6250, dtype=jnp.int32)
        src = jnp.concatenate([_s, _d, _loop])
        dst = jnp.concatenate([_d, _s, _loop])
        _o = jnp.argsort(dst, stable=True)
        src = src[_o]
        dst = dst[_o]
        edge_type_8 = jax.random.randint(jax.random.fold_in(_gk, 13), (206250,), 0, 8, jnp.int32)
        edge_weight1 = jax.random.uniform(jax.random.fold_in(_gk, 14), (206250, 1), jnp.float32, 0.0, 1)
        node_vec1 = jax.random.uniform(jax.random.fold_in(_gk, 15), (6250, 1), jnp.float32, 0.0, 0.999957)
        return (x, src, dst, edge_type_8, edge_weight1, node_vec1)
    x, src, dst, edge_type_8, edge_weight1, node_vec1 = _rec_inputs()

    def _L0_gnn_setup():
        import jax, jax.numpy as jnp
        import numpy as np
        N, E, D = (6250, 100000, 128)
        BN_EPS = 1e-05
        key = jax.random.key(seed)
        ks = jax.random.split(key, 10)
        s = 1.0 / np.sqrt(D)
        return {'h': jax.random.normal(ks[0], (N, D), jnp.float32), 'mask': jax.random.uniform(ks[1], (E, 1), jnp.float32), 'snorm_n': jax.random.uniform(ks[2], (N, 1), jnp.float32), 'W1': jax.random.normal(ks[3], (D, D), jnp.float32) * s, 'b1': jnp.zeros((D,), jnp.float32), 'W2': jax.random.normal(ks[4], (D, D), jnp.float32) * s, 'b2': jnp.zeros((D,), jnp.float32), 'eps': jnp.zeros((1,), jnp.float32), 'gamma': jnp.ones((D,), jnp.float32), 'beta': jnp.zeros((D,), jnp.float32), 'src': jax.random.randint(ks[5], (E,), 0, N, jnp.int32), 'dst': jax.random.randint(ks[6], (E,), 0, N, jnp.int32)}
    _L0_gnn_all = _L0_gnn_setup()
    _L0_gnn_in = {k: v for k, v in _L0_gnn_all.items() if k in ('W1', 'b1', 'W2', 'b2', 'eps', 'gamma', 'beta')}
    del _L0_gnn_all

    def _L1_gnn_setup():
        import jax, jax.numpy as jnp
        import numpy as np
        N_NODES = 12500
        EPS = 1e-05

        def batch_norm(x, gamma, beta):
            mu = jnp.mean(x, axis=0)
            var = jnp.mean(jnp.square(x - mu), axis=0)
            return gamma * (x - mu) * jax.lax.rsqrt(var + EPS) + beta

        def gcn_conv(x, W, b, src, dst, n):
            h = x @ W
            ones = jnp.ones(src.shape[0], dtype=x.dtype)
            deg = jax.ops.segment_sum(ones, dst, num_segments=n) + 1.0
            dinv = jax.lax.rsqrt(deg)
            norm = dinv[src] * dinv[dst]
            agg = jax.ops.segment_sum(h[src] * norm[:, None], dst, num_segments=n)
            agg = agg + h * jnp.square(dinv)[:, None]
            return agg + b
        key = jax.random.key(seed)
        ks = jax.random.split(key, 8)
        c_in, hidden = (128, 128)
        n, e = (N_NODES, 75000)
        x = jax.random.normal(ks[0], (n, c_in), dtype=jnp.float32)
        edge_index = jax.random.randint(ks[1], (2, e), 0, n, dtype=jnp.int64)
        s = 1.0 / np.sqrt(c_in)
        return {'x': x, 'edge_index': edge_index, 'bn0_gamma': jnp.ones((c_in,), jnp.float32), 'bn0_beta': jnp.zeros((c_in,), jnp.float32), 'W1': jax.random.uniform(ks[2], (c_in, hidden), jnp.float32, -s, s), 'b1': jnp.zeros((hidden,), jnp.float32), 'bn1_gamma': jnp.ones((hidden,), jnp.float32), 'bn1_beta': jnp.zeros((hidden,), jnp.float32), 'W2': jax.random.uniform(ks[3], (hidden, hidden), jnp.float32, -s, s), 'b2': jnp.zeros((hidden,), jnp.float32), 'bn2_gamma': jnp.ones((hidden,), jnp.float32), 'bn2_beta': jnp.zeros((hidden,), jnp.float32)}
    _L1_gnn_all = _L1_gnn_setup()
    _L1_gnn_in = {k: v for k, v in _L1_gnn_all.items() if k in ('bn0_gamma', 'bn0_beta', 'W1', 'b1', 'bn1_gamma', 'bn1_beta', 'W2', 'b2', 'bn2_gamma', 'bn2_beta')}
    del _L1_gnn_all

    def _L2_gnn_setup():
        import jax, jax.numpy as jnp
        import numpy as np
        N, E, D, R = (6250, 75000, 128, 8)

        def rgcn_conv(x, src, dst, etype, W, root, bias):
            n = x.shape[0]
            r = W.shape[0]
            xw = jnp.einsum('nd,rdo->rno', x, W)
            seg = etype * n + dst
            counts = jax.ops.segment_sum(jnp.ones(src.shape, dtype=x.dtype), seg, num_segments=r * n)
            norm = 1.0 / jnp.maximum(counts[seg], 1.0)
            msg = xw[etype, src] * norm[:, None]
            agg = jax.ops.segment_sum(msg, dst, num_segments=n)
            return agg + x @ root + bias
        key = jax.random.key(seed)
        ks = jax.random.split(key, 16)
        s = 1.0 / np.sqrt(D)
        inp = {'x': jax.random.normal(ks[0], (N, D), dtype=jnp.float32), 'edge_index': jax.random.randint(ks[1], (2, E), 0, N, dtype=jnp.int32), 'edge_type': jax.random.randint(ks[2], (E,), 0, R, dtype=jnp.int32), 'W1': jax.random.normal(ks[3], (R, D, D), dtype=jnp.float32) * s, 'root1': jax.random.normal(ks[4], (D, D), dtype=jnp.float32) * s, 'b1': jnp.zeros((D,), dtype=jnp.float32), 'W2': jax.random.normal(ks[5], (R, D, D), dtype=jnp.float32) * s, 'root2': jax.random.normal(ks[6], (D, D), dtype=jnp.float32) * s, 'b2': jnp.zeros((D,), dtype=jnp.float32), 'W3': jax.random.normal(ks[7], (R, D, D), dtype=jnp.float32) * s, 'root3': jax.random.normal(ks[8], (D, D), dtype=jnp.float32) * s, 'b3': jnp.zeros((D,), dtype=jnp.float32), 'res_w': jax.random.normal(ks[9], (D, D), dtype=jnp.float32) * s, 'res_b': jnp.zeros((D,), dtype=jnp.float32)}
        return inp
    _L2_gnn_all = _L2_gnn_setup()
    _L2_gnn_in = {k: v for k, v in _L2_gnn_all.items() if k in ('W1', 'root1', 'b1', 'W2', 'root2', 'b2', 'W3', 'root3', 'b3', 'res_w', 'res_b')}
    del _L2_gnn_all

    def _L3_gnn_setup():
        import jax, jax.numpy as jnp
        import numpy as np
        N_NODES = 6250
        N_EDGES = 75000
        D_IN = 128
        D_OUT = 128
        LN_EPS = 1e-05
        LEAKY_SLOPE = 0.2
        key = jax.random.key(seed)
        k1, k2, k3, k4 = jax.random.split(key, 4)
        x = jax.random.normal(k1, (N_NODES, D_IN), dtype=jnp.float32)
        edge_index = jax.random.randint(k2, (2, N_EDGES), 0, N_NODES, dtype=jnp.int64)
        gain = float(np.sqrt(2.0))
        lim_w = gain * np.sqrt(6.0 / (D_IN + D_OUT))
        W_lin = jax.random.uniform(k3, (D_OUT, D_IN), minval=-lim_w, maxval=lim_w, dtype=jnp.float32)
        lim_a = gain * np.sqrt(6.0 / (2 * D_OUT + 1))
        a = jax.random.uniform(k4, (2 * D_OUT,), minval=-lim_a, maxval=lim_a, dtype=jnp.float32)
        gamma = jnp.ones((D_OUT,), dtype=jnp.float32)
        beta = jnp.zeros((D_OUT,), dtype=jnp.float32)
        return {'x': x, 'edge_index': edge_index, 'W_lin': W_lin, 'a': a, 'gamma': gamma, 'beta': beta}
    _L3_gnn_all = _L3_gnn_setup()
    _L3_gnn_in = {k: v for k, v in _L3_gnn_all.items() if k in ('W_lin', 'a', 'gamma', 'beta')}
    del _L3_gnn_all
    return {'x': x, 'src': src, 'dst': dst, 'edge_type_8': edge_type_8, 'edge_weight1': edge_weight1, 'node_vec1': node_vec1, 'L0_gnn_W1': _L0_gnn_in['W1'], 'L0_gnn_b1': _L0_gnn_in['b1'], 'L0_gnn_W2': _L0_gnn_in['W2'], 'L0_gnn_b2': _L0_gnn_in['b2'], 'L0_gnn_eps': _L0_gnn_in['eps'], 'L0_gnn_gamma': _L0_gnn_in['gamma'], 'L0_gnn_beta': _L0_gnn_in['beta'], 'L1_gnn_bn0_gamma': _L1_gnn_in['bn0_gamma'], 'L1_gnn_bn0_beta': _L1_gnn_in['bn0_beta'], 'L1_gnn_W1': _L1_gnn_in['W1'], 'L1_gnn_b1': _L1_gnn_in['b1'], 'L1_gnn_bn1_gamma': _L1_gnn_in['bn1_gamma'], 'L1_gnn_bn1_beta': _L1_gnn_in['bn1_beta'], 'L1_gnn_W2': _L1_gnn_in['W2'], 'L1_gnn_b2': _L1_gnn_in['b2'], 'L1_gnn_bn2_gamma': _L1_gnn_in['bn2_gamma'], 'L1_gnn_bn2_beta': _L1_gnn_in['bn2_beta'], 'L2_gnn_W1': _L2_gnn_in['W1'], 'L2_gnn_root1': _L2_gnn_in['root1'], 'L2_gnn_b1': _L2_gnn_in['b1'], 'L2_gnn_W2': _L2_gnn_in['W2'], 'L2_gnn_root2': _L2_gnn_in['root2'], 'L2_gnn_b2': _L2_gnn_in['b2'], 'L2_gnn_W3': _L2_gnn_in['W3'], 'L2_gnn_root3': _L2_gnn_in['root3'], 'L2_gnn_b3': _L2_gnn_in['b3'], 'L2_gnn_res_w': _L2_gnn_in['res_w'], 'L2_gnn_res_b': _L2_gnn_in['res_b'], 'L3_gnn_W_lin': _L3_gnn_in['W_lin'], 'L3_gnn_a': _L3_gnn_in['a'], 'L3_gnn_gamma': _L3_gnn_in['gamma'], 'L3_gnn_beta': _L3_gnn_in['beta']}

def reference(x, src, dst, edge_type_8, edge_weight1, node_vec1, L0_gnn_W1, L0_gnn_b1, L0_gnn_W2, L0_gnn_b2, L0_gnn_eps, L0_gnn_gamma, L0_gnn_beta, L1_gnn_bn0_gamma, L1_gnn_bn0_beta, L1_gnn_W1, L1_gnn_b1, L1_gnn_bn1_gamma, L1_gnn_bn1_beta, L1_gnn_W2, L1_gnn_b2, L1_gnn_bn2_gamma, L1_gnn_bn2_beta, L2_gnn_W1, L2_gnn_root1, L2_gnn_b1, L2_gnn_W2, L2_gnn_root2, L2_gnn_b2, L2_gnn_W3, L2_gnn_root3, L2_gnn_b3, L2_gnn_res_w, L2_gnn_res_b, L3_gnn_W_lin, L3_gnn_a, L3_gnn_gamma, L3_gnn_beta):
    import jax
    import jax.numpy as jnp

    def _L0_gnn_ref(h, mask, snorm_n, W1, b1, W2, b2, eps, gamma, beta, src, dst):
        import jax, jax.numpy as jnp
        import numpy as np
        N, E, D = (6250, 100000, 128)
        BN_EPS = 1e-05
        h_in = h
        msg = h[src] * mask
        neigh = jax.ops.segment_sum(msg, dst, num_segments=h.shape[0])
        z = (1.0 + eps) * h + neigh
        z = jax.nn.relu(z @ W1 + b1) @ W2 + b2
        z = z * snorm_n
        mu = jnp.mean(z, axis=0)
        var = jnp.var(z, axis=0)
        z = (z - mu) * jax.lax.rsqrt(var + BN_EPS) * gamma + beta
        z = jax.nn.relu(z)
        return h_in + z

    def _L1_gnn_ref(x, edge_index, bn0_gamma, bn0_beta, W1, b1, bn1_gamma, bn1_beta, W2, b2, bn2_gamma, bn2_beta):
        import jax, jax.numpy as jnp
        import numpy as np
        N_NODES = 12500
        EPS = 1e-05

        def batch_norm(x, gamma, beta):
            mu = jnp.mean(x, axis=0)
            var = jnp.mean(jnp.square(x - mu), axis=0)
            return gamma * (x - mu) * jax.lax.rsqrt(var + EPS) + beta

        def gcn_conv(x, W, b, src, dst, n):
            h = x @ W
            ones = jnp.ones(src.shape[0], dtype=x.dtype)
            deg = jax.ops.segment_sum(ones, dst, num_segments=n) + 1.0
            dinv = jax.lax.rsqrt(deg)
            norm = dinv[src] * dinv[dst]
            agg = jax.ops.segment_sum(h[src] * norm[:, None], dst, num_segments=n)
            agg = agg + h * jnp.square(dinv)[:, None]
            return agg + b
        n = x.shape[0]
        src, dst = (edge_index[0], edge_index[1])
        x_norm = batch_norm(x, bn0_gamma, bn0_beta)
        h = batch_norm(jax.nn.relu(gcn_conv(x_norm, W1, b1, src, dst, n)), bn1_gamma, bn1_beta)
        h = batch_norm(jax.nn.relu(gcn_conv(h, W2, b2, src, dst, n)), bn2_gamma, bn2_beta)
        return x_norm + h

    def _L2_gnn_ref(x, edge_index, edge_type, W1, root1, b1, W2, root2, b2, W3, root3, b3, res_w, res_b):
        import jax, jax.numpy as jnp
        import numpy as np
        N, E, D, R = (6250, 75000, 128, 8)

        def rgcn_conv(x, src, dst, etype, W, root, bias):
            n = x.shape[0]
            r = W.shape[0]
            xw = jnp.einsum('nd,rdo->rno', x, W)
            seg = etype * n + dst
            counts = jax.ops.segment_sum(jnp.ones(src.shape, dtype=x.dtype), seg, num_segments=r * n)
            norm = 1.0 / jnp.maximum(counts[seg], 1.0)
            msg = xw[etype, src] * norm[:, None]
            agg = jax.ops.segment_sum(msg, dst, num_segments=n)
            return agg + x @ root + bias
        src, dst = (edge_index[0], edge_index[1])
        res = x @ res_w + res_b
        h = jax.nn.relu(rgcn_conv(x, src, dst, edge_type, W1, root1, b1))
        h = res + jax.nn.relu(h)
        h = jax.nn.relu(rgcn_conv(h, src, dst, edge_type, W2, root2, b2))
        h = res + jax.nn.relu(h)
        h = jax.nn.relu(rgcn_conv(h, src, dst, edge_type, W3, root3, b3))
        h = res + jax.nn.relu(h)
        return h

    def _L3_gnn_ref(x, edge_index, W_lin, a, gamma, beta):
        import jax, jax.numpy as jnp
        import numpy as np
        N_NODES = 6250
        N_EDGES = 75000
        D_IN = 128
        D_OUT = 128
        LN_EPS = 1e-05
        LEAKY_SLOPE = 0.2
        N = x.shape[0]
        h = x @ W_lin.T
        d = h.shape[1]
        s_src = h @ a[:d]
        s_dst = h @ a[d:]
        src, dst = (edge_index[0], edge_index[1])
        e = jax.nn.leaky_relu(s_src[src] + s_dst[dst], LEAKY_SLOPE)
        m = jax.ops.segment_max(e, dst, num_segments=N)
        ex = jnp.exp(e - m[dst])
        z = jax.ops.segment_sum(ex, dst, num_segments=N)
        alpha = ex / z[dst]
        msgs = h[src] * alpha[:, None]
        agg = jax.ops.segment_sum(msgs, dst, num_segments=N)
        y = agg + x
        mu = jnp.mean(y, axis=-1, keepdims=True)
        var = jnp.mean(jnp.square(y - mu), axis=-1, keepdims=True)
        return (y - mu) * jax.lax.rsqrt(var + LN_EPS) * gamma + beta
    edge_index = jnp.stack([src, dst])
    x = _layernorm(x + _L0_gnn_ref(x, edge_weight1, node_vec1, L0_gnn_W1, L0_gnn_b1, L0_gnn_W2, L0_gnn_b2, L0_gnn_eps, L0_gnn_gamma, L0_gnn_beta, src, dst), axis=-1)
    x = _layernorm(x + _L1_gnn_ref(x, edge_index, L1_gnn_bn0_gamma, L1_gnn_bn0_beta, L1_gnn_W1, L1_gnn_b1, L1_gnn_bn1_gamma, L1_gnn_bn1_beta, L1_gnn_W2, L1_gnn_b2, L1_gnn_bn2_gamma, L1_gnn_bn2_beta), axis=-1)
    x = _layernorm(x + _L2_gnn_ref(x, edge_index, edge_type_8, L2_gnn_W1, L2_gnn_root1, L2_gnn_b1, L2_gnn_W2, L2_gnn_root2, L2_gnn_b2, L2_gnn_W3, L2_gnn_root3, L2_gnn_b3, L2_gnn_res_w, L2_gnn_res_b), axis=-1)
    x = _layernorm(x + _L3_gnn_ref(x, edge_index, L3_gnn_W_lin, L3_gnn_a, L3_gnn_gamma, L3_gnn_beta), axis=-1)
    return x

_drawn_inputs = setup_inputs


def setup_inputs(seed=0):
    import zlib

    import numpy as np

    out = dict(_drawn_inputs(seed))
    spreads = {'L0_gnn_b1': (0.0, 0.8),
     'L0_gnn_b2': (0.0, 0.8),
     'L0_gnn_gamma': (1.0, 0.2),
     'L0_gnn_beta': (0.0, 0.1),
     'L1_gnn_bn0_gamma': (1.0, 0.2),
     'L1_gnn_bn0_beta': (0.0, 0.1),
     'L1_gnn_b1': (0.0, 0.1),
     'L1_gnn_bn1_gamma': (1.0, 0.2),
     'L1_gnn_bn1_beta': (0.0, 0.1),
     'L1_gnn_b2': (0.0, 0.1),
     'L1_gnn_bn2_gamma': (1.0, 0.2),
     'L1_gnn_bn2_beta': (0.0, 0.1),
     'L2_gnn_b1': (0.0, 0.1),
     'L2_gnn_b2': (0.0, 0.281),
     'L2_gnn_b3': (0.0, 0.4),
     'L2_gnn_res_b': (0.0, 0.1),
     'L3_gnn_gamma': (1.0, 0.2),
     'L3_gnn_beta': (0.0, 0.1)}
    factors = {}
    for name, (base, spread) in spreads.items():
        noise = np.random.default_rng([zlib.crc32(name.encode()), seed]).standard_normal(out[name].shape)
        drawn = base * np.exp(spread * noise) if base else spread * noise
        out[name] = jnp.asarray(drawn.astype(out[name].dtype))
    for name, factor in factors.items():
        out[name] = (out[name] * factor).astype(out[name].dtype)
    return out
```

```python
import concourse.bass as bass
from concourse import mybir
from contextlib import ExitStack

F32 = mybir.dt.float32
I32 = mybir.dt.int32
U32 = mybir.dt.uint32
ALU = mybir.AluOpType
ACT = mybir.ActivationFunctionType
AX = mybir.AxisListType

P = 128
N, E, D, REL = 6250, 206250, 128, 8
TILES = -(-N // P)
NPAD = TILES * P
LAST = N - (TILES - 1) * P
UNROLL = 16
HALF = UNROLL // 2
COLS = -(-E // (P * UNROLL)) * UNROLL
LASTCOLS = E - (P - 1) * COLS
CHUNKS = -(-(E // P + TILES) // UNROLL) * UNROLL
TURNS = CHUNKS // UNROLL
WIDE = CHUNKS * 4
ACCW = NPAD + P
PER = CHUNKS // P
PSLOTS = 2
ROW = D + 2
LN_EPS = 1e-5
LEAK = 0.2
LOW = -3.0e38
BLK = 448
BLKS = NPAD // BLK
assert BLKS * BLK == NPAD and BLKS % 2 == 0


class Stage(ExitStack):

    number = 0

    def __init__(self, nc):
        super().__init__()
        self.nc, self.own = nc, []
        Stage.number += 1

    def sem(self, name):
        self.own.append(self.nc.alloc_semaphore(f"{name}_{Stage.number}"))
        return self.own[-1]

    def sems(self, *names):
        return [self.sem(name) for name in names]

    def __exit__(self, *failure):
        super().__exit__(*failure)
        if self.own:
            self.nc.clear_and_free_semaphores(self.own)
            self.nc.all_engine_barrier()


class Memory:

    def __init__(self, nc, cs):
        def sb(name, shape, dt=F32):
            return cs.enter_context(nc.sbuf_tensor(name, shape, dt))

        self.big = [sb(f"big{i}", [P, WIDE]) for i in range(5)]
        self.edge_src = sb("edge_src", [P, CHUNKS], I32)
        self.edge_dst = sb("edge_dst", [P, CHUNKS])
        self.edge_type = sb("edge_type", [P, CHUNKS])
        self.edge_w = sb("edge_w", [P, CHUNKS])
        self.tile_of = sb("tile_of", [1, CHUNKS], I32)
        self.iota = sb("iota", [P, P])
        self.part = sb("part", [P, 1])
        self.ident = sb("ident", [P, P])
        self.before = sb("before", [P, P])
        self.ones = sb("ones", [P, P])
        self.shifted = sb("shifted", [P, 2, P])
        self.seen = sb("seen", [P, HALF, 2])
        self.mean = sb("mean", [P, P])
        self.small = sb("small", [P, 512])
        self.one_eps = self.small[:, 510:511]
        self.eps = self.small[:, 511:512]
        self.rows = sb("rows", [P, UNROLL, ROW])
        self.hot = sb("hot", [P, UNROLL, P])
        self.idx = sb("idx", [P, UNROLL], I32)
        self.recs = sb("recs", [P, UNROLL, 4])
        self.psum = [cs.enter_context(nc.psum_tensor(f"ps{i}", [P, 512], F32)) for i in range(8)]
        self.gathered = [cs.enter_context(nc.semaphore(f"gathered{u}")) for u in range(UNROLL)]
        self.gathered_to = 0
        self.written = [cs.enter_context(nc.semaphore(f"written{h}")) for h in range(2)]
        self.records = nc.dram_tensor("records", [CHUNKS * P + COLS, 4], F32, kind="Internal").ap()
        self.map = nc.dram_tensor("map", [CHUNKS], I32, kind="Internal").ap()
        self.edge_row = sb("edge_row", [P, CHUNKS], I32)
        self.edge_norm = sb("edge_norm", [P, CHUNKS])
        self.turned = sb("turned", [P, 2, P])
        self.kind = sb("kind", [P, PSLOTS, REL])
        self.count = sb("count", [P, (TILES + 1) * REL])
        self.dinv = sb("dinv", [P, TILES + 1])
        self.weights = sb("weights", [P, REL * D])
        self.par = sb("par", [P, 24])
        self.bnc = sb("bnc", [P, 25 * 6 + 8])
        self.att_table = nc.dram_tensor("att_table", [NPAD, ROW], F32, kind="Internal").ap()
        self.att_rows = nc.dram_tensor("att_rows", [2 * TURNS, P, HALF * ROW], F32, kind="Internal").ap()
        self.table = nc.dram_tensor("table", [REL * NPAD, D], F32, kind="Internal").ap()


def make_constants(nc, m):
    with Stage(nc) as cs:
        made = cs.sem("made")
        block = cs.enter_context(nc.Block())

        @block.gpsimd
        def _(pool):
            pool.iota(m.iota[:, :], [[1, P]], base=0, channel_multiplier=0, allow_small_or_imprecise_dtypes=True)
            pool.iota(m.part[:, :], [[0, 1]], base=0, channel_multiplier=1, allow_small_or_imprecise_dtypes=True)
            pool.memset(m.eps, LN_EPS)
            pool.memset(m.mean[:, :], 1.0 / D)
            pool.memset(m.ones[:, :], 1.0).then_inc(made, 1)
            pool.wait_ge(made, 1)
            pool.affine_select(out=m.ident[:, :], in_=m.ones[:, :], compare_op=ALU.is_equal, fill=0.0,
                               base=0, pattern=[[-1, P]], channel_multiplier=1)
            pool.affine_select(out=m.before[:, :], in_=m.ones[:, :], compare_op=ALU.is_gt, fill=0.0,
                               base=0, pattern=[[1, P]], channel_multiplier=-1)


def load_edges(nc, m, src, dst, etype, weight):
    raw = [m.big[0][:, k * COLS:(k + 1) * COLS] for k in range(4)]
    src_i, dst_i, type_i = (r.bitcast(I32) for r in raw[:3])
    rec = m.big[1][:, 0:4 * COLS].rearrange("p (c f) -> p c f", f=4)
    bin_f = m.big[2][:, 0:COLS]
    bin_i = m.big[3][:, 0:COLS].bitcast(I32)
    place_i = m.big[3][:, COLS:2 * COLS].bitcast(I32)
    with Stage(nc) as cs:
        blank, loaded, split, built, stored = cs.sems("blank", "loaded", "split", "built", "stored")
        block = cs.enter_context(nc.Block())

        @block.sync
        def _(sp):
            sp.wait_ge(blank, 4)
            for t, f in ((dst_i, dst), (src_i, src), (type_i, etype), (raw[3], weight)):
                for a, b in ((0, 112), (112, P - 1)):
                    sp.dma_start(t[a:b, :], f[a * COLS:b * COLS].rearrange("(p c) -> p c", c=COLS)).then_inc(loaded, 16)
                sp.dma_start(t[P - 1:P, 0:LASTCOLS],
                             f[(P - 1) * COLS:E].rearrange("(p c) -> p c", p=1)).then_inc(loaded, 16)
            sp.wait_ge(built, 2)
            sp.dma_start(m.records[0:CHUNKS * P, :].rearrange("(p c) f -> p (c f)", p=P), m.big[4][:, :]).then_inc(stored, 16)
            sp.wait_ge(stored, 16)

        @block.gpsimd
        def _(pool):
            empty = m.big[4][:, :].rearrange("p (c f) -> p c f", f=4)
            pool.memset(empty[:, :, :], 0.0).then_inc(built, 1)
            pool.wait_ge(built, 1)
            pool.memset(empty[:, :, 1], -1.0).then_inc(built, 1)

        @block.vector
        def _(dve):
            dve.memset(dst_i[:, LASTCOLS:COLS], TILES * P).then_inc(blank, 1)
            dve.memset(src_i[:, LASTCOLS:COLS], 0).then_inc(blank, 1)
            dve.memset(type_i[:, LASTCOLS:COLS], 0).then_inc(blank, 1)
            dve.memset(raw[3][:, LASTCOLS:COLS], 0.0).then_inc(blank, 1)
            dve.wait_ge(loaded, 16 * 12)
            dve.tensor_scalar(bin_i, dst_i, 7, None, ALU.arith_shift_right).then_inc(split, 1)
            dve.tensor_scalar(place_i, dst_i, P - 1, None, ALU.bitwise_and).then_inc(split, 1)
            dve.tensor_copy(rec[:, :, 0].bitcast(I32), src_i)
            dve.tensor_copy(rec[:, :, 2], type_i)
            dve.tensor_copy(rec[:, :, 3], raw[3])
            dve.wait_ge(split, 2)
            dve.tensor_copy(bin_f, bin_i)
            dve.tensor_copy(rec[:, :, 1], place_i)


def sort_edges(nc, m):
    bin_f = m.big[2][:, 0:COLS]
    same = m.big[2][:, COLS:2 * COLS]
    running = m.big[2][:, 2 * COLS:3 * COLS]
    one = m.big[2][:, 3 * COLS:4 * COLS]
    slot = m.big[3][:, 0:COLS]
    slot_i = m.big[3][:, COLS:2 * COLS].bitcast(I32)
    part_i = m.big[3][:, 2 * COLS:3 * COLS].bitcast(I32)
    row_i = m.big[3][:, 3 * COLS:4 * COLS].bitcast(I32)
    picked = m.big[0][:, 0:COLS]
    behind = m.big[0][:, COLS:2 * COLS]
    rec = m.big[1][:, 0:4 * COLS].rearrange("p (c f) -> p c f", f=4)
    total = m.small[:, 0:TILES]
    first = m.small[:, 64:64 + TILES]
    need_i = m.small[:, 128:128 + TILES].bitcast(I32)
    need = m.small[:, 192:192 + TILES]
    end = m.small[:, 256:256 + TILES]
    bin_no = m.small[:, 320:320 + TILES]
    chunk_no = m.small[:, 384:384 + PER]
    map_f = m.small[:, 400:400 + PER]
    map_i = m.small[:, 416:416 + PER].bitcast(I32)
    past = m.big[0][:, 0:PER * TILES].rearrange("p (c b) -> p c b", b=TILES)
    before_ps, total_ps = m.psum[0][:, 0:TILES], m.psum[1][:, 0:TILES]

    with Stage(nc) as cs:
        made, counted, summed, step, mapped, map_out, map_in = cs.sems("made", "counted", "summed", "step", "mapped", "map_out", "map_in")
        block = cs.enter_context(nc.Block())

        @block.gpsimd
        def _(pool):
            pool.iota(bin_no, [[1, TILES]], base=0, channel_multiplier=0, allow_small_or_imprecise_dtypes=True).then_inc(made, 1)
            pool.iota(chunk_no, [[1, PER]], base=0, channel_multiplier=PER, allow_small_or_imprecise_dtypes=True).then_inc(made, 1)
            pool.iota(behind, [[1, COLS]], base=CHUNKS * P, channel_multiplier=0, allow_small_or_imprecise_dtypes=True).then_inc(made, 1)
            pool.memset(one, 1.0).then_inc(made, 1)

        @block.tensor
        def _(pe):
            pe.wait_ge(counted, TILES)
            pe.matmul(before_ps, m.before[:, :], total, start=True, stop=True).then_inc(summed, 1)
            pe.matmul(total_ps, m.ones[:, :], total, start=True, stop=True).then_inc(summed, 1)

        @block.vector
        def _(dve):
            steps = [0]

            def then(ins):
                steps[0] += 1
                ins.then_inc(step, 1)
                dve.wait_ge(step, steps[0])

            dve.wait_ge(made, 4)
            dve.memset(slot, 0.0)
            with dve.Fori(0, TILES) as b:
                dve.tensor_scalar(same, bin_f, bin_no[:, bass.ds(b, 1)], 0.0, ALU.is_equal, ALU.add,
                                  accum_out=total[:, bass.ds(b, 1)]).then_inc(counted, 1)
                dve.wait_ge(counted, b + 1)
            dve.wait_ge(summed, 2)
            then(dve.tensor_scalar(need, total_ps, float(P - 1), None, ALU.add))
            then(dve.tensor_copy(need_i, need))
            then(dve.tensor_scalar(need_i, need_i, 7, None, ALU.arith_shift_right))
            then(dve.tensor_copy(need, need_i))
            then(dve.tensor_tensor_scan(end, m.ones[:, 0:TILES], need, 0.0, ALU.mult, ALU.add))
            then(dve.tensor_tensor(first, end, need, ALU.subtract))
            then(dve.scalar_tensor_tensor(first, first, float(P), before_ps, ALU.mult, ALU.add))
            then(dve.tensor_scalar(first, first, -1.0, None, ALU.add))
            then(dve.tensor_tensor(past, chunk_no.unsqueeze(2).to_broadcast([P, PER, TILES]),
                                   end.unsqueeze(1).to_broadcast([P, PER, TILES]), ALU.is_ge))
            then(dve.tensor_reduce(map_f, past, AX.X, ALU.add))
            dve.tensor_copy(map_i, map_f).then_inc(mapped, 1)
            dve.wait_ge(mapped, 1)
            base = steps[0]
            with dve.Fori(0, TILES) as b:
                dve.tensor_scalar(same, bin_f, bin_no[:, bass.ds(b, 1)], None, ALU.is_equal).then_inc(step, 1)
                dve.wait_ge(step, 4 * b + base + 1)
                dve.tensor_tensor_scan(running, one, same, first[:, bass.ds(b, 1)], ALU.mult, ALU.add).then_inc(step, 1)
                dve.wait_ge(step, 4 * b + base + 2)
                dve.tensor_tensor(picked, same, running, ALU.mult).then_inc(step, 1)
                dve.wait_ge(step, 4 * b + base + 3)
                dve.tensor_tensor(slot, slot, picked, ALU.add).then_inc(step, 1)
                dve.wait_ge(step, 4 * b + base + 4)
            steps[0] += 4 * TILES
            then(dve.tensor_copy(slot_i, slot))
            then(dve.tensor_scalar(part_i, slot_i, P - 1, None, ALU.bitwise_and))
            then(dve.tensor_scalar(slot_i, slot_i, 7, None, ALU.arith_shift_right))
            then(dve.tensor_copy(slot, slot_i))
            then(dve.tensor_copy(picked, part_i))
            then(dve.scalar_tensor_tensor(slot, picked, float(CHUNKS), slot, ALU.mult, ALU.add))
            then(dve.scalar_tensor_tensor(same, bin_f, float(TILES), behind, ALU.is_ge, ALU.mult))
            then(dve.tensor_tensor(slot, slot, same, ALU.add))
            then(dve.tensor_copy(row_i, slot))

        @block.sync
        def _(sp):
            sp.wait_ge(mapped, 1)
            sp.dma_start(m.map.rearrange("(p c) -> p c", p=P), map_i).then_inc(map_out, 16)
            sp.wait_ge(map_out, 16)
            sp.dma_start(m.tile_of[0:1, :], m.map.rearrange("(p c) -> p c", p=1)).then_inc(map_in, 16)
            sp.wait_ge(map_in, 16)

    with Stage(nc) as cs:
        staged, begun = cs.sems("staged", "begun")
        written = m.written
        block = cs.enter_context(nc.Block())

        @block.scalar
        def _(act):
            def stage(i, h):
                act.copy(m.idx[:, h * HALF:(h + 1) * HALF], row_i[:, bass.ds(i * UNROLL + h * HALF, HALF)]).then_inc(staged, 1)
                act.copy(m.recs[:, h * HALF:(h + 1) * HALF, :], rec[:, bass.ds(i * UNROLL + h * HALF, HALF), :]).then_inc(staged, 1)

            stage(0, 0)
            stage(0, 1)
            with act.Fori(1, COLS // UNROLL) as i:
                for h in range(2):
                    act.wait_ge(written[h], 16 * HALF * i)
                    stage(i, h)
            for h in range(2):
                act.wait_ge(written[h], 16 * HALF * (COLS // UNROLL))

        @block.gpsimd
        def _(pool):
            with pool.Fori(0, COLS // UNROLL) as i:
                for h in range(2):
                    pool.wait_ge(staged, 4 * i + 2 * h + 2)
                    pool.sem_inc(begun, 1)
                    for u in range(h * HALF, (h + 1) * HALF):
                        pool.indirect_dma_start(m.records, bass.IndirectOffsetOnAxis(ap=m.idx[:, u:u + 1].bitcast(U32), axis=0),
                                                m.recs[:, u, :], None).then_inc(written[h], 16)

    with Stage(nc) as cs:
        back = cs.sem("back")
        block = cs.enter_context(nc.Block())
        rec = m.big[0][:, :].rearrange("p (c f) -> p c f", f=4)

        @block.sync
        def _(sp):
            sp.dma_start(m.big[0][:, :], m.records[0:CHUNKS * P, :].rearrange("(p c) f -> p (c f)", p=P)).then_inc(back, 16)

        @block.vector
        def _(dve):
            dve.wait_ge(back, 16)
            dve.tensor_copy(m.edge_src[:, :], rec[:, :, 0].bitcast(I32))
            dve.tensor_copy(m.edge_dst[:, :], rec[:, :, 1])

        @block.scalar
        def _(act):
            act.wait_ge(back, 16)
            act.copy(m.edge_type[:, :], rec[:, :, 2])
            act.copy(m.edge_w[:, :], rec[:, :, 3])

    with Stage(nc) as cs:
        done = cs.sem("done")
        block = cs.enter_context(nc.Block())
        src_f, row_f = m.big[1][:, 0:CHUNKS], m.big[1][:, CHUNKS:2 * CHUNKS]

        @block.vector
        def _(dve):
            dve.tensor_copy(src_f, m.edge_src[:, :]).then_inc(done, 1)
            dve.wait_ge(done, 1)
            dve.scalar_tensor_tensor(row_f, m.edge_type[:, :], float(NPAD), src_f, ALU.mult, ALU.add).then_inc(done, 1)
            dve.wait_ge(done, 2)
            dve.tensor_copy(m.edge_row[:, :], row_f)



def gather_sum(nc, m, table, rows_of, acc, weight=None, scale_rows=None, count=False, norm=False):
    with Stage(nc) as cs:
        staged, begun, ready, product, added = cs.sems("staged", "begun", "ready", "product", "added")
        scaled, counted, typed, turned, copied, looked, found, mine = cs.sems("scaled", "counted", "typed", "turned", "copied", "looked", "found", "mine")
        gathered, before = m.gathered, m.gathered_to
        m.gathered_to += 16 * TURNS
        block = cs.enter_context(nc.Block())
        side = m.psum[4:4 + PSLOTS]
        turn_ps = m.psum[6:8]

        @block.scalar
        def _(act):
            with act.Fori(0, TURNS) as i:
                for u in range(UNROLL):
                    if u % HALF == 0:
                        act.wait_ge(product, i * UNROLL + u + HALF)
                        act.copy(m.idx[:, u:u + HALF], rows_of[:, bass.ds(i * UNROLL + u, HALF)]).then_inc(staged, 1)
                    if scale_rows is not None:
                        act.wait_ge(gathered[u], before + 16 * (i + 1))
                        act.activation(m.rows[:, u, 0:D], m.rows[:, u, 0:D], ACT.Copy,
                                       scale=scale_rows[:, bass.ds(i * UNROLL + u, 1)]).then_inc(scaled, 1)
                    if norm:
                        act.wait_ge(turned, i * UNROLL + u + 1)
                        act.wait_ge(looked, i * UNROLL + u + 1)
                        act.copy(m.turned[:, u % 2, :], turn_ps[u % 2][:, 0:P]).then_inc(copied, 1)

        @block.gpsimd
        def _(pool):
            with pool.Fori(0, TURNS) as i:
                for h in range(2):
                    pool.wait_ge(staged, 2 * i + h + 1)
                    pool.sem_inc(begun, 1)
                    for u in range(h * HALF, (h + 1) * HALF):
                        pool.indirect_dma_start(m.rows[:, u, 0:D], None, table,
                                                bass.IndirectOffsetOnAxis(ap=m.idx[:, u:u + 1].bitcast(U32), axis=0),
                                                ).then_inc(gathered[u], 16)

        @block.tensor
        def _(pe):
            pe.sem_inc(product, UNROLL)
            pe.sem_inc(added, PSLOTS)
            pe.sem_inc(counted, PSLOTS)
            pe.sem_inc(looked, 2)
            pe.sem_inc(found, PSLOTS)
            pe.sem_inc(copied, 2)
            with pe.Fori(0, TURNS) as i:
                if norm:
                    _, tiles = nc.values_load_multi_w_load_instructions(
                        m.tile_of[0:1, bass.ds(i * UNROLL, UNROLL)], engines=[pe.engine], min_val=0, max_val=TILES,
                        skip_runtime_bounds_check_because="a chunk's tile counts bins, of which there are TILES")

                def look_up(u):
                    pe.wait_ge(copied, 2 + i * UNROLL + u + 1)
                    pe.wait_ge(found, i * UNROLL + u + 1)
                    pe.matmul(side[u % PSLOTS][:, 0:REL], m.turned[:, u % 2, :], m.count[:, bass.ds(tiles[u] * REL, REL)],
                              start=True, stop=True).then_inc(looked, 1)

                for u in range(UNROLL):
                    pe.wait_ge(ready, i * UNROLL + u + 1)
                    if norm:
                        pe.wait_ge(copied, i * UNROLL + u + 1)
                        pe.transpose(turn_ps[u % 2][:, 0:P], m.hot[:, u, :], m.ident[:, :]).then_inc(turned, 1)
                    if scale_rows is None:
                        pe.wait_ge(gathered[u], before + 16 * (i + 1))
                    else:
                        pe.wait_ge(scaled, i * UNROLL + u + 1)
                    if count:
                        pe.wait_ge(typed, i * UNROLL + u + 1)
                        pe.wait_ge(counted, i * UNROLL + u + 1)
                        pe.matmul(side[u % PSLOTS][:, 0:REL], m.hot[:, u, :], m.kind[:, u % PSLOTS, :],
                                  start=True, stop=True).then_inc(mine, 1)
                    pe.wait_ge(added, i * UNROLL + u + 1)
                    pe.matmul(m.psum[u % PSLOTS][:, 0:P], m.rows[:, u, 0:D], m.hot[:, u, :],
                              start=True, stop=True).then_inc(product, 1)
                    if norm:
                        look_up(u)

        @block.vector
        def _(dve):
            with dve.Fori(0, TURNS) as i:
                _, tiles = nc.values_load_multi_w_load_instructions(
                    m.tile_of[0:1, bass.ds(i * UNROLL, UNROLL)], engines=[dve.engine], min_val=0, max_val=TILES,
                    skip_runtime_bounds_check_because="a chunk's tile counts bins, of which there are TILES")

                def add(u):
                    if norm:
                        dve.wait_ge(looked, 2 + i * UNROLL + u + 1)
                        dve.scalar_tensor_tensor(m.kind[:, u % PSLOTS, :], m.iota[:, 0:REL], m.edge_type[:, bass.ds(i * UNROLL + u, 1)],
                                                 side[u % PSLOTS][:, 0:REL], ALU.is_equal, ALU.mult,
                                                 accum_out=m.edge_norm[:, bass.ds(i * UNROLL + u, 1)]).then_inc(found, 1)
                    if count:
                        dve.wait_ge(mine, i * UNROLL + u + 1)
                        dve.wait_ge(counted, PSLOTS + i * UNROLL + u)
                        at = m.count[:, bass.ds(tiles[u] * REL, REL)]
                        dve.tensor_tensor(at, at, side[u % PSLOTS][:, 0:REL], ALU.add).then_inc(counted, 1)
                    dve.wait_ge(product, (i + 1) * UNROLL + u + 1)
                    dve.wait_ge(added, PSLOTS + i * UNROLL + u)
                    at = acc[:, bass.ds(tiles[u] * P, P)]
                    dve.tensor_tensor(at, at, m.psum[u % PSLOTS][:, 0:P], ALU.add).then_inc(added, 1)

                for u in range(UNROLL):
                    c = i * UNROLL + u
                    dve.wait_ge(product, c + 1)
                    if count:
                        dve.wait_ge(product, c + UNROLL - 1)
                        dve.tensor_scalar(m.kind[:, u % PSLOTS, :], m.iota[:, 0:REL], m.edge_type[:, bass.ds(c, 1)], None,
                                          ALU.is_equal).then_inc(typed, 1)
                    if norm:
                        dve.wait_ge(looked, c + 1)
                    if weight is None:
                        dve.tensor_scalar(m.hot[:, u, :], m.iota[:, :], m.edge_dst[:, bass.ds(c, 1)], None,
                                          ALU.is_equal).then_inc(ready, 1)
                    else:
                        dve.tensor_scalar(m.hot[:, u, :], m.iota[:, :], m.edge_dst[:, bass.ds(c, 1)],
                                          weight[:, bass.ds(c, 1)], ALU.is_equal, ALU.mult).then_inc(ready, 1)
                    if u >= 1:
                        add(u - 1)
                add(UNROLL - 1)


def linear(nc, m, w, x, out, func=ACT.Identity, bias=0.0, times=None):
    with Stage(nc) as cs:
        product, taken = cs.sems("product", "taken")
        block = cs.enter_context(nc.Block())

        @block.tensor
        def _(pe):
            pe.sem_inc(taken, 2)
            with pe.Fori(0, BLKS // 2) as j:
                for k in range(2):
                    pe.wait_ge(taken, 2 * j + k + 1)
                    pe.matmul(m.psum[k][:, 0:BLK], w, x[:, bass.ds((2 * j + k) * BLK, BLK)],
                              start=True, stop=True).then_inc(product, 1)

        @block.scalar
        def _(act):
            with act.Fori(0, BLKS // 2) as j:
                for k in range(2):
                    act.wait_ge(product, 2 * j + k + 1)
                    act.activation(out[:, bass.ds((2 * j + k) * BLK, BLK)], m.psum[k][:, 0:BLK], func,
                                   bias=bias).then_inc(taken, 1)

        if times is not None:
            @block.vector
            def _(dve):
                with dve.Fori(0, BLKS // 2) as j:
                    for k in range(2):
                        dve.wait_ge(taken, 2 * j + k + 3)
                        at = out[:, bass.ds((2 * j + k) * BLK, BLK)]
                        dve.tensor_tensor(at, at, times[:, bass.ds((2 * j + k) * BLK, BLK)], ALU.mult)



SETS = 4


def write_table(nc, m, x, width, stage, store, scale=None):
    step = min(width, 512)
    banks = width // step
    with Stage(nc) as cs:
        held, product, taken = cs.sems("held", "product", "taken")
        stored = [cs.sem(f"stored{k}") for k in range(SETS)]
        block = cs.enter_context(nc.Block())
        turns = TILES // SETS
        assert turns * SETS + 1 == TILES

        @block.vector
        def _(dve):
            def tile(j, k):
                dve.wait_ge(product, (j * SETS + k + 1) * banks)
                dve.tensor_copy(m.hot[:, k, :], x[:, bass.ds((j * SETS + k) * P, P)]).then_inc(held, 1)

            dve.sem_inc(product, SETS * banks)
            with dve.Fori(0, turns) as j:
                for k in range(SETS):
                    tile(j, k)
            tile(turns, 0)

        @block.tensor
        def _(pe):
            def tile(j, k):
                pe.wait_ge(held, j * SETS + k + 1)
                for h in range(banks):
                    pe.wait_ge(taken, (j * SETS + k) * banks + h + 1)
                    pe.matmul(m.psum[k * banks + h][:, 0:step], m.hot[:, k, :],
                              m.weights[:, h * step:(h + 1) * step], start=True, stop=True).then_inc(product, 1)

            pe.sem_inc(taken, SETS * banks)
            with pe.Fori(0, turns) as j:
                for k in range(SETS):
                    tile(j, k)
            tile(turns, 0)

        @block.scalar
        def _(act):
            def tile(j, k):
                for h in range(banks):
                    act.wait_ge(product, (SETS + j * SETS + k) * banks + h + 1)
                    act.activation(stage(k)[:, h * step:(h + 1) * step], m.psum[k * banks + h][:, 0:step], ACT.Copy,
                                   scale=1.0 if scale is None else scale[:, bass.ds(j * SETS + k, 1)]).then_inc(taken, 1)

            for k in range(SETS):
                tile(0, k)
            with act.Fori(1, turns) as j:
                for k in range(SETS):
                    act.wait_ge(stored[k], 16 * j)
                    tile(j, k)
            act.wait_ge(stored[0], 16 * turns)
            tile(turns, 0)

        @block.sync
        def _(sp):
            def tile(j, k):
                sp.wait_ge(taken, (SETS + j * SETS + k + 1) * banks)
                sp.dma_start(store(j * SETS + k), stage(k)).then_inc(stored[k], 16)

            with sp.Fori(0, turns) as j:
                for k in range(SETS):
                    tile(j, k)
            tile(turns, 0)
            sp.wait_ge(stored[0], 16 * (turns + 1))
            for k in range(1, SETS):
                sp.wait_ge(stored[k], 16 * turns)


def batch_norm(nc, m, x, out, gamma, beta, func=ACT.Identity):
    cut = 250
    parts = N // cut
    assert parts * cut == N
    stats = m.bnc[:, 0:6 * parts]
    mv, std, rstd, scale, shift = (m.bnc[:, 6 * parts + o:6 * parts + o + n] for o, n in ((0, 2), (2, 1), (3, 1), (4, 1), (5, 1)))
    with Stage(nc) as cs:
        step, rooted, ready = cs.sems("step", "rooted", "ready")
        block = cs.enter_context(nc.Block())

        @block.vector
        def _(dve):
            with dve.Fori(0, parts) as j:
                dve.bn_stats(stats[:, bass.ds(j * 6, 6)], x[:, bass.ds(j * cut, cut)]).then_inc(step, 1)
            dve.wait_ge(step, parts)
            dve.bn_aggr(mv, stats).then_inc(step, 1)
            dve.wait_ge(rooted, 1)
            dve.reciprocal(rstd, std).then_inc(step, 1)
            dve.wait_ge(step, parts + 2)
            dve.tensor_tensor(scale, gamma, rstd, ALU.mult).then_inc(step, 1)
            dve.wait_ge(step, parts + 3)
            dve.tensor_tensor(shift, scale, mv[:, 0:1], ALU.mult).then_inc(step, 1)
            dve.wait_ge(step, parts + 4)
            dve.tensor_tensor(shift, beta, shift, ALU.subtract).then_inc(ready, 1)

        @block.scalar
        def _(act):
            act.wait_ge(step, parts + 1)
            act.activation(std, mv[:, 1:2], ACT.Sqrt, bias=m.eps).then_inc(rooted, 1)
            act.wait_ge(ready, 1)
            act.activation(out[:, 0:NPAD], x[:, 0:NPAD], func, bias=shift, scale=scale)


def combine(nc, m, parts):
    with Stage(nc) as cs:
        step = cs.sem("step")
        block = cs.enter_context(nc.Block())

        @block.vector
        def _(dve):
            for n, (out, in0, scalar, in1, op0, op1) in enumerate(parts):
                if n:
                    dve.wait_ge(step, n)
                dve.scalar_tensor_tensor(out, in0, scalar, in1, op0, op1).then_inc(step, 1)


def layer_norm(nc, m, x, out, tmp):
    with Stage(nc) as cs:
        mean, centred, squared, var, rooted, inverse, done = cs.sems("mean", "centred", "squared", "var", "rooted", "inverse", "done")
        block = cs.enter_context(nc.Block())
        sq = [tmp[:, k * BLK:(k + 1) * BLK] for k in range(2)]
        std = [tmp[:, (2 + k) * BLK:(3 + k) * BLK] for k in range(2)]
        at = lambda a, j, k: a[:, bass.ds((2 * j + k) * BLK, BLK)]

        @block.tensor
        def _(pe):
            pe.sem_inc(centred, 2)
            pe.sem_inc(rooted, 2)
            with pe.Fori(0, BLKS // 2) as j:
                for k in range(2):
                    pe.wait_ge(centred, 2 * j + k + 1)
                    pe.matmul(m.psum[k][:, 0:BLK], m.mean[:, :], at(x, j, k), start=True, stop=True).then_inc(mean, 1)
                for k in range(2):
                    pe.wait_ge(squared, 2 * j + k + 1)
                    pe.wait_ge(rooted, 2 * j + k + 1)
                    pe.matmul(m.psum[2 + k][:, 0:BLK], m.mean[:, :], sq[k], start=True, stop=True).then_inc(var, 1)

        @block.vector
        def _(dve):
            with dve.Fori(0, BLKS // 2) as j:
                for k in range(2):
                    dve.wait_ge(mean, 2 * j + k + 1)
                    dve.tensor_tensor(at(x, j, k), at(x, j, k), m.psum[k][:, 0:BLK], ALU.subtract).then_inc(centred, 1)
                for k in range(2):
                    dve.wait_ge(rooted, 2 * j + k + 3)
                    dve.reciprocal(std[k], std[k]).then_inc(inverse, 1)
                    dve.wait_ge(inverse, 2 * j + k + 1)
                    dve.tensor_tensor(at(out, j, k), at(x, j, k), std[k], ALU.mult).then_inc(done, 1)

        @block.scalar
        def _(act):
            act.sem_inc(done, 2)
            with act.Fori(0, BLKS // 2) as j:
                for k in range(2):
                    act.wait_ge(centred, 2 * j + k + 3)
                    act.wait_ge(rooted, 2 * j + k + 1)
                    act.activation(sq[k], at(x, j, k), ACT.Square).then_inc(squared, 1)
                for k in range(2):
                    act.wait_ge(var, 2 * j + k + 1)
                    act.wait_ge(done, 2 * j + k + 1)
                    act.activation(std[k], m.psum[2 + k][:, 0:BLK], ACT.Sqrt, bias=m.eps).then_inc(rooted, 1)


def turn_tiles(nc, m, source, target):
    with Stage(nc) as cs:
        held, turned, taken = cs.sems("held", "turned", "taken")
        block = cs.enter_context(nc.Block())
        group = 7
        assert group * group == TILES

        @block.vector
        def _(dve):
            dve.sem_inc(turned, group)
            with dve.Fori(0, group) as j:
                for k in range(group):
                    dve.wait_ge(turned, j * group + k + 1)
                    dve.tensor_copy(m.hot[:, k, :], source[:, bass.ds((j * group + k) * P, P)]).then_inc(held, 1)

        @block.tensor
        def _(pe):
            pe.sem_inc(taken, group)
            with pe.Fori(0, group) as j:
                for k in range(group):
                    pe.wait_ge(held, j * group + k + 1)
                    pe.wait_ge(taken, j * group + k + 1)
                    pe.transpose(m.psum[k][:, 0:P], m.hot[:, k, :], m.ident[:, :]).then_inc(turned, 1)

        @block.scalar
        def _(act):
            with act.Fori(0, group) as j:
                for k in range(group):
                    act.wait_ge(turned, group + j * group + k + 1)
                    act.copy(target[:, bass.ds((j * group + k) * P, P)], m.psum[k][:, 0:P]).then_inc(taken, 1)


def load_vectors(nc, m, a):
    with Stage(nc) as cs:
        clear, loaded, done = cs.sems("clear", "loaded", "done")
        block = cs.enter_context(nc.Block())
        full = TILES - 1
        x_rows = m.big[4][:, 0:NPAD].rearrange("p (t d) -> p t d", d=D)
        w_nodes = m.big[3]

        @block.vector
        def _(dve):
            dve.memset(x_rows[:, full, :], 0.0).then_inc(clear, 1)
            dve.wait_ge(loaded, 16 * (len(VECTORS) + 1))
            dve.tensor_scalar(m.one_eps, m.one_eps, 1.0, None, ALU.add)

        @block.sync
        def _(sp):
            with nc.allow_non_contiguous_dma("a word to a partition"):
                for n, name in enumerate(VECTORS):
                    sp.dma_start(m.par[:, n:n + 1], a[name].rearrange("(p o) -> p o", o=1)).then_inc(loaded, 16)
                sp.dma_start(m.one_eps, a["L0_gnn_eps"].rearrange("(p o) -> p o", o=1).to_broadcast([P, 1])).then_inc(loaded, 16)
            sp.dma_start(x_rows[:, 0:full, :], a["x"][0:full * P, :].rearrange("(t p) d -> p t d", p=P)).then_inc(done, 16)
            sp.wait_ge(clear, 1)
            sp.dma_start(x_rows[0:LAST, full, :], a["x"][full * P:N, :]).then_inc(done, 16)
            sp.wait_ge(done, 32)


def load(nc, m, pairs, zero=()):
    with Stage(nc) as cs:
        loaded = cs.sem("loaded")
        block = cs.enter_context(nc.Block())

        @block.sync
        def _(sp):
            for out, in_ in pairs:
                sp.dma_start(out, in_).then_inc(loaded, 16)
            if pairs:
                sp.wait_ge(loaded, 16 * len(pairs))

        if zero:
            @block.vector
            def _(dve):
                for z in zero:
                    dve.memset(z, 0.0)


def degrees(nc, m, wide):
    with Stage(nc) as cs:
        step, rooted, spread, product, taken = cs.sems("step", "rooted", "spread", "product", "taken")
        block = cs.enter_context(nc.Block())
        group = 7
        assert group * group == TILES

        @block.vector
        def _(dve):
            dve.tensor_reduce(m.dinv[:, :], m.count[:, :].rearrange("p (t r) -> p t r", r=REL), AX.X, ALU.add).then_inc(step, 1)
            dve.wait_ge(step, 1)
            dve.tensor_scalar(m.count[:, :], m.count[:, :], 1.0, None, ALU.max).then_inc(step, 1)
            dve.wait_ge(step, 2)
            dve.reciprocal(m.count[:, :], m.count[:, :])
            dve.wait_ge(rooted, 1)
            dve.reciprocal(m.dinv[:, :], m.dinv[:, :]).then_inc(step, 1)
            dve.wait_ge(step, 3)
            dve.sem_inc(product, group)
            with dve.Fori(0, group) as j:
                for k in range(group):
                    dve.wait_ge(product, j * group + k + 1)
                    dve.tensor_scalar(m.hot[:, k, :], m.ident[:, :], m.dinv[:, bass.ds(j * group + k, 1)], None,
                                      ALU.mult).then_inc(spread, 1)

        @block.scalar
        def _(act):
            act.wait_ge(step, 1)
            act.activation(m.dinv[:, :], m.dinv[:, :], ACT.Sqrt, bias=1.0).then_inc(rooted, 1)
            with act.Fori(0, group) as j:
                for k in range(group):
                    act.wait_ge(product, group + j * group + k + 1)
                    act.copy(wide[:, bass.ds((j * group + k) * P, P)], m.psum[k][:, 0:P]).then_inc(taken, 1)

        @block.tensor
        def _(pe):
            pe.sem_inc(taken, group)
            with pe.Fori(0, group) as j:
                for k in range(group):
                    pe.wait_ge(spread, j * group + k + 1)
                    pe.wait_ge(taken, j * group + k + 1)
                    pe.matmul(m.psum[k][:, 0:P], m.ones[:, :], m.hot[:, k, :], start=True, stop=True).then_inc(product, 1)



def attention_table(nc, m, x, stage, target_score):
    turns = TILES // SETS
    a_source, a_target = m.weights[:, 2 * D:3 * D], m.weights[:, 3 * D:4 * D]
    with Stage(nc) as cs:
        held, product, taken, scored = cs.sems("held", "product", "taken", "scored")
        stored = [cs.sem(f"stored{k}") for k in range(SETS)]
        block = cs.enter_context(nc.Block())

        @block.vector
        def _(dve):
            def hold(j, k):
                dve.wait_ge(product, j * SETS + k + 1)
                dve.tensor_copy(m.hot[:, k, :], x[:, bass.ds((j * SETS + k) * P, P)]).then_inc(held, 1)

            def score(j, k):
                dve.wait_ge(taken, SETS + j * SETS + k + 1)
                dve.scalar_tensor_tensor(m.hot[:, SETS + k, :], stage(k)[:, 0:D], 1.0, a_source, ALU.mult, ALU.mult,
                                         accum_out=stage(k)[:, D:D + 1]).then_inc(scored, 1)
                dve.scalar_tensor_tensor(m.hot[:, 2 * SETS + k, :], stage(k)[:, 0:D], 1.0, a_target, ALU.mult, ALU.mult,
                                         accum_out=target_score[:, bass.ds(j * SETS + k, 1)]).then_inc(scored, 1)

            dve.sem_inc(product, SETS)
            with dve.Fori(0, turns) as j:
                for k in range(SETS):
                    hold(j, k)
                for k in range(SETS):
                    score(j, k)
                dve.wait_ge(scored, 2 * SETS * (j + 1))
            hold(turns, 0)
            score(turns, 0)

        @block.tensor
        def _(pe):
            def tile(j, k):
                pe.wait_ge(held, j * SETS + k + 1)
                pe.wait_ge(taken, j * SETS + k + 1)
                pe.matmul(m.psum[k][:, 0:D], m.hot[:, k, :], m.weights[:, D:2 * D], start=True, stop=True).then_inc(product, 1)

            pe.sem_inc(taken, SETS)
            with pe.Fori(0, turns) as j:
                for k in range(SETS):
                    tile(j, k)
            tile(turns, 0)

        @block.scalar
        def _(act):
            def tile(j, k):
                act.wait_ge(product, SETS + j * SETS + k + 1)
                act.copy(stage(k)[:, 0:D], m.psum[k][:, 0:D]).then_inc(taken, 1)

            for k in range(SETS):
                tile(0, k)
            with act.Fori(1, turns) as j:
                for k in range(SETS):
                    act.wait_ge(stored[k], 16 * j)
                    tile(j, k)
            act.wait_ge(stored[0], 16 * turns)
            tile(turns, 0)

        @block.sync
        def _(sp):
            def tile(j, k):
                sp.wait_ge(scored, 2 * (j * SETS + k + 1))
                sp.dma_start(m.att_table[bass.ds((j * SETS + k) * P, P), :], stage(k)).then_inc(stored[k], 16)

            with sp.Fori(0, turns) as j:
                for k in range(SETS):
                    tile(j, k)
            tile(turns, 0)
            sp.wait_ge(stored[0], 16 * (turns + 1))
            for k in range(1, SETS):
                sp.wait_ge(stored[k], 16 * turns)


def gather_max(nc, m, top):
    with Stage(nc) as cs:
        staged, begun, ready, shifted, turned, found, top_of = cs.sems(
            "staged", "begun", "ready", "shifted", "turned", "found", "top_of")
        kept = [cs.sem(f"kept{h}") for h in range(2)]
        gathered, before = m.gathered, m.gathered_to
        m.gathered_to += 16 * TURNS
        block = cs.enter_context(nc.Block())
        turn_ps = m.psum[0:2]

        @block.scalar
        def _(act):
            def stage(i, h):
                act.copy(m.idx[:, h * HALF:(h + 1) * HALF], m.edge_src[:, bass.ds(i * UNROLL + h * HALF, HALF)]).then_inc(staged, 1)

            def shift(i, u):
                act.wait_ge(ready, i * UNROLL + u + 1)
                act.wait_ge(gathered[u], before + 16 * (i + 1))
                act.wait_ge(turned, i * UNROLL + u + 1)
                act.activation(m.shifted[:, u % 2, :], m.hot[:, u, :], ACT.Identity, bias=m.rows[:, u, D:D + 1]).then_inc(shifted, 1)

            stage(0, 0)
            stage(0, 1)
            with act.Fori(0, TURNS - 1) as i:
                for h in range(2):
                    for u in range(h * HALF, (h + 1) * HALF):
                        shift(i, u)
                    act.wait_ge(kept[h], 16 * (i + 1))
                    act.wait_ge(shifted, i * UNROLL + (h + 1) * HALF)
                    stage(i + 1, h)
            for u in range(UNROLL):
                shift(TURNS - 1, u)

        @block.gpsimd
        def _(pool):
            with pool.Fori(0, TURNS) as i:
                for h in range(2):
                    pool.wait_ge(staged, 2 * i + h + 1)
                    pool.sem_inc(begun, 1)
                    for u in range(h * HALF, (h + 1) * HALF):
                        pool.indirect_dma_start(m.rows[:, u, :], None, m.att_table,
                                                bass.IndirectOffsetOnAxis(ap=m.idx[:, u:u + 1].bitcast(U32), axis=0),
                                                ).then_inc(gathered[u], 16)

        @block.sync
        def _(sp):
            with sp.Fori(0, TURNS) as i:
                for h in range(2):
                    for u in range(h * HALF, (h + 1) * HALF):
                        sp.wait_ge(gathered[u], before + 16 * (i + 1))
                    sp.dma_start(m.att_rows[bass.ds(i * 2 + h, 1), :, :].rearrange("o p f -> (o p) f"),
                                 m.rows[:, h * HALF:(h + 1) * HALF, :].rearrange("p u f -> p (u f)")).then_inc(kept[h], 16)
            for h in range(2):
                sp.wait_ge(kept[h], 16 * TURNS)

        @block.tensor
        def _(pe):
            pe.sem_inc(turned, 2)
            pe.sem_inc(found, 2)
            with pe.Fori(0, TURNS) as i:
                for u in range(UNROLL):
                    pe.wait_ge(shifted, i * UNROLL + u + 1)
                    pe.wait_ge(found, i * UNROLL + u + 1)
                    pe.transpose(turn_ps[u % 2][:, 0:P], m.shifted[:, u % 2, :], m.ident[:, :]).then_inc(turned, 1)

        @block.vector
        def _(dve):
            dve.sem_inc(top_of, 1)
            with dve.Fori(0, TURNS) as i:
                _, tiles = nc.values_load_multi_w_load_instructions(
                    m.tile_of[0:1, bass.ds(i * UNROLL, UNROLL)], engines=[dve.engine], min_val=0, max_val=TILES,
                    skip_runtime_bounds_check_because="a chunk's tile counts bins, of which there are TILES")

                def reduce(u):
                    dve.wait_ge(turned, 2 + i * UNROLL + u + 1)
                    dve.tensor_reduce(m.seen[:, u % HALF, 0:1], turn_ps[u % 2][:, 0:P], AX.X, ALU.max).then_inc(found, 1)
                    dve.wait_ge(found, 2 + i * UNROLL + u + 1)
                    dve.wait_ge(top_of, i * UNROLL + u + 1)
                    at = top[:, bass.ds(tiles[u], 1)]
                    dve.tensor_tensor(at, at, m.seen[:, u % HALF, 0:1], ALU.max).then_inc(top_of, 1)

                for u in range(UNROLL):
                    dve.tensor_scalar(m.hot[:, u, :], m.iota[:, :], m.edge_dst[:, bass.ds(i * UNROLL + u, 1)], LOW,
                                      ALU.not_equal, ALU.mult).then_inc(ready, 1)
                    if u >= 2:
                        reduce(u - 2)
                reduce(UNROLL - 2)
                reduce(UNROLL - 1)


def attend(nc, m, acc):
    with Stage(nc) as cs:
        ready, turned, copied, looked, seen, raw, powered, weighted, product, added, step = cs.sems(
            "ready", "turned", "copied", "looked", "seen", "raw", "powered", "weighted", "product", "added", "step")
        loaded = [cs.sem(f"loaded{h}") for h in range(2)]
        block = cs.enter_context(nc.Block())
        turn_ps, side, sums = m.psum[0:2], m.psum[2:4], m.psum[4:6]
        power = m.small[:, 480:480 + UNROLL]
        leaky = m.small[:, 496:496 + HALF]

        def tiles_of(engine, i):
            _, tiles = nc.values_load_multi_w_load_instructions(
                m.tile_of[0:1, bass.ds(i * UNROLL, UNROLL)], engines=[engine.engine], min_val=0, max_val=TILES,
                skip_runtime_bounds_check_because="a chunk's tile counts bins, of which there are TILES")
            return tiles

        @block.sync
        def _(sp):
            with sp.Fori(0, TURNS) as i:
                for h in range(2):
                    sp.wait_ge(product, i * UNROLL + (h + 1) * HALF)
                    sp.dma_start(m.rows[:, h * HALF:(h + 1) * HALF, :].rearrange("p u f -> p (u f)"),
                                 m.att_rows[bass.ds(i * 2 + h, 1), :, :].rearrange("o p f -> (o p) f")).then_inc(loaded[h], 16)

        @block.tensor
        def _(pe):
            pe.sem_inc(product, UNROLL)
            pe.sem_inc(added, 2)
            pe.sem_inc(copied, 2)
            pe.sem_inc(seen, 2)
            pe.sem_inc(looked, 2)
            with pe.Fori(0, TURNS) as i:
                tiles = tiles_of(pe, i)
                for h in range(2):
                    for u in range(h * HALF, (h + 1) * HALF):
                        c = i * UNROLL + u
                        pe.wait_ge(ready, c + 1)
                        pe.wait_ge(copied, c + 1)
                        pe.transpose(turn_ps[u % 2][:, 0:P], m.hot[:, u, :], m.ident[:, :]).then_inc(turned, 1)
                        pe.wait_ge(copied, c + 3)
                        pe.wait_ge(seen, c + 1)
                        pe.matmul(side[u % 2][:, 0:2], m.turned[:, u % 2, :], m.count[:, bass.ds(tiles[u] * REL, 2)],
                                  start=True, stop=True).then_inc(looked, 1)
                    for u in range(h * HALF, (h + 1) * HALF):
                        c = i * UNROLL + u
                        pe.wait_ge(weighted, c + 1)
                        pe.wait_ge(added, c + 1)
                        pe.matmul(sums[u % 2][:, 0:ROW], m.hot[:, u, :], m.rows[:, u, :], start=True, stop=True).then_inc(product, 1)

        @block.scalar
        def _(act):
            with act.Fori(0, TURNS) as i:
                for h in range(2):
                    for u in range(h * HALF, (h + 1) * HALF):
                        c = i * UNROLL + u
                        act.wait_ge(turned, c + 1)
                        act.wait_ge(looked, c + 1)
                        act.copy(m.turned[:, u % 2, :], turn_ps[u % 2][:, 0:P]).then_inc(copied, 1)
                    act.wait_ge(raw, 2 * i + h + 1)
                    act.activation(power[:, h * HALF:(h + 1) * HALF], leaky, ACT.Exp).then_inc(powered, 1)

        @block.vector
        def _(dve):
            with dve.Fori(0, TURNS) as i:
                tiles = tiles_of(dve, i)
                for h in range(2):
                    for u in range(h * HALF, (h + 1) * HALF):
                        c = i * UNROLL + u
                        dve.wait_ge(product, c + 1)
                        dve.tensor_scalar(m.hot[:, u, :], m.iota[:, :], m.edge_dst[:, bass.ds(c, 1)], None,
                                          ALU.is_equal).then_inc(ready, 1)
                        if u % HALF:
                            dve.wait_ge(looked, 2 + c)
                            dve.tensor_copy(m.seen[:, u % HALF - 1, :], side[(u - 1) % 2][:, 0:2]).then_inc(seen, 1)
                    last = i * UNROLL + (h + 1) * HALF
                    dve.wait_ge(looked, 2 + last)
                    dve.tensor_copy(m.seen[:, HALF - 1, :], side[1][:, 0:2]).then_inc(seen, 1)
                    dve.wait_ge(seen, 2 + last)
                    dve.wait_ge(loaded[h], 16 * (i + 1))
                    n = 2 * (2 * i + h)
                    score = m.rows[:, h * HALF:(h + 1) * HALF, D]
                    dve.tensor_tensor(leaky, score, m.seen[:, :, 1], ALU.add).then_inc(step, 1)
                    dve.wait_ge(step, n + 1)
                    dve.scalar_tensor_tensor(leaky, leaky, LEAK, leaky, ALU.mult, ALU.max).then_inc(step, 1)
                    dve.wait_ge(step, n + 2)
                    dve.tensor_tensor(leaky, leaky, m.seen[:, :, 0], ALU.subtract).then_inc(raw, 1)
                    dve.wait_ge(powered, 2 * i + h + 1)
                    for u in range(h * HALF, (h + 1) * HALF):
                        dve.tensor_scalar(m.hot[:, u, :], m.hot[:, u, :], power[:, u:u + 1], None, ALU.mult).then_inc(weighted, 1)
                    for u in range(h * HALF, (h + 1) * HALF):
                        c = i * UNROLL + u
                        dve.wait_ge(product, UNROLL + c + 1)
                        dve.wait_ge(added, 2 + c)
                        at = acc[:, bass.ds(tiles[u] * ROW, ROW)]
                        dve.tensor_tensor(at, at, sums[u % 2][:, 0:ROW], ALU.add).then_inc(added, 1)


def attention(nc, m, a, out):
    B = [b[:, 0:NPAD] for b in m.big]
    W = m.weights
    spread = lambda f, n: f.rearrange("(o d) -> o d", o=1).to_broadcast([P, n])
    target_score, top = m.small[:, 0:TILES + 1], m.small[:, 64:64 + TILES + 1]
    load(nc, m, [(W[:, 0:D], a["L3_gnn_W_lin"]), (W[:, 2 * D:4 * D], spread(a["L3_gnn_a"], 2 * D)),
                 (W[:, 4 * D:5 * D], spread(a["L3_gnn_gamma"], D)), (W[:, 5 * D:6 * D], spread(a["L3_gnn_beta"], D))],
         zero=[m.big[1][:, 0:(TILES + 1) * ROW], m.count[:, :], target_score])

    with Stage(nc) as cs:
        turned = cs.sem("turned")
        block = cs.enter_context(nc.Block())

        @block.tensor
        def _(pe):
            pe.transpose(m.psum[0][:, 0:D], W[:, 0:D], m.ident[:, :]).then_inc(turned, 1)

        @block.scalar
        def _(act):
            act.wait_ge(turned, 1)
            act.copy(W[:, D:2 * D], m.psum[0][:, 0:D])

        @block.vector
        def _(dve):
            dve.memset(top, LOW)
            dve.memset(m.rows[:, 0:SETS, D + 1:D + 2], 1.0)

    attention_table(nc, m, B[0], lambda k: m.rows[:, k, :], target_score)
    gather_max(nc, m, top)

    with Stage(nc) as cs:
        step = cs.sem("step")
        block = cs.enter_context(nc.Block())
        pair = m.count[:, :].rearrange("p (t r) -> p t r", r=REL)

        @block.vector
        def _(dve):
            dve.tensor_copy(pair[:, :, 1], target_score)
            dve.tensor_tensor(top, top, target_score, ALU.add).then_inc(step, 1)
            dve.wait_ge(step, 1)
            dve.scalar_tensor_tensor(pair[:, :, 0], top, LEAK, top, ALU.mult, ALU.max)

    attend(nc, m, m.big[1])
    turn_tiles(nc, m, B[0], B[3])
    finish(nc, m, m.big[1], B[3], B[2], B[4], out)


def finish(nc, m, acc, x, y, tmp, out):
    shape = [P, TILES, D]
    view = lambda b: b.rearrange("p (t d) -> p t d", d=D)
    sums = acc[:, 0:TILES * ROW].rearrange("p (t r) -> p t r", r=ROW)
    x, y, tmp = view(x), view(y), view(tmp)
    z, mean, var = (m.small[:, 128 + 64 * n:128 + 64 * n + TILES] for n in range(3))
    gamma, beta = m.weights[:, 4 * D:5 * D], m.weights[:, 5 * D:6 * D]
    per_node = lambda v: v.unsqueeze(2).to_broadcast(shape)
    per_feature = lambda v: v.unsqueeze(1).to_broadcast(shape)
    with Stage(nc) as cs:
        step, asked, rooted, stored = cs.sems("step", "asked", "rooted", "stored")
        block = cs.enter_context(nc.Block())

        @block.vector
        def _(dve):
            steps = [0]

            def then(ins):
                steps[0] += 1
                ins.then_inc(step, 1)
                dve.wait_ge(step, steps[0])

            def norm(turn):
                then(dve.tensor_reduce(mean, y, AX.X, ALU.add))
                then(dve.tensor_scalar(mean, mean, 1.0 / D, None, ALU.mult))
                then(dve.tensor_tensor(y, y, per_node(mean), ALU.subtract))
                then(dve.tensor_tensor(tmp, y, y, ALU.mult))
                then(dve.tensor_reduce(var, tmp, AX.X, ALU.add))
                dve.tensor_scalar(var, var, 1.0 / D, None, ALU.mult).then_inc(asked, 1)
                dve.wait_ge(rooted, turn)
                then(dve.reciprocal(var, var))

            then(dve.tensor_scalar(z, sums[:, :, D + 1], 1e-30, None, ALU.max))
            then(dve.reciprocal(z, z))
            then(dve.tensor_tensor(y, sums[:, :, 0:D], per_node(z), ALU.mult))
            then(dve.tensor_tensor(y, y, x, ALU.add))
            norm(1)
            then(dve.tensor_tensor(y, y, per_node(var), ALU.mult))
            then(dve.tensor_tensor(y, y, per_feature(gamma), ALU.mult))
            then(dve.tensor_tensor(y, y, per_feature(beta), ALU.add))
            then(dve.tensor_tensor(y, y, x, ALU.add))
            norm(2)
            dve.tensor_tensor(y, y, per_node(var), ALU.mult).then_inc(asked, 1)

        @block.scalar
        def _(act):
            for turn in (1, 2):
                act.wait_ge(asked, turn)
                act.activation(var, var, ACT.Sqrt, bias=m.eps).then_inc(rooted, 1)

        @block.sync
        def _(sp):
            full = TILES - 1
            sp.wait_ge(asked, 3)
            sp.dma_start(out[0:full * P, :].rearrange("(t p) d -> p t d", p=P), y[:, 0:full, :]).then_inc(stored, 16)
            sp.dma_start(out[full * P:N, :], y[0:LAST, full, :]).then_inc(stored, 16)
            sp.wait_ge(stored, 32)


VECTORS = ["L0_gnn_b1", "L0_gnn_b2", "L0_gnn_gamma", "L0_gnn_beta", "L1_gnn_bn0_gamma", "L1_gnn_bn0_beta",
           "L1_gnn_b1", "L1_gnn_bn1_gamma", "L1_gnn_bn1_beta", "L1_gnn_b2", "L1_gnn_bn2_gamma", "L1_gnn_bn2_beta",
           "L2_gnn_b1", "L2_gnn_b2", "L2_gnn_b3", "L2_gnn_res_b"]


def build(nc, a, out):
    with ExitStack() as cs:
        m = Memory(nc, cs)
        vec = {name: m.par[:, n:n + 1] for n, name in enumerate(VECTORS)}
        B = [b[:, 0:NPAD] for b in m.big]
        acc_whole = m.big[1][:, 0:ACCW]
        W = m.weights

        make_constants(nc, m)
        load_edges(nc, m, a["src"], a["dst"], a["edge_type_8"], a["edge_weight1"].rearrange("e o -> (e o)"))
        sort_edges(nc, m)

        load_vectors(nc, m, a)
        turn_tiles(nc, m, B[4], B[0])
        load(nc, m, [(W[:, 0:D], a["L0_gnn_W1"]), (W[:, D:2 * D], a["L0_gnn_W2"]),
                     (B[4][:, 0:N], a["node_vec1"].rearrange("n o -> o n").to_broadcast([P, N]))],
             zero=[acc_whole, m.count[:, :], B[4][:, N:NPAD]])
        gather_sum(nc, m, a["x"], m.edge_src, m.big[1], scale_rows=m.edge_w, count=True)
        combine(nc, m, [(B[2], B[0], m.one_eps, B[1], ALU.mult, ALU.add)])
        linear(nc, m, W[:, 0:D], B[2], B[3], ACT.Relu, vec["L0_gnn_b1"])
        linear(nc, m, W[:, D:2 * D], B[3], B[2], ACT.Identity, vec["L0_gnn_b2"], times=B[4])
        batch_norm(nc, m, B[2], B[2], vec["L0_gnn_gamma"], vec["L0_gnn_beta"], ACT.Relu)
        combine(nc, m, [(B[2], B[0], 2.0, B[2], ALU.mult, ALU.add)])
        layer_norm(nc, m, B[2], B[0], B[3])

        degrees(nc, m, B[4])
        batch_norm(nc, m, B[0], B[2], vec["L1_gnn_bn0_gamma"], vec["L1_gnn_bn0_beta"])
        load(nc, m, [(W[:, 0:D], a["L1_gnn_W1"]), (W[:, D:2 * D], a["L1_gnn_W2"])])
        table = m.table[0:NPAD, :]
        for layer in (1, 2):
            x = B[2] if layer == 1 else B[3]
            if layer == 2:
                load(nc, m, [(W[:, 0:D], a["L1_gnn_W2"])])
            linear(nc, m, W[:, 0:D], x, B[1], times=B[4])
            write_table(nc, m, x, D, lambda k: m.rows[:, k, 0:D], lambda t: table[bass.ds(t * P, P), :], scale=m.dinv)
            gather_sum(nc, m, table, m.edge_src, m.big[1], norm=layer == 1)
            combine(nc, m, [(B[1], B[1], 1.0, B[4], ALU.mult, ALU.mult)])
            relu_bias(nc, m, B[1], B[3], vec[f"L1_gnn_b{layer}"])
            batch_norm(nc, m, B[3], B[3], vec[f"L1_gnn_bn{layer}_gamma"], vec[f"L1_gnn_bn{layer}_beta"])
        combine(nc, m, [(B[3], B[3], 1.0, B[2], ALU.mult, ALU.add), (B[3], B[3], 1.0, B[0], ALU.mult, ALU.add)])
        layer_norm(nc, m, B[3], B[0], B[2])

        load(nc, m, [(W[:, 0:D], a["L2_gnn_res_w"])])
        linear(nc, m, W[:, 0:D], B[0], B[2], bias=vec["L2_gnn_res_b"])
        for layer in (1, 2, 3):
            x = B[0] if layer == 1 else B[3]
            load(nc, m, [(W[:, 0:D], a[f"L2_gnn_root{layer}"])])
            linear(nc, m, W[:, 0:D], x, B[1])
            load(nc, m, [(W[:, :].rearrange("p (r d) -> p r d", d=D), a[f"L2_gnn_W{layer}"].rearrange("r p d -> p r d"))])
            by_tile = m.table.rearrange("(r n) d -> n r d", n=NPAD)
            write_table(nc, m, x, REL * D, lambda k: m.big[4][:, k * REL * D:(k + 1) * REL * D],
                        lambda t: by_tile[bass.ds(t * P, P), :, :])
            gather_sum(nc, m, m.table, m.edge_row, m.big[1], weight=m.edge_norm)
            relu_bias(nc, m, B[1], B[3], vec[f"L2_gnn_b{layer}"])
            combine(nc, m, [(B[3], B[3], 1.0, B[2], ALU.mult, ALU.add)])
        combine(nc, m, [(B[3], B[3], 1.0, B[0], ALU.mult, ALU.add)])
        layer_norm(nc, m, B[3], B[0], B[2])
        attention(nc, m, a, out)


def relu_bias(nc, m, x, out, bias):
    with Stage(nc) as cs:
        block = cs.enter_context(nc.Block())

        @block.scalar
        def _(act):
            act.activation(out, x, ACT.Relu, bias=bias)


def kernel(**inputs):
    import numpy as _np
    import concourse.bacc as _bacc
    from concourse import mybir as _mybir
    from concourse.bass_utils import run_bass_kernel_spmd as _run

    nc = _bacc.Bacc("TRN2", target_bir_lowering=False, num_devices=1)
    arrays, args = {}, {}
    for name, value in inputs.items():
        v = _np.ascontiguousarray(value)
        arrays[f"in_{name}"] = v
        args[name] = nc.dram_tensor(f"in_{name}", v.shape, _mybir.dt.from_np(v.dtype), kind="ExternalInput").ap()
    out = nc.dram_tensor("out", (N, D), F32, kind="ExternalOutput").ap()
    build(nc, args, out)
    r = _run(nc, [arrays], core_ids=[0])
    return r.results[0]["out"]
```

```python
import concourse.bass as bass
from concourse import mybir
from contextlib import ExitStack

F32 = mybir.dt.float32
I32 = mybir.dt.int32
U32 = mybir.dt.uint32
ALU = mybir.AluOpType
ACT = mybir.ActivationFunctionType
AX = mybir.AxisListType

P = 128
N, E, D, REL = 6250, 206250, 128, 8
TILES = -(-N // P)
NPAD = TILES * P
LAST = N - (TILES - 1) * P
UNROLL = 16
HALF = UNROLL // 2
COLS = -(-E // (P * UNROLL)) * UNROLL
LASTCOLS = E - (P - 1) * COLS
CHUNKS = -(-(E // P + TILES) // UNROLL) * UNROLL
TURNS = CHUNKS // UNROLL
WIDE = CHUNKS * 4
ACCW = NPAD + P
PER = CHUNKS // P
PSLOTS = 2
ROW = D + 2
LN_EPS = 1e-5
LEAK = 0.2
LOW = -3.0e38
FLOOR = -1.0e30
BLK = 448
BLKS = NPAD // BLK
assert BLKS * BLK == NPAD and BLKS % 2 == 0


class Stage(ExitStack):

    number = 0

    def __init__(self, nc):
        super().__init__()
        self.nc, self.own = nc, []
        Stage.number += 1

    def sem(self, name):
        self.own.append(self.nc.alloc_semaphore(f"{name}_{Stage.number}"))
        return self.own[-1]

    def sems(self, *names):
        return [self.sem(name) for name in names]

    def __exit__(self, *failure):
        super().__exit__(*failure)
        if self.own:
            self.nc.clear_and_free_semaphores(self.own)
            self.nc.all_engine_barrier()


class Memory:

    def __init__(self, nc, cs):
        def sb(name, shape, dt=F32):
            return cs.enter_context(nc.sbuf_tensor(name, shape, dt))

        self.big = [sb(f"big{i}", [P, WIDE]) for i in range(5)]
        self.edge_src = sb("edge_src", [P, CHUNKS + HALF], I32)
        self.edge_dst = sb("edge_dst", [P, CHUNKS])
        self.edge_type = sb("edge_type", [P, CHUNKS])
        self.edge_w = sb("edge_w", [P, CHUNKS])
        self.tile_of = sb("tile_of", [1, CHUNKS], I32)
        self.iota = sb("iota", [P, P])
        self.part = sb("part", [P, 1])
        self.ident = sb("ident", [P, P])
        self.before = sb("before", [P, P])
        self.ones = sb("ones", [P, P])
        self.target_score = sb("target_score", [P, TILES + 1])[:, :]
        self.mean = sb("mean", [P, P])
        self.small = sb("small", [P, 512])
        self.one_eps = self.small[:, 510:511]
        self.eps = self.small[:, 511:512]
        self.rows = sb("rows", [P, UNROLL, ROW])
        self.hot = sb("hot", [P, UNROLL, P])
        self.idx = sb("idx", [P, UNROLL], I32)
        self.recs = sb("recs", [P, UNROLL, 4])
        self.psum = [cs.enter_context(nc.psum_tensor(f"ps{i}", [P, 512], F32)) for i in range(8)]
        self.gathered = [cs.enter_context(nc.semaphore(f"gathered{u}")) for u in range(UNROLL)]
        self.gathered_to = 0
        self.written = [cs.enter_context(nc.semaphore(f"written{h}")) for h in range(2)]
        self.records = nc.dram_tensor("records", [CHUNKS * P + COLS, 4], F32, kind="Internal").ap()
        self.unsorted = sb("unsorted", [1, 1], I32)
        self.col_map = nc.dram_tensor("col_map", [CHUNKS], I32, kind="Internal").ap()
        self.tile_row = nc.dram_tensor("tile_row", [CHUNKS], F32, kind="Internal").ap()
        self.map = nc.dram_tensor("map", [CHUNKS], I32, kind="Internal").ap()
        self.edge_row = sb("edge_row", [P, CHUNKS], I32)
        self.col_of = self.edge_row[0:1, :]
        self.edge_norm = self.edge_w
        self.turned = sb("turned", [P, 2, P])
        self.kind = sb("kind", [P, PSLOTS, REL])
        self.count = sb("count", [P, (TILES + 1) * REL])
        self.dinv = sb("dinv", [P, TILES + 1])
        self.weights = sb("weights", [P, REL * D])
        self.par = sb("par", [P, 24])
        self.bnc = sb("bnc", [P, 25 * 6 + 8])
        self.att_table = nc.dram_tensor("att_table", [NPAD, ROW], F32, kind="Internal").ap()
        self.table = nc.dram_tensor("table", [REL * NPAD, D], F32, kind="Internal").ap()


def make_constants(nc, m):
    with Stage(nc) as cs:
        made = cs.sem("made")
        block = cs.enter_context(nc.Block())

        @block.gpsimd
        def _(pool):
            pool.iota(m.iota[:, :], [[1, P]], base=0, channel_multiplier=0, allow_small_or_imprecise_dtypes=True)
            pool.iota(m.part[:, :], [[0, 1]], base=0, channel_multiplier=1, allow_small_or_imprecise_dtypes=True)
            pool.memset(m.eps, LN_EPS)
            pool.memset(m.mean[:, :], 1.0 / D)
            pool.memset(m.ones[:, :], 1.0).then_inc(made, 1)
            pool.wait_ge(made, 1)
            pool.affine_select(out=m.ident[:, :], in_=m.ones[:, :], compare_op=ALU.is_equal, fill=0.0,
                               base=0, pattern=[[-1, P]], channel_multiplier=1)
            pool.affine_select(out=m.before[:, :], in_=m.ones[:, :], compare_op=ALU.is_gt, fill=0.0,
                               base=0, pattern=[[1, P]], channel_multiplier=-1)


def load_edges(nc, m, src, dst, etype, weight):
    raw = [m.big[0][:, k * COLS:(k + 1) * COLS] for k in range(4)]
    src_i, dst_i, type_i = (r.bitcast(I32) for r in raw[:3])
    rec = m.big[1][:, 0:4 * COLS].rearrange("p (c f) -> p c f", f=4)
    bin_f = m.big[2][:, 0:COLS]
    bin_i = m.big[3][:, 0:COLS].bitcast(I32)
    place_i = m.big[3][:, COLS:2 * COLS].bitcast(I32)
    with Stage(nc) as cs:
        blank, loaded, split, built, stored = cs.sems("blank", "loaded", "split", "built", "stored")
        block = cs.enter_context(nc.Block())

        @block.sync
        def _(sp):
            sp.wait_ge(blank, 4)
            for t, f in ((dst_i, dst), (src_i, src), (type_i, etype), (raw[3], weight)):
                for a, b in ((0, 112), (112, P - 1)):
                    sp.dma_start(t[a:b, :], f[a * COLS:b * COLS].rearrange("(p c) -> p c", c=COLS)).then_inc(loaded, 16)
                sp.dma_start(t[P - 1:P, 0:LASTCOLS],
                             f[(P - 1) * COLS:E].rearrange("(p c) -> p c", p=1)).then_inc(loaded, 16)
            sp.wait_ge(built, 2)
            sp.dma_start(m.records[0:CHUNKS * P, :].rearrange("(p c) f -> p (c f)", p=P), m.big[4][:, :]).then_inc(stored, 16)
            sp.wait_ge(stored, 16)

        @block.gpsimd
        def _(pool):
            empty = m.big[4][:, :].rearrange("p (c f) -> p c f", f=4)
            pool.memset(empty[:, :, :], 0.0).then_inc(built, 1)
            pool.wait_ge(built, 1)
            pool.memset(empty[:, :, 1], -1.0).then_inc(built, 1)

        @block.vector
        def _(dve):
            dve.memset(dst_i[:, LASTCOLS:COLS], TILES * P).then_inc(blank, 1)
            dve.memset(src_i[:, LASTCOLS:COLS], 0).then_inc(blank, 1)
            dve.memset(type_i[:, LASTCOLS:COLS], 0).then_inc(blank, 1)
            dve.memset(raw[3][:, LASTCOLS:COLS], 0.0).then_inc(blank, 1)
            dve.wait_ge(loaded, 16 * 12)
            dve.tensor_scalar(bin_i, dst_i, 7, None, ALU.arith_shift_right).then_inc(split, 1)
            dve.tensor_scalar(place_i, dst_i, P - 1, None, ALU.bitwise_and).then_inc(split, 1)
            dve.tensor_copy(rec[:, :, 0].bitcast(I32), src_i)
            dve.tensor_copy(rec[:, :, 2], type_i)
            dve.tensor_copy(rec[:, :, 3], raw[3])
            dve.wait_ge(split, 2)
            dve.tensor_copy(bin_f, bin_i)
            dve.tensor_copy(rec[:, :, 1], place_i)


def sort_edges(nc, m):
    bin_f = m.big[2][:, 0:COLS]
    same = m.big[2][:, COLS:2 * COLS]
    running = m.big[2][:, 2 * COLS:3 * COLS]
    one = m.big[2][:, 3 * COLS:4 * COLS]
    slot = m.big[3][:, 0:COLS]
    slot_i = m.big[3][:, COLS:2 * COLS].bitcast(I32)
    part_i = m.big[3][:, 2 * COLS:3 * COLS].bitcast(I32)
    row_i = m.big[3][:, 3 * COLS:4 * COLS].bitcast(I32)
    picked = m.big[0][:, 0:COLS]
    behind = m.big[0][:, COLS:2 * COLS]
    rec = m.big[1][:, 0:4 * COLS].rearrange("p (c f) -> p c f", f=4)
    total = m.small[:, 0:TILES]
    first = m.small[:, 64:64 + TILES]
    need_i = m.small[:, 128:128 + TILES].bitcast(I32)
    need = m.small[:, 192:192 + TILES]
    end = m.small[:, 256:256 + TILES]
    bin_no = m.small[:, 320:320 + TILES]
    chunk_no = m.small[:, 384:384 + PER]
    map_f = m.small[:, 400:400 + PER]
    map_i = m.small[:, 416:416 + PER].bitcast(I32)
    past = m.big[0][:, 0:PER * TILES].rearrange("p (c b) -> p c b", b=TILES)
    before_ps, total_ps = m.psum[0][:, 0:TILES], m.psum[1][:, 0:TILES]

    with Stage(nc) as cs:
        made, counted, summed, step, mapped, map_out, map_in = cs.sems("made", "counted", "summed", "step", "mapped", "map_out", "map_in")
        block = cs.enter_context(nc.Block())

        @block.gpsimd
        def _(pool):
            pool.iota(bin_no, [[1, TILES]], base=0, channel_multiplier=0, allow_small_or_imprecise_dtypes=True).then_inc(made, 1)
            pool.iota(chunk_no, [[1, PER]], base=0, channel_multiplier=PER, allow_small_or_imprecise_dtypes=True).then_inc(made, 1)
            pool.iota(behind, [[1, COLS]], base=CHUNKS * P, channel_multiplier=0, allow_small_or_imprecise_dtypes=True).then_inc(made, 1)
            pool.memset(one, 1.0).then_inc(made, 1)

        @block.tensor
        def _(pe):
            pe.wait_ge(counted, TILES)
            pe.matmul(before_ps, m.before[:, :], total, start=True, stop=True).then_inc(summed, 1)
            pe.matmul(total_ps, m.ones[:, :], total, start=True, stop=True).then_inc(summed, 1)

        @block.vector
        def _(dve):
            steps = [0]

            def then(ins):
                steps[0] += 1
                ins.then_inc(step, 1)
                dve.wait_ge(step, steps[0])

            dve.wait_ge(made, 4)
            dve.memset(slot, 0.0)
            with dve.Fori(0, TILES) as b:
                dve.tensor_scalar(same, bin_f, bin_no[:, bass.ds(b, 1)], 0.0, ALU.is_equal, ALU.add,
                                  accum_out=total[:, bass.ds(b, 1)]).then_inc(counted, 1)
                dve.wait_ge(counted, b + 1)
            dve.wait_ge(summed, 2)
            then(dve.tensor_scalar(need, total_ps, float(P - 1), None, ALU.add))
            then(dve.tensor_copy(need_i, need))
            then(dve.tensor_scalar(need_i, need_i, 7, None, ALU.arith_shift_right))
            then(dve.tensor_copy(need, need_i))
            then(dve.tensor_tensor_scan(end, m.ones[:, 0:TILES], need, 0.0, ALU.mult, ALU.add))
            then(dve.tensor_tensor(first, end, need, ALU.subtract))
            then(dve.scalar_tensor_tensor(first, first, float(P), before_ps, ALU.mult, ALU.add))
            then(dve.tensor_scalar(first, first, -1.0, None, ALU.add))
            then(dve.tensor_tensor(past, chunk_no.unsqueeze(2).to_broadcast([P, PER, TILES]),
                                   end.unsqueeze(1).to_broadcast([P, PER, TILES]), ALU.is_ge))
            then(dve.tensor_reduce(map_f, past, AX.X, ALU.add))
            dve.tensor_copy(map_i, map_f).then_inc(mapped, 1)
            dve.wait_ge(mapped, 1)
            base = steps[0]
            with dve.Fori(0, TILES) as b:
                dve.tensor_scalar(same, bin_f, bin_no[:, bass.ds(b, 1)], None, ALU.is_equal).then_inc(step, 1)
                dve.wait_ge(step, 4 * b + base + 1)
                dve.tensor_tensor_scan(running, one, same, first[:, bass.ds(b, 1)], ALU.mult, ALU.add).then_inc(step, 1)
                dve.wait_ge(step, 4 * b + base + 2)
                dve.tensor_tensor(picked, same, running, ALU.mult).then_inc(step, 1)
                dve.wait_ge(step, 4 * b + base + 3)
                dve.tensor_tensor(slot, slot, picked, ALU.add).then_inc(step, 1)
                dve.wait_ge(step, 4 * b + base + 4)
            steps[0] += 4 * TILES
            then(dve.tensor_copy(slot_i, slot))
            then(dve.tensor_scalar(part_i, slot_i, P - 1, None, ALU.bitwise_and))
            then(dve.tensor_scalar(slot_i, slot_i, 7, None, ALU.arith_shift_right))
            then(dve.tensor_copy(slot, slot_i))
            then(dve.tensor_copy(picked, part_i))
            then(dve.scalar_tensor_tensor(slot, picked, float(CHUNKS), slot, ALU.mult, ALU.add))
            then(dve.scalar_tensor_tensor(same, bin_f, float(TILES), behind, ALU.is_ge, ALU.mult))
            then(dve.tensor_tensor(slot, slot, same, ALU.add))
            then(dve.tensor_copy(row_i, slot))

        @block.sync
        def _(sp):
            sp.wait_ge(mapped, 1)
            sp.dma_start(m.map.rearrange("(p c) -> p c", p=P), map_i).then_inc(map_out, 16)
            sp.wait_ge(map_out, 16)
            sp.dma_start(m.tile_of[0:1, :], m.map.rearrange("(p c) -> p c", p=1)).then_inc(map_in, 16)
            sp.wait_ge(map_in, 16)

    with Stage(nc) as cs:
        staged, begun = cs.sems("staged", "begun")
        written = m.written
        block = cs.enter_context(nc.Block())

        @block.scalar
        def _(act):
            def stage(i, h):
                act.copy(m.idx[:, h * HALF:(h + 1) * HALF], row_i[:, bass.ds(i * UNROLL + h * HALF, HALF)]).then_inc(staged, 1)
                act.copy(m.recs[:, h * HALF:(h + 1) * HALF, :], rec[:, bass.ds(i * UNROLL + h * HALF, HALF), :]).then_inc(staged, 1)

            stage(0, 0)
            stage(0, 1)
            with act.Fori(1, COLS // UNROLL) as i:
                for h in range(2):
                    act.wait_ge(written[h], 16 * HALF * i)
                    stage(i, h)
            for h in range(2):
                act.wait_ge(written[h], 16 * HALF * (COLS // UNROLL))

        @block.gpsimd
        def _(pool):
            with pool.Fori(0, COLS // UNROLL) as i:
                for h in range(2):
                    pool.wait_ge(staged, 4 * i + 2 * h + 2)
                    pool.sem_inc(begun, 1)
                    for u in range(h * HALF, (h + 1) * HALF):
                        pool.indirect_dma_start(m.records, bass.IndirectOffsetOnAxis(ap=m.idx[:, u:u + 1].bitcast(U32), axis=0),
                                                m.recs[:, u, :], None).then_inc(written[h], 16)

    with Stage(nc) as cs:
        back = cs.sem("back")
        block = cs.enter_context(nc.Block())
        rec = m.big[0][:, :].rearrange("p (c f) -> p c f", f=4)

        @block.sync
        def _(sp):
            sp.dma_start(m.big[0][:, :], m.records[0:CHUNKS * P, :].rearrange("(p c) f -> p (c f)", p=P)).then_inc(back, 16)

        @block.vector
        def _(dve):
            dve.wait_ge(back, 16)
            dve.memset(m.edge_src[:, CHUNKS:], 0)
            dve.tensor_copy(m.edge_src[:, 0:CHUNKS], rec[:, :, 0].bitcast(I32))
            dve.tensor_copy(m.edge_dst[:, :], rec[:, :, 1])

        @block.scalar
        def _(act):
            act.wait_ge(back, 16)
            act.copy(m.edge_type[:, :], rec[:, :, 2])
            act.copy(m.edge_w[:, :], rec[:, :, 3])


def edge_rows(nc, m):
    with Stage(nc) as cs:
        done = cs.sem("done")
        block = cs.enter_context(nc.Block())
        src_f, row_f = m.big[1][:, 0:CHUNKS], m.big[1][:, CHUNKS:2 * CHUNKS]

        @block.vector
        def _(dve):
            dve.tensor_copy(src_f, m.edge_src[:, 0:CHUNKS]).then_inc(done, 1)
            dve.wait_ge(done, 1)
            dve.scalar_tensor_tensor(row_f, m.edge_type[:, :], float(NPAD), src_f, ALU.mult, ALU.add).then_inc(done, 1)
            dve.wait_ge(done, 2)
            dve.tensor_copy(m.edge_row[:, :], row_f)


def load_columns(nc, m, src, dst, etype, weight):
    raw = [m.big[0][:, k * CHUNKS:(k + 1) * CHUNKS] for k in range(4)]
    rec = m.big[1][:, :].rearrange("p (c f) -> p c f", f=4)
    full = E // (P * P) * P
    rest = E // P - full
    over = E % P
    last = (PER - 1) * P
    assert full == last
    with Stage(nc) as cs:
        blank, held, turned, taken = cs.sems("blank", "held", "turned", "taken")
        loaded = cs.sem("loaded")
        block = cs.enter_context(nc.Block())

        @block.gpsimd
        def _(pool):
            pool.memset(raw[0][:, last:].bitcast(I32), 0).then_inc(blank, 1)
            pool.memset(raw[1][:, last:].bitcast(I32), TILES * P).then_inc(blank, 1)
            pool.memset(raw[2][:, last:].bitcast(I32), 0).then_inc(blank, 1)
            pool.memset(raw[3][:, last:], 0.0).then_inc(blank, 1)

        @block.sync
        def _(sp):
            fields = [(r.bitcast(f.dtype), f) for r, f in zip(raw, (src, dst, etype, weight))]
            for t, f in fields:
                sp.dma_start(t[:, 0:last].rearrange("p (g j) -> p g j", j=P),
                             f[0:full * P].rearrange("(g p j) -> p g j", p=P, j=P)).then_inc(loaded, 16)
            sp.wait_ge(blank, 4)
            for t, f in fields:
                sp.dma_start(t[0:rest, last:], f[full * P:(full + rest) * P].rearrange("(p j) -> p j", j=P)).then_inc(loaded, 16)
                sp.dma_start(t[rest:rest + 1, last:last + over],
                             f[(full + rest) * P:E].rearrange("(p j) -> p j", p=1)).then_inc(loaded, 16)

        @block.vector
        def _(dve):
            dve.wait_ge(loaded, 16 * 12)
            dve.sem_inc(turned, 4)
            with dve.Fori(0, PER) as g:
                for k in range(4):
                    dve.wait_ge(turned, 4 * g + k + 1)
                    at = raw[k][:, bass.ds(g * P, P)]
                    dve.tensor_copy(m.hot[:, k, :], at if k == 3 else at.bitcast(I32)).then_inc(held, 1)

        @block.tensor
        def _(pe):
            pe.sem_inc(taken, 4)
            with pe.Fori(0, PER) as g:
                for k in range(4):
                    pe.wait_ge(held, 4 * g + k + 1)
                    pe.wait_ge(taken, 4 * g + k + 1)
                    pe.transpose(m.psum[k][:, 0:P], m.hot[:, k, :], m.ident[:, :]).then_inc(turned, 1)

        @block.scalar
        def _(act):
            with act.Fori(0, PER) as g:
                for k in range(4):
                    act.wait_ge(turned, 4 + 4 * g + k + 1)
                    act.copy(rec[:, bass.ds(g * P, P), k], m.psum[k][:, 0:P]).then_inc(taken, 1)


def pair_columns(nc, m):
    rec = m.big[1][:, :].rearrange("p (c f) -> p c f", f=4)
    part = lambda b, k: m.big[b][:, k * CHUNKS:(k + 1) * CHUNKS]
    bins, first, final, count = (part(2, k) for k in range(4))
    one, end, jump, junk = (part(3, k) for k in range(4))
    start, lead, whole = (part(0, k) for k in range(3))
    other_junk = part(0, 3)
    chunk_no, col, shift, tile = (m.small[:, 16 * k:16 * k + PER] for k in range(4))
    col_i, tile_i = (m.small[:, 64 + 16 * k:64 + 16 * k + PER].bitcast(I32) for k in range(2))
    wrong = m.small[:, 96:100]
    flag = m.small[:, 100:101]
    quarter = CHUNKS // 4
    with Stage(nc) as cs:
        made, ready, product, taken, step, judged, added, mapped, map_out, map_in = cs.sems(
            "made", "ready", "product", "taken", "step", "judged", "added", "mapped", "map_out", "map_in")
        block = cs.enter_context(nc.Block())

        @block.gpsimd
        def _(pool):
            pool.iota(chunk_no, [[1, PER]], base=0, channel_multiplier=PER, allow_small_or_imprecise_dtypes=True).then_inc(made, 1)
            pool.memset(one, 1.0).then_inc(made, 1)

        @block.tensor
        def _(pe):
            pe.wait_ge(ready, 3)
            for k in range(2):
                for q in range(4):
                    pe.matmul(m.psum[4 * k + q][:, 0:quarter], m.hot[:, k, :], bins[:, q * quarter:(q + 1) * quarter],
                              start=True, stop=True).then_inc(product, 1)
            pe.wait_ge(taken, 8)
            pe.wait_ge(judged, 1)
            pe.matmul(m.psum[0][:, 0:1], m.ones[:, :], wrong[:, 3:4], start=True, stop=True).then_inc(added, 1)

        @block.scalar
        def _(act):
            for k, row in enumerate((first, final)):
                for q in range(4):
                    act.wait_ge(product, 4 * k + q + 1)
                    act.copy(row[:, q * quarter:(q + 1) * quarter], m.psum[4 * k + q][:, 0:quarter]).then_inc(taken, 1)

        @block.vector
        def _(dve):
            steps = [0]

            def then(ins):
                steps[0] += 1
                ins.then_inc(step, 1)
                dve.wait_ge(step, steps[0])

            dve.tensor_scalar(m.hot[:, 0, :], m.ones[:, :], m.ident[:, 0:1], None, ALU.mult).then_inc(ready, 1)
            dve.tensor_scalar(m.hot[:, 1, :], m.ones[:, :], m.ident[:, P - 1:P], None, ALU.mult).then_inc(ready, 1)
            then(dve.tensor_copy(whole.bitcast(I32), rec[:, :, 1]))
            then(dve.tensor_scalar(whole.bitcast(I32), whole.bitcast(I32), 7, None, ALU.arith_shift_right))
            dve.tensor_copy(bins, whole.bitcast(I32)).then_inc(ready, 1)
            dve.wait_ge(ready, 3)
            dve.wait_ge(taken, 8)
            dve.wait_ge(made, 2)
            then(dve.scalar_tensor_tensor(junk, bins, 0.0, first, ALU.add, ALU.is_lt, accum_out=wrong[:, 0:1]))
            then(dve.scalar_tensor_tensor(junk, bins, 0.0, final, ALU.add, ALU.is_gt, accum_out=wrong[:, 1:2]))
            then(dve.scalar_tensor_tensor(junk[:, 1:], final[:, 0:CHUNKS - 1], 0.0, first[:, 1:], ALU.add, ALU.is_gt,
                                          accum_out=wrong[:, 2:3]))
            dve.tensor_reduce(wrong[:, 3:4], wrong[:, 0:3], AX.X, ALU.add).then_inc(judged, 1)
            then(dve.scalar_tensor_tensor(count, final, 1.0, first, ALU.add, ALU.subtract))
            then(dve.tensor_tensor_scan(end, one, count, 0.0, ALU.mult, ALU.add))
            then(dve.tensor_tensor(start, end, count, ALU.subtract))
            then(dve.tensor_tensor(lead, first, start, ALU.subtract))
            then(dve.tensor_tensor(jump[:, 1:], lead[:, 1:], lead[:, 0:CHUNKS - 1], ALU.subtract))
            then(dve.tensor_copy(jump[:, 0:1], lead[:, 0:1]))
            base = steps[0]
            with dve.Fori(0, PER) as j:
                dve.tensor_scalar(junk, end, chunk_no[:, bass.ds(j, 1)], 0.0, ALU.is_le, ALU.add,
                                  accum_out=col[:, bass.ds(j, 1)]).then_inc(step, 1)
                dve.scalar_tensor_tensor(other_junk, start, chunk_no[:, bass.ds(j, 1)], jump, ALU.is_le, ALU.mult,
                                         accum_out=shift[:, bass.ds(j, 1)]).then_inc(step, 1)
                dve.wait_ge(step, 2 * j + base + 2)
            steps[0] += 2 * PER
            then(dve.tensor_tensor(tile, shift, chunk_no, ALU.add))
            dve.tensor_copy(col_i, col).then_inc(mapped, 1)
            dve.tensor_copy(tile_i, tile).then_inc(mapped, 1)
            dve.wait_ge(added, 1)
            then(dve.tensor_scalar(flag, m.psum[0][:, 0:1], 1.0, None, ALU.min))
            dve.tensor_copy(m.unsorted[0:1, 0:1], flag[0:1, :])

        @block.sync
        def _(sp):
            sp.wait_ge(mapped, 2)
            sp.dma_start(m.map.rearrange("(p c) -> p c", p=P), tile_i).then_inc(map_out, 16)
            sp.dma_start(m.col_map.rearrange("(p c) -> p c", p=P), col_i).then_inc(map_out, 16)
            sp.dma_start(m.tile_row.rearrange("(p c) -> p c", p=P), tile).then_inc(map_out, 16)
            sp.wait_ge(map_out, 48)
            sp.dma_start(m.tile_of[0:1, :], m.map.rearrange("(p c) -> p c", p=1)).then_inc(map_in, 16)
            sp.dma_start(m.col_of[0:1, :], m.col_map.rearrange("(p c) -> p c", p=1)).then_inc(map_in, 16)
            sp.wait_ge(map_in, 32)


def spread_columns(nc, m):
    rec = m.big[1][:, :].rearrange("p (c f) -> p c f", f=4)
    by_chunk = m.big[4][:, :].rearrange("p (c f) -> p c f", f=4)
    tile = m.big[2][:, 0:CHUNKS]
    with Stage(nc) as cs:
        spread, copied = cs.sems("spread", "copied")
        block = cs.enter_context(nc.Block())

        @block.sync
        def _(sp):
            sp.dma_start(tile, m.tile_row.rearrange("(o c) -> o c", o=1).to_broadcast([P, CHUNKS])).then_inc(spread, 16)

        def columns(engine, copy, h):
            with engine.Fori(0, TURNS) as i:
                _, cols = nc.values_load_multi_w_load_instructions(
                    m.col_of[0:1, bass.ds(i * UNROLL + h * HALF, HALF)], engines=[engine.engine], min_val=0, max_val=CHUNKS - 1,
                    skip_runtime_bounds_check_because="pairs of sorted edges, with one for each column behind them, are no fewer than chunks")
                for u in range(HALF):
                    copy(by_chunk[:, bass.ds(i * UNROLL + h * HALF + u, 1), :], rec[:, bass.ds(cols[u], 1), :]).then_inc(copied, 1)

        @block.scalar
        def _(act):
            columns(act, act.copy, 0)
            act.wait_ge(copied, CHUNKS)
            act.copy(m.edge_type[:, :], by_chunk[:, :, 2])
            act.copy(m.edge_w[:, :], by_chunk[:, :, 3])

        @block.vector
        def _(dve):
            columns(dve, dve.tensor_copy, 1)
            dve.wait_ge(copied, CHUNKS)
            dve.memset(m.edge_src[:, CHUNKS:], 0)
            dve.tensor_copy(m.edge_src[:, 0:CHUNKS], by_chunk[:, :, 0])
            dve.wait_ge(spread, 16)
            dve.scalar_tensor_tensor(m.edge_dst[:, :], tile, -float(P), by_chunk[:, :, 1], ALU.mult, ALU.add)


def gather_sum(nc, m, table, rows_of, acc, weight=None, scale_rows=None, count=False, norm=False):
    with Stage(nc) as cs:
        staged, begun, ready, product, added = cs.sems("staged", "begun", "ready", "product", "added")
        scaled, counted, typed, turned, copied, looked, found, mine = cs.sems("scaled", "counted", "typed", "turned", "copied", "looked", "found", "mine")
        gathered, before = m.gathered, m.gathered_to
        m.gathered_to += 16 * TURNS
        block = cs.enter_context(nc.Block())
        side = m.psum[4:4 + PSLOTS]
        turn_ps = m.psum[6:8]

        @block.scalar
        def _(act):
            with act.Fori(0, TURNS) as i:
                for u in range(UNROLL):
                    if u % HALF == 0:
                        act.wait_ge(product, i * UNROLL + u + HALF)
                        act.copy(m.idx[:, u:u + HALF], rows_of[:, bass.ds(i * UNROLL + u, HALF)]).then_inc(staged, 1)
                    if scale_rows is not None:
                        act.wait_ge(gathered[u], before + 16 * (i + 1))
                        act.activation(m.rows[:, u, 0:D], m.rows[:, u, 0:D], ACT.Copy,
                                       scale=scale_rows[:, bass.ds(i * UNROLL + u, 1)]).then_inc(scaled, 1)
                    if norm:
                        act.wait_ge(turned, i * UNROLL + u + 1)
                        act.wait_ge(looked, i * UNROLL + u + 1)
                        act.copy(m.turned[:, u % 2, :], turn_ps[u % 2][:, 0:P]).then_inc(copied, 1)

        @block.gpsimd
        def _(pool):
            with pool.Fori(0, TURNS) as i:
                for h in range(2):
                    pool.wait_ge(staged, 2 * i + h + 1)
                    pool.sem_inc(begun, 1)
                    for u in range(h * HALF, (h + 1) * HALF):
                        pool.indirect_dma_start(m.rows[:, u, 0:D], None, table,
                                                bass.IndirectOffsetOnAxis(ap=m.idx[:, u:u + 1].bitcast(U32), axis=0),
                                                ).then_inc(gathered[u], 16)

        @block.tensor
        def _(pe):
            pe.sem_inc(product, UNROLL)
            pe.sem_inc(added, PSLOTS)
            pe.sem_inc(counted, PSLOTS)
            pe.sem_inc(looked, 2)
            pe.sem_inc(found, PSLOTS)
            pe.sem_inc(copied, 2)
            with pe.Fori(0, TURNS) as i:
                if norm:
                    _, tiles = nc.values_load_multi_w_load_instructions(
                        m.tile_of[0:1, bass.ds(i * UNROLL, UNROLL)], engines=[pe.engine], min_val=0, max_val=TILES,
                        skip_runtime_bounds_check_because="a chunk's tile counts bins, of which there are TILES")

                def look_up(u):
                    pe.wait_ge(copied, 2 + i * UNROLL + u + 1)
                    pe.wait_ge(found, i * UNROLL + u + 1)
                    pe.matmul(side[u % PSLOTS][:, 0:REL], m.turned[:, u % 2, :], m.count[:, bass.ds(tiles[u] * REL, REL)],
                              start=True, stop=True).then_inc(looked, 1)

                for u in range(UNROLL):
                    pe.wait_ge(ready, i * UNROLL + u + 1)
                    if norm:
                        pe.wait_ge(copied, i * UNROLL + u + 1)
                        pe.transpose(turn_ps[u % 2][:, 0:P], m.hot[:, u, :], m.ident[:, :]).then_inc(turned, 1)
                    if scale_rows is None:
                        pe.wait_ge(gathered[u], before + 16 * (i + 1))
                    else:
                        pe.wait_ge(scaled, i * UNROLL + u + 1)
                    if count:
                        pe.wait_ge(typed, i * UNROLL + u + 1)
                        pe.wait_ge(counted, i * UNROLL + u + 1)
                        pe.matmul(side[u % PSLOTS][:, 0:REL], m.hot[:, u, :], m.kind[:, u % PSLOTS, :],
                                  start=True, stop=True).then_inc(mine, 1)
                    pe.wait_ge(added, i * UNROLL + u + 1)
                    pe.matmul(m.psum[u % PSLOTS][:, 0:P], m.rows[:, u, 0:D], m.hot[:, u, :],
                              start=True, stop=True).then_inc(product, 1)
                    if norm:
                        look_up(u)

        @block.vector
        def _(dve):
            with dve.Fori(0, TURNS) as i:
                _, tiles = nc.values_load_multi_w_load_instructions(
                    m.tile_of[0:1, bass.ds(i * UNROLL, UNROLL)], engines=[dve.engine], min_val=0, max_val=TILES,
                    skip_runtime_bounds_check_because="a chunk's tile counts bins, of which there are TILES")

                def add(u):
                    if norm:
                        dve.wait_ge(looked, 2 + i * UNROLL + u + 1)
                        dve.scalar_tensor_tensor(m.kind[:, u % PSLOTS, :], m.iota[:, 0:REL], m.edge_type[:, bass.ds(i * UNROLL + u, 1)],
                                                 side[u % PSLOTS][:, 0:REL], ALU.is_equal, ALU.mult,
                                                 accum_out=m.edge_norm[:, bass.ds(i * UNROLL + u, 1)]).then_inc(found, 1)
                    if count:
                        dve.wait_ge(mine, i * UNROLL + u + 1)
                        dve.wait_ge(counted, PSLOTS + i * UNROLL + u)
                        at = m.count[:, bass.ds(tiles[u] * REL, REL)]
                        dve.tensor_tensor(at, at, side[u % PSLOTS][:, 0:REL], ALU.add).then_inc(counted, 1)
                    dve.wait_ge(product, (i + 1) * UNROLL + u + 1)
                    dve.wait_ge(added, PSLOTS + i * UNROLL + u)
                    at = acc[:, bass.ds(tiles[u] * P, P)]
                    dve.tensor_tensor(at, at, m.psum[u % PSLOTS][:, 0:P], ALU.add).then_inc(added, 1)

                for u in range(UNROLL):
                    c = i * UNROLL + u
                    dve.wait_ge(product, c + 1)
                    if count:
                        dve.wait_ge(product, c + UNROLL - 1)
                        dve.tensor_scalar(m.kind[:, u % PSLOTS, :], m.iota[:, 0:REL], m.edge_type[:, bass.ds(c, 1)], None,
                                          ALU.is_equal).then_inc(typed, 1)
                    if norm:
                        dve.wait_ge(looked, c + 1)
                    if weight is None:
                        dve.tensor_scalar(m.hot[:, u, :], m.iota[:, :], m.edge_dst[:, bass.ds(c, 1)], None,
                                          ALU.is_equal).then_inc(ready, 1)
                    else:
                        dve.tensor_scalar(m.hot[:, u, :], m.iota[:, :], m.edge_dst[:, bass.ds(c, 1)],
                                          weight[:, bass.ds(c, 1)], ALU.is_equal, ALU.mult).then_inc(ready, 1)
                    if u >= 1:
                        add(u - 1)
                add(UNROLL - 1)


def linear(nc, m, w, x, out, func=ACT.Identity, bias=0.0, times=None):
    with Stage(nc) as cs:
        product, taken = cs.sems("product", "taken")
        block = cs.enter_context(nc.Block())

        @block.tensor
        def _(pe):
            pe.sem_inc(taken, 2)
            with pe.Fori(0, BLKS // 2) as j:
                for k in range(2):
                    pe.wait_ge(taken, 2 * j + k + 1)
                    pe.matmul(m.psum[k][:, 0:BLK], w, x[:, bass.ds((2 * j + k) * BLK, BLK)],
                              start=True, stop=True).then_inc(product, 1)

        @block.scalar
        def _(act):
            with act.Fori(0, BLKS // 2) as j:
                for k in range(2):
                    act.wait_ge(product, 2 * j + k + 1)
                    act.activation(out[:, bass.ds((2 * j + k) * BLK, BLK)], m.psum[k][:, 0:BLK], func,
                                   bias=bias).then_inc(taken, 1)

        if times is not None:
            @block.vector
            def _(dve):
                with dve.Fori(0, BLKS // 2) as j:
                    for k in range(2):
                        dve.wait_ge(taken, 2 * j + k + 3)
                        at = out[:, bass.ds((2 * j + k) * BLK, BLK)]
                        dve.tensor_tensor(at, at, times[:, bass.ds((2 * j + k) * BLK, BLK)], ALU.mult)



SETS = 4


def write_table(nc, m, x, width, stage, store, scale=None):
    step = min(width, 512)
    banks = width // step
    with Stage(nc) as cs:
        held, product, taken = cs.sems("held", "product", "taken")
        stored = [cs.sem(f"stored{k}") for k in range(SETS)]
        block = cs.enter_context(nc.Block())
        turns = TILES // SETS
        assert turns * SETS + 1 == TILES

        @block.vector
        def _(dve):
            def tile(j, k):
                dve.wait_ge(product, (j * SETS + k + 1) * banks)
                dve.tensor_copy(m.hot[:, k, :], x[:, bass.ds((j * SETS + k) * P, P)]).then_inc(held, 1)

            dve.sem_inc(product, SETS * banks)
            with dve.Fori(0, turns) as j:
                for k in range(SETS):
                    tile(j, k)
            tile(turns, 0)

        @block.tensor
        def _(pe):
            def tile(j, k):
                pe.wait_ge(held, j * SETS + k + 1)
                for h in range(banks):
                    pe.wait_ge(taken, (j * SETS + k) * banks + h + 1)
                    pe.matmul(m.psum[k * banks + h][:, 0:step], m.hot[:, k, :],
                              m.weights[:, h * step:(h + 1) * step], start=True, stop=True).then_inc(product, 1)

            pe.sem_inc(taken, SETS * banks)
            with pe.Fori(0, turns) as j:
                for k in range(SETS):
                    tile(j, k)
            tile(turns, 0)

        @block.scalar
        def _(act):
            def tile(j, k):
                for h in range(banks):
                    act.wait_ge(product, (SETS + j * SETS + k) * banks + h + 1)
                    act.activation(stage(k)[:, h * step:(h + 1) * step], m.psum[k * banks + h][:, 0:step], ACT.Copy,
                                   scale=1.0 if scale is None else scale[:, bass.ds(j * SETS + k, 1)]).then_inc(taken, 1)

            for k in range(SETS):
                tile(0, k)
            with act.Fori(1, turns) as j:
                for k in range(SETS):
                    act.wait_ge(stored[k], 16 * j)
                    tile(j, k)
            act.wait_ge(stored[0], 16 * turns)
            tile(turns, 0)

        @block.sync
        def _(sp):
            def tile(j, k):
                sp.wait_ge(taken, (SETS + j * SETS + k + 1) * banks)
                sp.dma_start(store(j * SETS + k), stage(k)).then_inc(stored[k], 16)

            with sp.Fori(0, turns) as j:
                for k in range(SETS):
                    tile(j, k)
            tile(turns, 0)
            sp.wait_ge(stored[0], 16 * (turns + 1))
            for k in range(1, SETS):
                sp.wait_ge(stored[k], 16 * turns)


def batch_norm(nc, m, x, out, gamma, beta, func=ACT.Identity):
    cut = 250
    parts = N // cut
    assert parts * cut == N
    stats = m.bnc[:, 0:6 * parts]
    mv, std, rstd, scale, shift = (m.bnc[:, 6 * parts + o:6 * parts + o + n] for o, n in ((0, 2), (2, 1), (3, 1), (4, 1), (5, 1)))
    with Stage(nc) as cs:
        step, rooted, ready = cs.sems("step", "rooted", "ready")
        block = cs.enter_context(nc.Block())

        @block.vector
        def _(dve):
            with dve.Fori(0, parts) as j:
                dve.bn_stats(stats[:, bass.ds(j * 6, 6)], x[:, bass.ds(j * cut, cut)]).then_inc(step, 1)
            dve.wait_ge(step, parts)
            dve.bn_aggr(mv, stats).then_inc(step, 1)
            dve.wait_ge(rooted, 1)
            dve.reciprocal(rstd, std).then_inc(step, 1)
            dve.wait_ge(step, parts + 2)
            dve.tensor_tensor(scale, gamma, rstd, ALU.mult).then_inc(step, 1)
            dve.wait_ge(step, parts + 3)
            dve.tensor_tensor(shift, scale, mv[:, 0:1], ALU.mult).then_inc(step, 1)
            dve.wait_ge(step, parts + 4)
            dve.tensor_tensor(shift, beta, shift, ALU.subtract).then_inc(ready, 1)

        @block.scalar
        def _(act):
            act.wait_ge(step, parts + 1)
            act.activation(std, mv[:, 1:2], ACT.Sqrt, bias=m.eps).then_inc(rooted, 1)
            act.wait_ge(ready, 1)
            act.activation(out[:, 0:NPAD], x[:, 0:NPAD], func, bias=shift, scale=scale)


def combine(nc, m, parts):
    with Stage(nc) as cs:
        step = cs.sem("step")
        block = cs.enter_context(nc.Block())

        @block.vector
        def _(dve):
            for n, (out, in0, scalar, in1, op0, op1) in enumerate(parts):
                if n:
                    dve.wait_ge(step, n)
                dve.scalar_tensor_tensor(out, in0, scalar, in1, op0, op1).then_inc(step, 1)


def layer_norm(nc, m, x, out, tmp):
    with Stage(nc) as cs:
        mean, centred, squared, var, rooted, inverse, done = cs.sems("mean", "centred", "squared", "var", "rooted", "inverse", "done")
        block = cs.enter_context(nc.Block())
        sq = [tmp[:, k * BLK:(k + 1) * BLK] for k in range(2)]
        std = [tmp[:, (2 + k) * BLK:(3 + k) * BLK] for k in range(2)]
        at = lambda a, j, k: a[:, bass.ds((2 * j + k) * BLK, BLK)]

        @block.tensor
        def _(pe):
            pe.sem_inc(centred, 2)
            pe.sem_inc(rooted, 2)
            with pe.Fori(0, BLKS // 2) as j:
                for k in range(2):
                    pe.wait_ge(centred, 2 * j + k + 1)
                    pe.matmul(m.psum[k][:, 0:BLK], m.mean[:, :], at(x, j, k), start=True, stop=True).then_inc(mean, 1)
                for k in range(2):
                    pe.wait_ge(squared, 2 * j + k + 1)
                    pe.wait_ge(rooted, 2 * j + k + 1)
                    pe.matmul(m.psum[2 + k][:, 0:BLK], m.mean[:, :], sq[k], start=True, stop=True).then_inc(var, 1)

        @block.vector
        def _(dve):
            with dve.Fori(0, BLKS // 2) as j:
                for k in range(2):
                    dve.wait_ge(mean, 2 * j + k + 1)
                    dve.tensor_tensor(at(x, j, k), at(x, j, k), m.psum[k][:, 0:BLK], ALU.subtract).then_inc(centred, 1)
                for k in range(2):
                    dve.wait_ge(rooted, 2 * j + k + 3)
                    dve.reciprocal(std[k], std[k]).then_inc(inverse, 1)
                    dve.wait_ge(inverse, 2 * j + k + 1)
                    dve.tensor_tensor(at(out, j, k), at(x, j, k), std[k], ALU.mult).then_inc(done, 1)

        @block.scalar
        def _(act):
            act.sem_inc(done, 2)
            with act.Fori(0, BLKS // 2) as j:
                for k in range(2):
                    act.wait_ge(centred, 2 * j + k + 3)
                    act.wait_ge(rooted, 2 * j + k + 1)
                    act.activation(sq[k], at(x, j, k), ACT.Square).then_inc(squared, 1)
                for k in range(2):
                    act.wait_ge(var, 2 * j + k + 1)
                    act.wait_ge(done, 2 * j + k + 1)
                    act.activation(std[k], m.psum[2 + k][:, 0:BLK], ACT.Sqrt, bias=m.eps).then_inc(rooted, 1)


def turn_tiles(nc, m, source, target):
    with Stage(nc) as cs:
        held, turned, taken = cs.sems("held", "turned", "taken")
        block = cs.enter_context(nc.Block())
        group = 7
        assert group * group == TILES

        @block.vector
        def _(dve):
            dve.sem_inc(turned, group)
            with dve.Fori(0, group) as j:
                for k in range(group):
                    dve.wait_ge(turned, j * group + k + 1)
                    dve.tensor_copy(m.hot[:, k, :], source[:, bass.ds((j * group + k) * P, P)]).then_inc(held, 1)

        @block.tensor
        def _(pe):
            pe.sem_inc(taken, group)
            with pe.Fori(0, group) as j:
                for k in range(group):
                    pe.wait_ge(held, j * group + k + 1)
                    pe.wait_ge(taken, j * group + k + 1)
                    pe.transpose(m.psum[k][:, 0:P], m.hot[:, k, :], m.ident[:, :]).then_inc(turned, 1)

        @block.scalar
        def _(act):
            with act.Fori(0, group) as j:
                for k in range(group):
                    act.wait_ge(turned, group + j * group + k + 1)
                    act.copy(target[:, bass.ds((j * group + k) * P, P)], m.psum[k][:, 0:P]).then_inc(taken, 1)


def load_vectors(nc, m, a):
    with Stage(nc) as cs:
        clear, loaded, done = cs.sems("clear", "loaded", "done")
        block = cs.enter_context(nc.Block())
        full = TILES - 1
        x_rows = m.big[4][:, 0:NPAD].rearrange("p (t d) -> p t d", d=D)
        w_nodes = m.big[3]

        @block.vector
        def _(dve):
            dve.memset(x_rows[:, full, :], 0.0).then_inc(clear, 1)
            dve.wait_ge(loaded, 16 * (len(VECTORS) + 1))
            dve.tensor_scalar(m.one_eps, m.one_eps, 1.0, None, ALU.add)

        @block.sync
        def _(sp):
            with nc.allow_non_contiguous_dma("a word to a partition"):
                for n, name in enumerate(VECTORS):
                    sp.dma_start(m.par[:, n:n + 1], a[name].rearrange("(p o) -> p o", o=1)).then_inc(loaded, 16)
                sp.dma_start(m.one_eps, a["L0_gnn_eps"].rearrange("(p o) -> p o", o=1).to_broadcast([P, 1])).then_inc(loaded, 16)
            sp.dma_start(x_rows[:, 0:full, :], a["x"][0:full * P, :].rearrange("(t p) d -> p t d", p=P)).then_inc(done, 16)
            sp.wait_ge(clear, 1)
            sp.dma_start(x_rows[0:LAST, full, :], a["x"][full * P:N, :]).then_inc(done, 16)
            sp.wait_ge(done, 32)


def load(nc, m, pairs, zero=()):
    with Stage(nc) as cs:
        loaded = cs.sem("loaded")
        block = cs.enter_context(nc.Block())

        @block.sync
        def _(sp):
            for out, in_ in pairs:
                sp.dma_start(out, in_).then_inc(loaded, 16)
            if pairs:
                sp.wait_ge(loaded, 16 * len(pairs))

        if zero:
            @block.vector
            def _(dve):
                for z in zero:
                    dve.memset(z, 0.0)


def degrees(nc, m, wide):
    with Stage(nc) as cs:
        step, rooted, spread, product, taken = cs.sems("step", "rooted", "spread", "product", "taken")
        block = cs.enter_context(nc.Block())
        group = 7
        assert group * group == TILES

        @block.vector
        def _(dve):
            dve.tensor_reduce(m.dinv[:, :], m.count[:, :].rearrange("p (t r) -> p t r", r=REL), AX.X, ALU.add).then_inc(step, 1)
            dve.wait_ge(step, 1)
            dve.tensor_scalar(m.count[:, :], m.count[:, :], 1.0, None, ALU.max).then_inc(step, 1)
            dve.wait_ge(step, 2)
            dve.reciprocal(m.count[:, :], m.count[:, :])
            dve.wait_ge(rooted, 1)
            dve.reciprocal(m.dinv[:, :], m.dinv[:, :]).then_inc(step, 1)
            dve.wait_ge(step, 3)
            dve.sem_inc(product, group)
            with dve.Fori(0, group) as j:
                for k in range(group):
                    dve.wait_ge(product, j * group + k + 1)
                    dve.tensor_scalar(m.hot[:, k, :], m.ident[:, :], m.dinv[:, bass.ds(j * group + k, 1)], None,
                                      ALU.mult).then_inc(spread, 1)

        @block.scalar
        def _(act):
            act.wait_ge(step, 1)
            act.activation(m.dinv[:, :], m.dinv[:, :], ACT.Sqrt, bias=1.0).then_inc(rooted, 1)
            with act.Fori(0, group) as j:
                for k in range(group):
                    act.wait_ge(product, group + j * group + k + 1)
                    act.copy(wide[:, bass.ds((j * group + k) * P, P)], m.psum[k][:, 0:P]).then_inc(taken, 1)

        @block.tensor
        def _(pe):
            pe.sem_inc(taken, group)
            with pe.Fori(0, group) as j:
                for k in range(group):
                    pe.wait_ge(spread, j * group + k + 1)
                    pe.wait_ge(taken, j * group + k + 1)
                    pe.matmul(m.psum[k][:, 0:P], m.ones[:, :], m.hot[:, k, :], start=True, stop=True).then_inc(product, 1)



def attention_table(nc, m, x, stage, target_score):
    turns = TILES // SETS
    a_source, a_target = m.weights[:, 2 * D:3 * D], m.weights[:, 3 * D:4 * D]
    with Stage(nc) as cs:
        held, product, taken, scored = cs.sems("held", "product", "taken", "scored")
        stored = [cs.sem(f"stored{k}") for k in range(SETS)]
        block = cs.enter_context(nc.Block())

        @block.vector
        def _(dve):
            def hold(j, k):
                dve.wait_ge(product, j * SETS + k + 1)
                dve.tensor_copy(m.hot[:, k, :], x[:, bass.ds((j * SETS + k) * P, P)]).then_inc(held, 1)

            def score(j, k):
                dve.wait_ge(taken, SETS + j * SETS + k + 1)
                dve.scalar_tensor_tensor(m.hot[:, SETS + k, :], stage(k)[:, 0:D], 1.0, a_source, ALU.mult, ALU.mult,
                                         accum_out=stage(k)[:, D:D + 1]).then_inc(scored, 1)
                dve.scalar_tensor_tensor(m.hot[:, 2 * SETS + k, :], stage(k)[:, 0:D], 1.0, a_target, ALU.mult, ALU.mult,
                                         accum_out=target_score[:, bass.ds(j * SETS + k, 1)]).then_inc(scored, 1)

            dve.sem_inc(product, SETS)
            with dve.Fori(0, turns) as j:
                for k in range(SETS):
                    hold(j, k)
                for k in range(SETS):
                    score(j, k)
                dve.wait_ge(scored, 2 * SETS * (j + 1))
            hold(turns, 0)
            score(turns, 0)

        @block.tensor
        def _(pe):
            def tile(j, k):
                pe.wait_ge(held, j * SETS + k + 1)
                pe.wait_ge(taken, j * SETS + k + 1)
                pe.matmul(m.psum[k][:, 0:D], m.hot[:, k, :], m.weights[:, D:2 * D], start=True, stop=True).then_inc(product, 1)

            pe.sem_inc(taken, SETS)
            with pe.Fori(0, turns) as j:
                for k in range(SETS):
                    tile(j, k)
            tile(turns, 0)

        @block.scalar
        def _(act):
            def tile(j, k):
                act.wait_ge(product, SETS + j * SETS + k + 1)
                act.copy(stage(k)[:, 0:D], m.psum[k][:, 0:D]).then_inc(taken, 1)

            for k in range(SETS):
                tile(0, k)
            with act.Fori(1, turns) as j:
                for k in range(SETS):
                    act.wait_ge(stored[k], 16 * j)
                    tile(j, k)
            act.wait_ge(stored[0], 16 * turns)
            tile(turns, 0)

        @block.sync
        def _(sp):
            def tile(j, k):
                sp.wait_ge(scored, 2 * (j * SETS + k + 1))
                sp.dma_start(m.att_table[bass.ds((j * SETS + k) * P, P), :], stage(k)).then_inc(stored[k], 16)

            with sp.Fori(0, turns) as j:
                for k in range(SETS):
                    tile(j, k)
            tile(turns, 0)
            sp.wait_ge(stored[0], 16 * (turns + 1))
            for k in range(1, SETS):
                sp.wait_ge(stored[k], 16 * turns)


def wait(engine, sem, count):
    if not isinstance(count, int) or count > 0:
        engine.wait_ge(sem, count)


def attend(nc, m, acc, neg_target, neg_max):
    QUARTER = UNROLL // 4
    with Stage(nc) as cs:
        (staged, begun, marked, lifted, turned, summed, scored, lowest, new_max, grown, kept, powered, shrunk, back, weights,
         product, added) = cs.sems("staged", "begun", "marked", "lifted", "turned", "summed", "scored", "lowest", "new_max", "grown",
                                   "kept", "powered", "shrunk", "back", "weights", "product", "added")
        gathered, before = m.gathered, m.gathered_to
        m.gathered_to += 16 * TURNS
        block = cs.enter_context(nc.Block())
        mark = m.hot[:, 0:2, :]
        lift = m.hot[:, 2:4, :]
        score = m.hot[:, 4:6, :]
        power = m.hot[:, 6:8, :]
        weight = m.hot[:, 8:10, :]
        both = m.hot[:, 10:12, :]
        turn_ps, back_ps, sums = m.psum[0:2], m.psum[2:4], m.psum[4:6]
        low = m.small[:, 480:482]
        neg = m.small[:, 482:484]
        drop = m.small[:, 484:486]
        factor = m.small[:, 486:490]

        def tiles_of(engine, first, n):
            _, tiles = nc.values_load_multi_w_load_instructions(
                m.tile_of[0:1, bass.ds(first, n)], engines=[engine.engine], min_val=0, max_val=TILES,
                skip_runtime_bounds_check_because="a chunk's tile counts bins, of which there are TILES")
            return tiles

        def turns(engine, lags, steps, needs_tiles):
            deepest = max(lag for lag, _ in lags)
            tiles = tiles_of(engine, 0, UNROLL) if needs_tiles else None
            for u in range(UNROLL):
                for lag, name in lags:
                    if u >= lag:
                        steps(0, u - lag, name, tiles and tiles[u - lag])
            with engine.Fori(1, TURNS) as i:
                tiles = tiles_of(engine, i * UNROLL - deepest, UNROLL + deepest) if needs_tiles else None
                for u in range(UNROLL):
                    for lag, name in lags:
                        steps(i, u - lag, name, tiles and tiles[deepest + u - lag])
            tiles = tiles_of(engine, TURNS * UNROLL - deepest, deepest) if needs_tiles and deepest else None
            for u in range(deepest):
                for lag, name in lags:
                    if lag > u:
                        steps(TURNS, u - lag, name, tiles and tiles[deepest + u - lag])

        @block.gpsimd
        def _(pool):
            with pool.Fori(0, TURNS) as i:
                for u in range(UNROLL):
                    if u % QUARTER == 0:
                        pool.wait_ge(staged, 4 * i + u // QUARTER + 1)
                        pool.sem_inc(begun, 1)
                    pool.indirect_dma_start(m.rows[:, u, :], None, m.att_table,
                                            bass.IndirectOffsetOnAxis(ap=m.idx[:, u:u + 1].bitcast(U32), axis=0),
                                            ).then_inc(gathered[u], 16)

        @block.scalar
        def _(act):
            def stage(turn, q):
                at = bass.ds(turn * UNROLL + q * QUARTER, QUARTER)
                act.copy(m.idx[:, q * QUARTER:(q + 1) * QUARTER], m.edge_src[:, at]).then_inc(staged, 1)

            def steps(i, u, what, tile):
                c = i * UNROLL + u
                if what == "sum":
                    act.wait_ge(turned, c + 1)
                    wait(act, scored, c - 1)
                    act.activation(both[:, u % 2, :], turn_ps[u % 2][:, 0:P], ACT.Identity,
                                   bias=m.target_score[:, bass.ds(tile, 1)]).then_inc(summed, 1)
                elif what == "back":
                    act.wait_ge(back, c + 1)
                    wait(act, product, c - 1)
                    act.copy(weight[:, u % 2, :], back_ps[u % 2][:, 0:P]).then_inc(weights, 1)
                elif what == "lift":
                    slot = u % UNROLL
                    act.wait_ge(marked, c + 1)
                    act.wait_ge(gathered[slot], before + 16 * (i + 1 if u >= 0 else i))
                    wait(act, turned, c - 1)
                    act.activation(lift[:, u % 2, :], mark[:, u % 2, :], ACT.Identity,
                                   bias=m.rows[:, slot, D:D + 1]).then_inc(lifted, 1)
                    if u % QUARTER == 0:
                        q = (u // QUARTER + 2) % 4
                        if q < 2:
                            ahead = i + 1
                        else:
                            ahead = i
                        if not isinstance(ahead, int) or ahead > 0:
                            act.wait_ge(product, (ahead - 1) * UNROLL + (q + 1) * QUARTER)
                            stage(ahead, q)
                elif what == "power":
                    act.wait_ge(new_max, c + 1)
                    wait(act, back, c - 1)
                    act.activation(power[:, u % 2, :], score[:, u % 2, :], ACT.Exp, bias=neg[:, u % 2:u % 2 + 1]).then_inc(powered, 1)
                else:
                    act.wait_ge(grown, c + 1)
                    wait(act, added, c - 3)
                    act.activation(factor[:, u % 4:u % 4 + 1], drop[:, u % 2:u % 2 + 1], ACT.Exp).then_inc(shrunk, 1)

            for q in range(4):
                stage(0, q)
            turns(act, ((2, "sum"), (1, "lift"), (4, "power"), (5, "back"), (5, "shrink")), steps, True)

        @block.tensor
        def _(pe):
            def steps(i, u, what, tile):
                c = i * UNROLL + u
                if what == "turn":
                    pe.wait_ge(lifted, c + 1)
                    wait(pe, summed, c - 1)
                    pe.transpose(turn_ps[u % 2][:, 0:P], lift[:, u % 2, :], m.ident[:, :]).then_inc(turned, 1)
                elif what == "back":
                    pe.wait_ge(powered, c + 1)
                    wait(pe, weights, c - 1)
                    pe.transpose(back_ps[u % 2][:, 0:P], power[:, u % 2, :], m.ident[:, :]).then_inc(back, 1)
                else:
                    pe.wait_ge(weights, c + 1)
                    wait(pe, added, c - 1)
                    pe.matmul(sums[u % 2][:, 0:ROW], weight[:, u % 2, :], m.rows[:, u % UNROLL, :],
                              start=True, stop=True).then_inc(product, 1)

            turns(pe, ((1, "turn"), (4, "back"), (5, "sum")), steps, False)

        @block.vector
        def _(dve):
            def steps(i, u, what, tile):
                c = i * UNROLL + u
                if what == "mark":
                    wait(dve, lifted, c - 1)
                    dve.tensor_scalar(mark[:, u % 2, :], m.iota[:, :], m.edge_dst[:, bass.ds(c, 1)], LOW,
                                      ALU.not_equal, ALU.mult).then_inc(marked, 1)
                elif what == "add":
                    dve.wait_ge(product, c + 1)
                    dve.wait_ge(shrunk, c + 1)
                    wait(dve, added, c)
                    at = acc[:, bass.ds(tile * ROW, ROW)]
                    dve.scalar_tensor_tensor(at, at, factor[:, u % 4:u % 4 + 1], sums[u % 2][:, 0:ROW],
                                             ALU.mult, ALU.add).then_inc(added, 1)
                elif what == "score":
                    dve.wait_ge(summed, c + 1)
                    wait(dve, powered, c - 1)
                    dve.scalar_tensor_tensor(score[:, u % 2, :], both[:, u % 2, :], LEAK, both[:, u % 2, :],
                                             ALU.mult, ALU.max).then_inc(scored, 1)
                elif what == "lowest":
                    dve.wait_ge(scored, c + 1)
                    dve.tensor_reduce(low[:, u % 2:u % 2 + 1], score[:, u % 2, :], AX.X, ALU.max, negate=True).then_inc(lowest, 1)
                elif what == "new":
                    wait(dve, powered, c - 1)
                    wait(dve, kept, c)
                    dve.wait_ge(lowest, c + 1)
                    dve.tensor_tensor(neg[:, u % 2:u % 2 + 1], low[:, u % 2:u % 2 + 1], neg_max[:, bass.ds(tile, 1)],
                                      ALU.min).then_inc(new_max, 1)
                elif what == "drop":
                    wait(dve, shrunk, c - 1)
                    dve.wait_ge(new_max, c + 1)
                    dve.tensor_tensor(drop[:, u % 2:u % 2 + 1], neg[:, u % 2:u % 2 + 1], neg_max[:, bass.ds(tile, 1)],
                                      ALU.subtract).then_inc(grown, 1)
                elif what == "keep":
                    at = neg_max[:, bass.ds(tile, 1)]
                    dve.wait_ge(grown, c + 1)
                    dve.tensor_tensor(at, at, neg[:, u % 2:u % 2 + 1], ALU.min).then_inc(kept, 1)

            turns(dve, ((3, "score"), (4, "drop"), (0, "mark"), (4, "keep"), (3, "lowest"), (6, "add"), (3, "new")), steps, True)


def attention(nc, m, a, out):
    B = [b[:, 0:NPAD] for b in m.big]
    W = m.weights
    spread = lambda f, n: f.rearrange("(o d) -> o d", o=1).to_broadcast([P, n])
    target_score, neg_max = m.target_score, m.small[:, 64:64 + TILES + 1]
    load(nc, m, [(W[:, 0:D], a["L3_gnn_W_lin"]), (W[:, 2 * D:4 * D], spread(a["L3_gnn_a"], 2 * D)),
                 (W[:, 4 * D:5 * D], spread(a["L3_gnn_gamma"], D)), (W[:, 5 * D:6 * D], spread(a["L3_gnn_beta"], D))],
         zero=[m.big[1][:, 0:(TILES + 1) * ROW], target_score])

    with Stage(nc) as cs:
        turned = cs.sem("turned")
        block = cs.enter_context(nc.Block())

        @block.tensor
        def _(pe):
            pe.transpose(m.psum[0][:, 0:D], W[:, 0:D], m.ident[:, :]).then_inc(turned, 1)

        @block.scalar
        def _(act):
            act.wait_ge(turned, 1)
            act.copy(W[:, D:2 * D], m.psum[0][:, 0:D])

        @block.vector
        def _(dve):
            dve.memset(neg_max, -FLOOR)
            dve.memset(m.rows[:, 0:SETS, D + 1:D + 2], 1.0)

    attention_table(nc, m, B[0], lambda k: m.rows[:, k, :], target_score)
    attend(nc, m, m.big[1], target_score, neg_max)
    turn_tiles(nc, m, B[0], B[3])
    finish(nc, m, m.big[1], B[3], B[2], B[4], out)


def finish(nc, m, acc, x, y, tmp, out):
    shape = [P, TILES, D]
    view = lambda b: b.rearrange("p (t d) -> p t d", d=D)
    sums = acc[:, 0:TILES * ROW].rearrange("p (t r) -> p t r", r=ROW)
    x, y, tmp = view(x), view(y), view(tmp)
    z, mean, var = (m.small[:, 128 + 64 * n:128 + 64 * n + TILES] for n in range(3))
    gamma, beta = m.weights[:, 4 * D:5 * D], m.weights[:, 5 * D:6 * D]
    per_node = lambda v: v.unsqueeze(2).to_broadcast(shape)
    per_feature = lambda v: v.unsqueeze(1).to_broadcast(shape)
    with Stage(nc) as cs:
        step, asked, rooted, stored = cs.sems("step", "asked", "rooted", "stored")
        block = cs.enter_context(nc.Block())

        @block.vector
        def _(dve):
            steps = [0]

            def then(ins):
                steps[0] += 1
                ins.then_inc(step, 1)
                dve.wait_ge(step, steps[0])

            def norm(turn):
                then(dve.tensor_reduce(mean, y, AX.X, ALU.add))
                then(dve.tensor_scalar(mean, mean, 1.0 / D, None, ALU.mult))
                then(dve.tensor_tensor(y, y, per_node(mean), ALU.subtract))
                then(dve.tensor_tensor(tmp, y, y, ALU.mult))
                then(dve.tensor_reduce(var, tmp, AX.X, ALU.add))
                dve.tensor_scalar(var, var, 1.0 / D, None, ALU.mult).then_inc(asked, 1)
                dve.wait_ge(rooted, turn)
                then(dve.reciprocal(var, var))

            then(dve.tensor_scalar(z, sums[:, :, D + 1], 1e-30, None, ALU.max))
            then(dve.reciprocal(z, z))
            then(dve.tensor_tensor(y, sums[:, :, 0:D], per_node(z), ALU.mult))
            then(dve.tensor_tensor(y, y, x, ALU.add))
            norm(1)
            then(dve.tensor_tensor(y, y, per_node(var), ALU.mult))
            then(dve.tensor_tensor(y, y, per_feature(gamma), ALU.mult))
            then(dve.tensor_tensor(y, y, per_feature(beta), ALU.add))
            then(dve.tensor_tensor(y, y, x, ALU.add))
            norm(2)
            dve.tensor_tensor(y, y, per_node(var), ALU.mult).then_inc(asked, 1)

        @block.scalar
        def _(act):
            for turn in (1, 2):
                act.wait_ge(asked, turn)
                act.activation(var, var, ACT.Sqrt, bias=m.eps).then_inc(rooted, 1)

        @block.sync
        def _(sp):
            full = TILES - 1
            sp.wait_ge(asked, 3)
            sp.dma_start(out[0:full * P, :].rearrange("(t p) d -> p t d", p=P), y[:, 0:full, :]).then_inc(stored, 16)
            sp.dma_start(out[full * P:N, :], y[0:LAST, full, :]).then_inc(stored, 16)
            sp.wait_ge(stored, 32)


VECTORS = ["L0_gnn_b1", "L0_gnn_b2", "L0_gnn_gamma", "L0_gnn_beta", "L1_gnn_bn0_gamma", "L1_gnn_bn0_beta",
           "L1_gnn_b1", "L1_gnn_bn1_gamma", "L1_gnn_bn1_beta", "L1_gnn_b2", "L1_gnn_bn2_gamma", "L1_gnn_bn2_beta",
           "L2_gnn_b1", "L2_gnn_b2", "L2_gnn_b3", "L2_gnn_res_b"]


def build(nc, a, out):
    with ExitStack() as cs:
        m = Memory(nc, cs)
        vec = {name: m.par[:, n:n + 1] for n, name in enumerate(VECTORS)}
        B = [b[:, 0:NPAD] for b in m.big]
        acc_whole = m.big[1][:, 0:ACCW]
        W = m.weights

        make_constants(nc, m)
        edges = a["src"], a["dst"], a["edge_type_8"], a["edge_weight1"].rearrange("e o -> (e o)")
        load_columns(nc, m, *edges)
        pair_columns(nc, m)
        unsorted = nc.values_load(m.unsorted[0:1, 0:1], min_val=0, max_val=1)
        with nc.If(unsorted != 0):
            nc.all_engine_barrier()
            load_edges(nc, m, *edges)
            sort_edges(nc, m)
        with nc.Else():
            nc.all_engine_barrier()
            spread_columns(nc, m)
        edge_rows(nc, m)

        load_vectors(nc, m, a)
        turn_tiles(nc, m, B[4], B[0])
        load(nc, m, [(W[:, 0:D], a["L0_gnn_W1"]), (W[:, D:2 * D], a["L0_gnn_W2"]),
                     (B[4][:, 0:N], a["node_vec1"].rearrange("n o -> o n").to_broadcast([P, N]))],
             zero=[acc_whole, m.count[:, :], B[4][:, N:NPAD]])
        gather_sum(nc, m, a["x"], m.edge_src, m.big[1], scale_rows=m.edge_w, count=True)
        combine(nc, m, [(B[2], B[0], m.one_eps, B[1], ALU.mult, ALU.add)])
        linear(nc, m, W[:, 0:D], B[2], B[3], ACT.Relu, vec["L0_gnn_b1"])
        linear(nc, m, W[:, D:2 * D], B[3], B[2], ACT.Identity, vec["L0_gnn_b2"], times=B[4])
        batch_norm(nc, m, B[2], B[2], vec["L0_gnn_gamma"], vec["L0_gnn_beta"], ACT.Relu)
        combine(nc, m, [(B[2], B[0], 2.0, B[2], ALU.mult, ALU.add)])
        layer_norm(nc, m, B[2], B[0], B[3])

        degrees(nc, m, B[4])
        batch_norm(nc, m, B[0], B[2], vec["L1_gnn_bn0_gamma"], vec["L1_gnn_bn0_beta"])
        load(nc, m, [(W[:, 0:D], a["L1_gnn_W1"]), (W[:, D:2 * D], a["L1_gnn_W2"])])
        table = m.table[0:NPAD, :]
        for layer in (1, 2):
            x = B[2] if layer == 1 else B[3]
            if layer == 2:
                load(nc, m, [(W[:, 0:D], a["L1_gnn_W2"])])
            linear(nc, m, W[:, 0:D], x, B[1], times=B[4])
            write_table(nc, m, x, D, lambda k: m.rows[:, k, 0:D], lambda t: table[bass.ds(t * P, P), :], scale=m.dinv)
            gather_sum(nc, m, table, m.edge_src, m.big[1], norm=layer == 1)
            combine(nc, m, [(B[1], B[1], 1.0, B[4], ALU.mult, ALU.mult)])
            relu_bias(nc, m, B[1], B[3], vec[f"L1_gnn_b{layer}"])
            batch_norm(nc, m, B[3], B[3], vec[f"L1_gnn_bn{layer}_gamma"], vec[f"L1_gnn_bn{layer}_beta"])
        combine(nc, m, [(B[3], B[3], 1.0, B[2], ALU.mult, ALU.add), (B[3], B[3], 1.0, B[0], ALU.mult, ALU.add)])
        layer_norm(nc, m, B[3], B[0], B[2])

        load(nc, m, [(W[:, 0:D], a["L2_gnn_res_w"])])
        linear(nc, m, W[:, 0:D], B[0], B[2], bias=vec["L2_gnn_res_b"])
        for layer in (1, 2, 3):
            x = B[0] if layer == 1 else B[3]
            load(nc, m, [(W[:, 0:D], a[f"L2_gnn_root{layer}"])])
            linear(nc, m, W[:, 0:D], x, B[1])
            load(nc, m, [(W[:, :].rearrange("p (r d) -> p r d", d=D), a[f"L2_gnn_W{layer}"].rearrange("r p d -> p r d"))])
            by_tile = m.table.rearrange("(r n) d -> n r d", n=NPAD)
            write_table(nc, m, x, REL * D, lambda k: m.big[4][:, k * REL * D:(k + 1) * REL * D],
                        lambda t: by_tile[bass.ds(t * P, P), :, :])
            gather_sum(nc, m, m.table, m.edge_row, m.big[1], weight=m.edge_norm)
            relu_bias(nc, m, B[1], B[3], vec[f"L2_gnn_b{layer}"])
            combine(nc, m, [(B[3], B[3], 1.0, B[2], ALU.mult, ALU.add)])
        combine(nc, m, [(B[3], B[3], 1.0, B[0], ALU.mult, ALU.add)])
        layer_norm(nc, m, B[3], B[0], B[2])
        attention(nc, m, a, out)


def relu_bias(nc, m, x, out, bias):
    with Stage(nc) as cs:
        block = cs.enter_context(nc.Block())

        @block.scalar
        def _(act):
            act.activation(out, x, ACT.Relu, bias=bias)


def kernel(**inputs):
    import numpy as _np
    import concourse.bacc as _bacc
    from concourse import mybir as _mybir
    from concourse.bass_utils import run_bass_kernel_spmd as _run

    nc = _bacc.Bacc("TRN2", target_bir_lowering=False, num_devices=1)
    arrays, args = {}, {}
    for name, value in inputs.items():
        v = _np.ascontiguousarray(value)
        arrays[f"in_{name}"] = v
        args[name] = nc.dram_tensor(f"in_{name}", v.shape, _mybir.dt.from_np(v.dtype), kind="ExternalInput").ap()
    out = nc.dram_tensor("out", (N, D), F32, kind="ExternalOutput").ap()
    build(nc, args, out)
    r = _run(nc, [arrays], core_ids=[0])
    return r.results[0]["out"]
```

```python
import concourse.bass as bass
from concourse import mybir
from contextlib import ExitStack

F32 = mybir.dt.float32
I32 = mybir.dt.int32
U32 = mybir.dt.uint32
ALU = mybir.AluOpType
ACT = mybir.ActivationFunctionType
AX = mybir.AxisListType

P = 128
N, E, D, REL = 6250, 206250, 128, 8
TILES = -(-N // P)
NPAD = TILES * P
LAST = N - (TILES - 1) * P
UNROLL = 16
HALF = UNROLL // 2
QUARTER = UNROLL // 4
COLS = -(-E // (P * UNROLL)) * UNROLL
LASTCOLS = E - (P - 1) * COLS
CHUNKS = -(-(E // P + TILES) // UNROLL) * UNROLL
TURNS = CHUNKS // UNROLL
WIDE = CHUNKS * 4
ACCW = NPAD + P
PER = CHUNKS // P
ROW = D + 2
LN_EPS = 1e-5
LEAK = 0.2
LOW = -2.0 ** 112
FLOOR = -1.0e30
BLK = 448
BLKS = NPAD // BLK
assert BLKS * BLK == NPAD and BLKS % 2 == 0


class Stage(ExitStack):

    number = 0

    def __init__(self, nc):
        super().__init__()
        self.nc, self.own = nc, []
        Stage.number += 1

    def sem(self, name):
        self.own.append(self.nc.alloc_semaphore(f"{name}_{Stage.number}"))
        return self.own[-1]

    def sems(self, *names):
        return [self.sem(name) for name in names]

    def __exit__(self, *failure):
        super().__exit__(*failure)
        if self.own:
            self.nc.clear_and_free_semaphores(self.own)
            self.nc.all_engine_barrier()


class Memory:

    def __init__(self, nc, cs):
        def sb(name, shape, dt=F32):
            return cs.enter_context(nc.sbuf_tensor(name, shape, dt))

        self.big = [sb(f"big{i}", [P, WIDE]) for i in range(5)]
        self.edge_src = sb("edge_src", [P, CHUNKS + HALF], I32)
        self.edge_dst = sb("edge_dst", [P, CHUNKS])
        self.edge_type = sb("edge_type", [P, CHUNKS])
        self.edge_w = sb("edge_w", [P, CHUNKS])
        self.tile_of = sb("tile_of", [1, CHUNKS], I32)
        self.iota = sb("iota", [P, P])
        self.part = sb("part", [P, 1])
        self.ident = sb("ident", [P, P])
        self.before = sb("before", [P, P])
        self.ones = sb("ones", [P, P])
        self.target_score = sb("target_score", [P, TILES + 1])[:, :]
        self.mean = sb("mean", [P, P])
        self.small = sb("small", [P, 512])
        self.one_eps = self.small[:, 510:511]
        self.eps = self.small[:, 511:512]
        self.rows = sb("rows", [P, UNROLL, ROW])
        self.hot = sb("hot", [P, UNROLL, P])
        self.idx = sb("idx", [P, UNROLL], I32)
        self.recs = sb("recs", [P, UNROLL, 4])
        self.psum = [cs.enter_context(nc.psum_tensor(f"ps{i}", [P, 512], F32)) for i in range(8)]
        self.gathered = [cs.enter_context(nc.semaphore(f"gathered{u}")) for u in range(UNROLL)]
        self.gathered_to = 0
        self.written = [cs.enter_context(nc.semaphore(f"written{h}")) for h in range(2)]
        self.records = nc.dram_tensor("records", [CHUNKS * P + COLS, 4], F32, kind="Internal").ap()
        self.unsorted = sb("unsorted", [1, 1], I32)
        self.col_map = nc.dram_tensor("col_map", [CHUNKS], I32, kind="Internal").ap()
        self.tile_row = nc.dram_tensor("tile_row", [CHUNKS], F32, kind="Internal").ap()
        self.map = nc.dram_tensor("map", [CHUNKS], I32, kind="Internal").ap()
        self.edge_row = sb("edge_row", [P, CHUNKS + HALF], I32)
        self.col_of = self.edge_row[0:1, 0:CHUNKS]
        self.edge_norm = self.edge_w
        self.turned = sb("turned", [P, 2, P])
        self.kind = sb("kind", [P, 4, REL])
        self.count = sb("count", [P, (TILES + 1) * REL])
        self.dinv = sb("dinv", [P, TILES + 1])
        self.weights = sb("weights", [P, REL * D])
        self.par = sb("par", [P, 24])
        self.bnc = sb("bnc", [P, 25 * 6 + 8])
        self.att_table = nc.dram_tensor("att_table", [NPAD, ROW], F32, kind="Internal").ap()
        self.table = nc.dram_tensor("table", [REL * NPAD, D], F32, kind="Internal").ap()


def make_constants(nc, m):
    with Stage(nc) as cs:
        made = cs.sem("made")
        block = cs.enter_context(nc.Block())

        @block.gpsimd
        def _(pool):
            pool.iota(m.iota[:, :], [[1, P]], base=0, channel_multiplier=0, allow_small_or_imprecise_dtypes=True)
            pool.iota(m.part[:, :], [[0, 1]], base=0, channel_multiplier=1, allow_small_or_imprecise_dtypes=True)
            pool.memset(m.eps, LN_EPS)
            pool.memset(m.mean[:, :], 1.0 / D)
            pool.memset(m.ones[:, :], 1.0).then_inc(made, 1)
            pool.wait_ge(made, 1)
            pool.affine_select(out=m.ident[:, :], in_=m.ones[:, :], compare_op=ALU.is_equal, fill=0.0,
                               base=0, pattern=[[-1, P]], channel_multiplier=1)
            pool.affine_select(out=m.before[:, :], in_=m.ones[:, :], compare_op=ALU.is_gt, fill=0.0,
                               base=0, pattern=[[1, P]], channel_multiplier=-1)


def load_edges(nc, m, src, dst, etype, weight):
    raw = [m.big[0][:, k * COLS:(k + 1) * COLS] for k in range(4)]
    src_i, dst_i, type_i = (r.bitcast(I32) for r in raw[:3])
    rec = m.big[1][:, 0:4 * COLS].rearrange("p (c f) -> p c f", f=4)
    bin_f = m.big[2][:, 0:COLS]
    bin_i = m.big[3][:, 0:COLS].bitcast(I32)
    place_i = m.big[3][:, COLS:2 * COLS].bitcast(I32)
    with Stage(nc) as cs:
        blank, loaded, split, built, stored = cs.sems("blank", "loaded", "split", "built", "stored")
        block = cs.enter_context(nc.Block())

        @block.sync
        def _(sp):
            sp.wait_ge(blank, 4)
            for t, f in ((dst_i, dst), (src_i, src), (type_i, etype), (raw[3], weight)):
                for a, b in ((0, 112), (112, P - 1)):
                    sp.dma_start(t[a:b, :], f[a * COLS:b * COLS].rearrange("(p c) -> p c", c=COLS)).then_inc(loaded, 16)
                sp.dma_start(t[P - 1:P, 0:LASTCOLS],
                             f[(P - 1) * COLS:E].rearrange("(p c) -> p c", p=1)).then_inc(loaded, 16)
            sp.wait_ge(built, 2)
            sp.dma_start(m.records[0:CHUNKS * P, :].rearrange("(p c) f -> p (c f)", p=P), m.big[4][:, :]).then_inc(stored, 16)
            sp.wait_ge(stored, 16)

        @block.gpsimd
        def _(pool):
            empty = m.big[4][:, :].rearrange("p (c f) -> p c f", f=4)
            pool.memset(empty[:, :, :], 0.0).then_inc(built, 1)
            pool.wait_ge(built, 1)
            pool.memset(empty[:, :, 1], -1.0).then_inc(built, 1)

        @block.vector
        def _(dve):
            dve.memset(dst_i[:, LASTCOLS:COLS], TILES * P).then_inc(blank, 1)
            dve.memset(src_i[:, LASTCOLS:COLS], 0).then_inc(blank, 1)
            dve.memset(type_i[:, LASTCOLS:COLS], 0).then_inc(blank, 1)
            dve.memset(raw[3][:, LASTCOLS:COLS], 0.0).then_inc(blank, 1)
            dve.wait_ge(loaded, 16 * 12)
            dve.tensor_scalar(bin_i, dst_i, 7, None, ALU.arith_shift_right).then_inc(split, 1)
            dve.tensor_scalar(place_i, dst_i, P - 1, None, ALU.bitwise_and).then_inc(split, 1)
            dve.tensor_copy(rec[:, :, 0].bitcast(I32), src_i)
            dve.tensor_copy(rec[:, :, 2], type_i)
            dve.tensor_copy(rec[:, :, 3], raw[3])
            dve.wait_ge(split, 2)
            dve.tensor_copy(bin_f, bin_i)
            dve.tensor_copy(rec[:, :, 1], place_i)


def sort_edges(nc, m):
    bin_f = m.big[2][:, 0:COLS]
    same = m.big[2][:, COLS:2 * COLS]
    running = m.big[2][:, 2 * COLS:3 * COLS]
    one = m.big[2][:, 3 * COLS:4 * COLS]
    slot = m.big[3][:, 0:COLS]
    slot_i = m.big[3][:, COLS:2 * COLS].bitcast(I32)
    part_i = m.big[3][:, 2 * COLS:3 * COLS].bitcast(I32)
    row_i = m.big[3][:, 3 * COLS:4 * COLS].bitcast(I32)
    picked = m.big[0][:, 0:COLS]
    behind = m.big[0][:, COLS:2 * COLS]
    rec = m.big[1][:, 0:4 * COLS].rearrange("p (c f) -> p c f", f=4)
    total = m.small[:, 0:TILES]
    first = m.small[:, 64:64 + TILES]
    need_i = m.small[:, 128:128 + TILES].bitcast(I32)
    need = m.small[:, 192:192 + TILES]
    end = m.small[:, 256:256 + TILES]
    bin_no = m.small[:, 320:320 + TILES]
    chunk_no = m.small[:, 384:384 + PER]
    map_f = m.small[:, 400:400 + PER]
    map_i = m.small[:, 416:416 + PER].bitcast(I32)
    past = m.big[0][:, 0:PER * TILES].rearrange("p (c b) -> p c b", b=TILES)
    before_ps, total_ps = m.psum[0][:, 0:TILES], m.psum[1][:, 0:TILES]

    with Stage(nc) as cs:
        made, counted, summed, step, mapped, map_out, map_in = cs.sems("made", "counted", "summed", "step", "mapped", "map_out", "map_in")
        block = cs.enter_context(nc.Block())

        @block.gpsimd
        def _(pool):
            pool.iota(bin_no, [[1, TILES]], base=0, channel_multiplier=0, allow_small_or_imprecise_dtypes=True).then_inc(made, 1)
            pool.iota(chunk_no, [[1, PER]], base=0, channel_multiplier=PER, allow_small_or_imprecise_dtypes=True).then_inc(made, 1)
            pool.iota(behind, [[1, COLS]], base=CHUNKS * P, channel_multiplier=0, allow_small_or_imprecise_dtypes=True).then_inc(made, 1)
            pool.memset(one, 1.0).then_inc(made, 1)

        @block.tensor
        def _(pe):
            pe.wait_ge(counted, TILES)
            pe.matmul(before_ps, m.before[:, :], total, start=True, stop=True).then_inc(summed, 1)
            pe.matmul(total_ps, m.ones[:, :], total, start=True, stop=True).then_inc(summed, 1)

        @block.vector
        def _(dve):
            steps = [0]

            def then(ins):
                steps[0] += 1
                ins.then_inc(step, 1)
                dve.wait_ge(step, steps[0])

            dve.wait_ge(made, 4)
            dve.memset(slot, 0.0)
            with dve.Fori(0, TILES) as b:
                dve.tensor_scalar(same, bin_f, bin_no[:, bass.ds(b, 1)], 0.0, ALU.is_equal, ALU.add,
                                  accum_out=total[:, bass.ds(b, 1)]).then_inc(counted, 1)
                dve.wait_ge(counted, b + 1)
            dve.wait_ge(summed, 2)
            then(dve.tensor_scalar(need, total_ps, float(P - 1), None, ALU.add))
            then(dve.tensor_copy(need_i, need))
            then(dve.tensor_scalar(need_i, need_i, 7, None, ALU.arith_shift_right))
            then(dve.tensor_copy(need, need_i))
            then(dve.tensor_tensor_scan(end, m.ones[:, 0:TILES], need, 0.0, ALU.mult, ALU.add))
            then(dve.tensor_tensor(first, end, need, ALU.subtract))
            then(dve.scalar_tensor_tensor(first, first, float(P), before_ps, ALU.mult, ALU.add))
            then(dve.tensor_scalar(first, first, -1.0, None, ALU.add))
            then(dve.tensor_tensor(past, chunk_no.unsqueeze(2).to_broadcast([P, PER, TILES]),
                                   end.unsqueeze(1).to_broadcast([P, PER, TILES]), ALU.is_ge))
            then(dve.tensor_reduce(map_f, past, AX.X, ALU.add))
            dve.tensor_copy(map_i, map_f).then_inc(mapped, 1)
            dve.wait_ge(mapped, 1)
            base = steps[0]
            with dve.Fori(0, TILES) as b:
                dve.tensor_scalar(same, bin_f, bin_no[:, bass.ds(b, 1)], None, ALU.is_equal).then_inc(step, 1)
                dve.wait_ge(step, 4 * b + base + 1)
                dve.tensor_tensor_scan(running, one, same, first[:, bass.ds(b, 1)], ALU.mult, ALU.add).then_inc(step, 1)
                dve.wait_ge(step, 4 * b + base + 2)
                dve.tensor_tensor(picked, same, running, ALU.mult).then_inc(step, 1)
                dve.wait_ge(step, 4 * b + base + 3)
                dve.tensor_tensor(slot, slot, picked, ALU.add).then_inc(step, 1)
                dve.wait_ge(step, 4 * b + base + 4)
            steps[0] += 4 * TILES
            then(dve.tensor_copy(slot_i, slot))
            then(dve.tensor_scalar(part_i, slot_i, P - 1, None, ALU.bitwise_and))
            then(dve.tensor_scalar(slot_i, slot_i, 7, None, ALU.arith_shift_right))
            then(dve.tensor_copy(slot, slot_i))
            then(dve.tensor_copy(picked, part_i))
            then(dve.scalar_tensor_tensor(slot, picked, float(CHUNKS), slot, ALU.mult, ALU.add))
            then(dve.scalar_tensor_tensor(same, bin_f, float(TILES), behind, ALU.is_ge, ALU.mult))
            then(dve.tensor_tensor(slot, slot, same, ALU.add))
            then(dve.tensor_copy(row_i, slot))

        @block.sync
        def _(sp):
            sp.wait_ge(mapped, 1)
            sp.dma_start(m.map.rearrange("(p c) -> p c", p=P), map_i).then_inc(map_out, 16)
            sp.wait_ge(map_out, 16)
            sp.dma_start(m.tile_of[0:1, :], m.map.rearrange("(p c) -> p c", p=1)).then_inc(map_in, 16)
            sp.wait_ge(map_in, 16)

    with Stage(nc) as cs:
        staged, begun = cs.sems("staged", "begun")
        written = m.written
        block = cs.enter_context(nc.Block())

        @block.scalar
        def _(act):
            def stage(i, h):
                act.copy(m.idx[:, h * HALF:(h + 1) * HALF], row_i[:, bass.ds(i * UNROLL + h * HALF, HALF)]).then_inc(staged, 1)
                act.copy(m.recs[:, h * HALF:(h + 1) * HALF, :], rec[:, bass.ds(i * UNROLL + h * HALF, HALF), :]).then_inc(staged, 1)

            stage(0, 0)
            stage(0, 1)
            with act.Fori(1, COLS // UNROLL) as i:
                for h in range(2):
                    act.wait_ge(written[h], 16 * HALF * i)
                    stage(i, h)
            for h in range(2):
                act.wait_ge(written[h], 16 * HALF * (COLS // UNROLL))

        @block.gpsimd
        def _(pool):
            with pool.Fori(0, COLS // UNROLL) as i:
                for h in range(2):
                    pool.wait_ge(staged, 4 * i + 2 * h + 2)
                    pool.sem_inc(begun, 1)
                    for u in range(h * HALF, (h + 1) * HALF):
                        pool.indirect_dma_start(m.records, bass.IndirectOffsetOnAxis(ap=m.idx[:, u:u + 1].bitcast(U32), axis=0),
                                                m.recs[:, u, :], None).then_inc(written[h], 16)

    with Stage(nc) as cs:
        back = cs.sem("back")
        block = cs.enter_context(nc.Block())
        rec = m.big[0][:, :].rearrange("p (c f) -> p c f", f=4)

        @block.sync
        def _(sp):
            sp.dma_start(m.big[0][:, :], m.records[0:CHUNKS * P, :].rearrange("(p c) f -> p (c f)", p=P)).then_inc(back, 16)

        @block.vector
        def _(dve):
            dve.wait_ge(back, 16)
            dve.memset(m.edge_src[:, CHUNKS:], 0)
            dve.tensor_copy(m.edge_src[:, 0:CHUNKS], rec[:, :, 0].bitcast(I32))
            dve.tensor_copy(m.edge_dst[:, :], rec[:, :, 1])

        @block.scalar
        def _(act):
            act.wait_ge(back, 16)
            act.copy(m.edge_type[:, :], rec[:, :, 2])
            act.copy(m.edge_w[:, :], rec[:, :, 3])


def edge_rows(nc, m):
    with Stage(nc) as cs:
        done = cs.sem("done")
        block = cs.enter_context(nc.Block())
        src_f, row_f = m.big[1][:, 0:CHUNKS], m.big[1][:, CHUNKS:2 * CHUNKS]

        @block.vector
        def _(dve):
            dve.tensor_copy(src_f, m.edge_src[:, 0:CHUNKS]).then_inc(done, 1)
            dve.wait_ge(done, 1)
            dve.scalar_tensor_tensor(row_f, m.edge_type[:, :], float(NPAD), src_f, ALU.mult, ALU.add).then_inc(done, 1)
            dve.wait_ge(done, 2)
            dve.memset(m.edge_row[:, CHUNKS:], 0)
            dve.tensor_copy(m.edge_row[:, 0:CHUNKS], row_f)


def load_columns(nc, m, src, dst, etype, weight):
    raw = [m.big[0][:, k * CHUNKS:(k + 1) * CHUNKS] for k in range(4)]
    rec = m.big[1][:, :].rearrange("p (c f) -> p c f", f=4)
    full = E // (P * P) * P
    rest = E // P - full
    over = E % P
    last = (PER - 1) * P
    assert full == last
    with Stage(nc) as cs:
        blank, held, turned, taken = cs.sems("blank", "held", "turned", "taken")
        loaded = cs.sem("loaded")
        block = cs.enter_context(nc.Block())

        @block.gpsimd
        def _(pool):
            pool.memset(raw[0][:, last:].bitcast(I32), 0).then_inc(blank, 1)
            pool.memset(raw[1][:, last:].bitcast(I32), TILES * P).then_inc(blank, 1)
            pool.memset(raw[2][:, last:].bitcast(I32), 0).then_inc(blank, 1)
            pool.memset(raw[3][:, last:], 0.0).then_inc(blank, 1)

        @block.sync
        def _(sp):
            fields = [(r.bitcast(f.dtype), f) for r, f in zip(raw, (src, dst, etype, weight))]
            for t, f in fields:
                sp.dma_start(t[:, 0:last].rearrange("p (g j) -> p g j", j=P),
                             f[0:full * P].rearrange("(g p j) -> p g j", p=P, j=P)).then_inc(loaded, 16)
            sp.wait_ge(blank, 4)
            for t, f in fields:
                sp.dma_start(t[0:rest, last:], f[full * P:(full + rest) * P].rearrange("(p j) -> p j", j=P)).then_inc(loaded, 16)
                sp.dma_start(t[rest:rest + 1, last:last + over],
                             f[(full + rest) * P:E].rearrange("(p j) -> p j", p=1)).then_inc(loaded, 16)

        @block.vector
        def _(dve):
            dve.wait_ge(loaded, 16 * 12)
            dve.sem_inc(turned, 4)
            with dve.Fori(0, PER) as g:
                for k in range(4):
                    dve.wait_ge(turned, 4 * g + k + 1)
                    at = raw[k][:, bass.ds(g * P, P)]
                    dve.tensor_copy(m.hot[:, k, :], at if k == 3 else at.bitcast(I32)).then_inc(held, 1)

        @block.tensor
        def _(pe):
            pe.sem_inc(taken, 4)
            with pe.Fori(0, PER) as g:
                for k in range(4):
                    pe.wait_ge(held, 4 * g + k + 1)
                    pe.wait_ge(taken, 4 * g + k + 1)
                    pe.transpose(m.psum[k][:, 0:P], m.hot[:, k, :], m.ident[:, :]).then_inc(turned, 1)

        @block.scalar
        def _(act):
            with act.Fori(0, PER) as g:
                for k in range(4):
                    act.wait_ge(turned, 4 + 4 * g + k + 1)
                    act.copy(rec[:, bass.ds(g * P, P), k], m.psum[k][:, 0:P]).then_inc(taken, 1)


def pair_columns(nc, m):
    rec = m.big[1][:, :].rearrange("p (c f) -> p c f", f=4)
    part = lambda b, k: m.big[b][:, k * CHUNKS:(k + 1) * CHUNKS]
    bins, first, final, count = (part(2, k) for k in range(4))
    one, end, jump, junk = (part(3, k) for k in range(4))
    start, lead, whole = (part(0, k) for k in range(3))
    other_junk = part(0, 3)
    chunk_no, col, shift, tile = (m.small[:, 16 * k:16 * k + PER] for k in range(4))
    col_i, tile_i = (m.small[:, 64 + 16 * k:64 + 16 * k + PER].bitcast(I32) for k in range(2))
    wrong = m.small[:, 96:100]
    flag = m.small[:, 100:101]
    quarter = CHUNKS // 4
    with Stage(nc) as cs:
        made, ready, product, taken, step, judged, added, mapped, map_out, map_in = cs.sems(
            "made", "ready", "product", "taken", "step", "judged", "added", "mapped", "map_out", "map_in")
        block = cs.enter_context(nc.Block())

        @block.gpsimd
        def _(pool):
            pool.iota(chunk_no, [[1, PER]], base=0, channel_multiplier=PER, allow_small_or_imprecise_dtypes=True).then_inc(made, 1)
            pool.memset(one, 1.0).then_inc(made, 1)

        @block.tensor
        def _(pe):
            pe.wait_ge(ready, 3)
            for k in range(2):
                for q in range(4):
                    pe.matmul(m.psum[4 * k + q][:, 0:quarter], m.hot[:, k, :], bins[:, q * quarter:(q + 1) * quarter],
                              start=True, stop=True).then_inc(product, 1)
            pe.wait_ge(taken, 8)
            pe.wait_ge(judged, 1)
            pe.matmul(m.psum[0][:, 0:1], m.ones[:, :], wrong[:, 3:4], start=True, stop=True).then_inc(added, 1)

        @block.scalar
        def _(act):
            for k, row in enumerate((first, final)):
                for q in range(4):
                    act.wait_ge(product, 4 * k + q + 1)
                    act.copy(row[:, q * quarter:(q + 1) * quarter], m.psum[4 * k + q][:, 0:quarter]).then_inc(taken, 1)

        @block.vector
        def _(dve):
            steps = [0]

            def then(ins):
                steps[0] += 1
                ins.then_inc(step, 1)
                dve.wait_ge(step, steps[0])

            dve.tensor_scalar(m.hot[:, 0, :], m.ones[:, :], m.ident[:, 0:1], None, ALU.mult).then_inc(ready, 1)
            dve.tensor_scalar(m.hot[:, 1, :], m.ones[:, :], m.ident[:, P - 1:P], None, ALU.mult).then_inc(ready, 1)
            then(dve.tensor_copy(whole.bitcast(I32), rec[:, :, 1]))
            then(dve.tensor_scalar(whole.bitcast(I32), whole.bitcast(I32), 7, None, ALU.arith_shift_right))
            dve.tensor_copy(bins, whole.bitcast(I32)).then_inc(ready, 1)
            dve.wait_ge(ready, 3)
            dve.wait_ge(taken, 8)
            dve.wait_ge(made, 2)
            then(dve.scalar_tensor_tensor(junk, bins, 0.0, first, ALU.add, ALU.is_lt, accum_out=wrong[:, 0:1]))
            then(dve.scalar_tensor_tensor(junk, bins, 0.0, final, ALU.add, ALU.is_gt, accum_out=wrong[:, 1:2]))
            then(dve.scalar_tensor_tensor(junk[:, 1:], final[:, 0:CHUNKS - 1], 0.0, first[:, 1:], ALU.add, ALU.is_gt,
                                          accum_out=wrong[:, 2:3]))
            dve.tensor_reduce(wrong[:, 3:4], wrong[:, 0:3], AX.X, ALU.add).then_inc(judged, 1)
            then(dve.scalar_tensor_tensor(count, final, 1.0, first, ALU.add, ALU.subtract))
            then(dve.tensor_tensor_scan(end, one, count, 0.0, ALU.mult, ALU.add))
            then(dve.tensor_tensor(start, end, count, ALU.subtract))
            then(dve.tensor_tensor(lead, first, start, ALU.subtract))
            then(dve.tensor_tensor(jump[:, 1:], lead[:, 1:], lead[:, 0:CHUNKS - 1], ALU.subtract))
            then(dve.tensor_copy(jump[:, 0:1], lead[:, 0:1]))
            base = steps[0]
            with dve.Fori(0, PER) as j:
                dve.tensor_scalar(junk, end, chunk_no[:, bass.ds(j, 1)], 0.0, ALU.is_le, ALU.add,
                                  accum_out=col[:, bass.ds(j, 1)]).then_inc(step, 1)
                dve.scalar_tensor_tensor(other_junk, start, chunk_no[:, bass.ds(j, 1)], jump, ALU.is_le, ALU.mult,
                                         accum_out=shift[:, bass.ds(j, 1)]).then_inc(step, 1)
                dve.wait_ge(step, 2 * j + base + 2)
            steps[0] += 2 * PER
            then(dve.tensor_tensor(tile, shift, chunk_no, ALU.add))
            dve.tensor_copy(col_i, col).then_inc(mapped, 1)
            dve.tensor_copy(tile_i, tile).then_inc(mapped, 1)
            dve.wait_ge(added, 1)
            then(dve.tensor_scalar(flag, m.psum[0][:, 0:1], 1.0, None, ALU.min))
            dve.tensor_copy(m.unsorted[0:1, 0:1], flag[0:1, :])

        @block.sync
        def _(sp):
            sp.wait_ge(mapped, 2)
            sp.dma_start(m.map.rearrange("(p c) -> p c", p=P), tile_i).then_inc(map_out, 16)
            sp.dma_start(m.col_map.rearrange("(p c) -> p c", p=P), col_i).then_inc(map_out, 16)
            sp.dma_start(m.tile_row.rearrange("(p c) -> p c", p=P), tile).then_inc(map_out, 16)
            sp.wait_ge(map_out, 48)
            sp.dma_start(m.tile_of[0:1, :], m.map.rearrange("(p c) -> p c", p=1)).then_inc(map_in, 16)
            sp.dma_start(m.col_of[0:1, :], m.col_map.rearrange("(p c) -> p c", p=1)).then_inc(map_in, 16)
            sp.wait_ge(map_in, 32)


def spread_columns(nc, m):
    rec = m.big[1][:, :].rearrange("p (c f) -> p c f", f=4)
    by_chunk = m.big[4][:, :].rearrange("p (c f) -> p c f", f=4)
    tile = m.big[2][:, 0:CHUNKS]
    with Stage(nc) as cs:
        spread, begun = cs.sems("spread", "begun")
        picked, moved = (dict(zip("apv", cs.sems(*(f"{what}_by_{e}" for e in ("act", "pool", "dve"))))) for what in ("picked", "moved"))
        block = cs.enter_context(nc.Block())

        @block.sync
        def _(sp):
            sp.dma_start(tile, m.tile_row.rearrange("(o c) -> o c", o=1).to_broadcast([P, CHUNKS])).then_inc(spread, 16)

        def columns(engine, copy, first, n, picked, moved):
            held = m.rows[:, first:first + n, 0:4]
            engine.sem_inc(moved, 1)
            with engine.Fori(0, TURNS) as i:
                _, cols = nc.values_load_multi_w_load_instructions(
                    m.col_of[0:1, bass.ds(i * UNROLL + first, n)], engines=[engine.engine], min_val=0, max_val=CHUNKS - 1,
                    skip_runtime_bounds_check_because="pairs of sorted edges, with one for each column behind them, are no fewer than chunks")
                engine.wait_ge(moved, i + 1)
                engine.sem_inc(begun, 1)
                for u in range(n):
                    copy(held[:, u:u + 1, :], rec[:, bass.ds(cols[u], 1), :]).then_inc(picked, 1)
                engine.wait_ge(picked, (i + 1) * n)
                engine.sem_inc(begun, 1)
                copy(by_chunk[:, bass.ds(i * UNROLL + first, n), :], held).then_inc(moved, 1)

        @block.gpsimd
        def _(pool):
            columns(pool, pool.tensor_copy, 11, 5, picked["p"], moved["p"])

        @block.scalar
        def _(act):
            columns(act, act.copy, 0, 5, picked["a"], moved["a"])
            for by in "apv":
                act.wait_ge(moved[by], TURNS + 1)
            act.copy(m.edge_type[:, :], by_chunk[:, :, 2])
            act.copy(m.edge_w[:, :], by_chunk[:, :, 3])

        @block.vector
        def _(dve):
            columns(dve, dve.tensor_copy, 5, 6, picked["v"], moved["v"])
            for by in "apv":
                dve.wait_ge(moved[by], TURNS + 1)
            dve.memset(m.edge_src[:, CHUNKS:], 0)
            dve.tensor_copy(m.edge_src[:, 0:CHUNKS], by_chunk[:, :, 0])
            dve.wait_ge(spread, 16)
            dve.scalar_tensor_tensor(m.edge_dst[:, :], tile, -float(P), by_chunk[:, :, 1], ALU.mult, ALU.add)


def wait(engine, sem, count):
    if not isinstance(count, int) or count > 0:
        engine.wait_ge(sem, count)


def turns(nc, m, engine, stages, steps, tiled=()):
    deepest = max(lag for lag, _ in stages)
    lags = [lag for lag, stage in stages if stage in tiled]

    def tiles_of(first, n):
        if not lags:
            return None
        _, tiles = nc.values_load_multi_w_load_instructions(
            m.tile_of[0:1, bass.ds(first, n)], engines=[engine.engine], min_val=0, max_val=TILES,
            skip_runtime_bounds_check_because="a chunk's tile counts bins, of which there are TILES")
        return tiles

    early, late = (min(lags), max(lags)) if lags else (0, 0)
    tiles = tiles_of(0, UNROLL - early)
    for u in range(UNROLL):
        for lag, stage in stages:
            if u >= lag:
                steps(0, u - lag, stage, tiles[u - lag] if stage in tiled else None)
    with engine.Fori(1, TURNS) as i:
        tiles = tiles_of(i * UNROLL - late, UNROLL + late - early)
        for u in range(UNROLL):
            for lag, stage in stages:
                steps(i, u - lag, stage, tiles[late + u - lag] if stage in tiled else None)
    tiles = tiles_of(TURNS * UNROLL - late, late)
    for u in range(deepest):
        for lag, stage in stages:
            if lag > u:
                steps(TURNS, u - lag, stage, tiles[late + u - lag] if stage in tiled else None)


def stage_indices(act, m, rows_of, staged, turn, q):
    act.copy(m.idx[:, q * QUARTER:(q + 1) * QUARTER],
             rows_of[:, bass.ds(turn * UNROLL + q * QUARTER, QUARTER)]).then_inc(staged, 1)


def stage_ahead(act, m, rows_of, staged, product, turn, u):
    q = (u // QUARTER + 2) % 4
    ahead = turn + 1 if q < 2 else turn
    if not isinstance(ahead, int) or ahead > 0:
        act.wait_ge(product, (ahead - 1) * UNROLL + (q + 1) * QUARTER)
        stage_indices(act, m, rows_of, staged, ahead, q)


def gather(pool, m, table, width, staged, begun, freed=None):
    def turn(i, first):
        for u in range(UNROLL):
            if u % QUARTER == 0:
                pool.wait_ge(staged, 4 * i + u // QUARTER + 1)
                pool.sem_inc(begun, 1)
                if freed is not None and not first:
                    pool.wait_ge(freed, (i - 1) * UNROLL + u + QUARTER)
                    pool.sem_inc(begun, 1)
            pool.indirect_dma_start(m.rows[:, u, 0:width], None, table,
                                    bass.IndirectOffsetOnAxis(ap=m.idx[:, u:u + 1].bitcast(U32), axis=0),
                                    ).then_inc(m.gathered[u], 16)

    if freed is not None:
        turn(0, True)
    with pool.Fori(0 if freed is None else 1, TURNS) as i:
        turn(i, False)


def gather_sum(nc, m, table, rows_of, acc, weight=None, scale_rows=None, count=False, norm=False):
    with Stage(nc) as cs:
        staged, begun, ready, product, added = cs.sems("staged", "begun", "ready", "product", "added")
        scaled, counted, typed, turned, copied, looked, found, mine = cs.sems(
            "scaled", "counted", "typed", "turned", "copied", "looked", "found", "mine")
        gathered, before = m.gathered, m.gathered_to
        m.gathered_to += 16 * TURNS
        block = cs.enter_context(nc.Block())
        sums, side, turn_ps = m.psum[0:2], m.psum[2:4], m.psum[4:6]

        @block.gpsimd
        def _(pool):
            gather(pool, m, table, D, staged, begun)

        @block.scalar
        def _(act):
            def steps(i, u, what, tile):
                c = i * UNROLL + u
                if what == "stage":
                    if u % QUARTER == 0:
                        stage_ahead(act, m, rows_of, staged, product, i, u)
                elif what == "scale":
                    act.wait_ge(gathered[u % UNROLL], before + 16 * (i + 1 if u >= 0 else i))
                    act.activation(m.rows[:, u % UNROLL, 0:D], m.rows[:, u % UNROLL, 0:D], ACT.Copy,
                                   scale=scale_rows[:, bass.ds(c, 1)]).then_inc(scaled, 1)
                else:
                    act.wait_ge(turned, c + 1)
                    wait(act, looked, c - 1)
                    act.copy(m.turned[:, u % 2, :], turn_ps[u % 2][:, 0:P]).then_inc(copied, 1)

            for q in range(4):
                stage_indices(act, m, rows_of, staged, 0, q)
            stages = [(0, "stage")] + [(1, "scale")] * (scale_rows is not None) + [(2, "copy")] * norm
            turns(nc, m, act, stages, steps)

        @block.tensor
        def _(pe):
            def steps(i, u, what, tile):
                c = i * UNROLL + u
                hot = m.hot[:, u % UNROLL, :]
                if what == "turn":
                    pe.wait_ge(ready, c + 1)
                    wait(pe, copied, c - 1)
                    pe.transpose(turn_ps[u % 2][:, 0:P], hot, m.ident[:, :]).then_inc(turned, 1)
                elif what == "count":
                    pe.wait_ge(ready, c + 1)
                    pe.wait_ge(typed, c + 1)
                    wait(pe, counted, c - 1)
                    pe.matmul(side[u % 2][:, 0:REL], hot, m.kind[:, u % 4, :], start=True, stop=True).then_inc(mine, 1)
                elif what == "sum":
                    pe.wait_ge(ready, c + 1)
                    if scale_rows is None:
                        pe.wait_ge(gathered[u % UNROLL], before + 16 * (i + 1 if u >= 0 else i))
                    else:
                        pe.wait_ge(scaled, c + 1)
                    wait(pe, added, c - 1)
                    pe.matmul(sums[u % 2][:, 0:P], m.rows[:, u % UNROLL, 0:D], hot, start=True, stop=True).then_inc(product, 1)
                else:
                    pe.wait_ge(copied, c + 1)
                    wait(pe, found, c - 1)
                    pe.matmul(side[u % 2][:, 0:REL], m.turned[:, u % 2, :], m.count[:, bass.ds(tile * REL, REL)],
                              start=True, stop=True).then_inc(looked, 1)

            stages = [(1, "turn")] * norm + [(2, "count")] * count + [(2, "sum")] + [(3, "look up")] * norm
            turns(nc, m, pe, stages, steps, ("look up",))

        @block.vector
        def _(dve):
            def steps(i, u, what, tile):
                c = i * UNROLL + u
                kind = m.kind[:, u % 4, :]
                if what == "hot":
                    wait(dve, product, c - UNROLL + 1)
                    weights = () if weight is None else (weight[:, bass.ds(c, 1)], ALU.is_equal, ALU.mult)
                    dve.tensor_scalar(m.hot[:, u % UNROLL, :], m.iota[:, :], m.edge_dst[:, bass.ds(c, 1)],
                                      *(weights or (None, ALU.is_equal))).then_inc(ready, 1)
                elif what == "kind":
                    wait(dve, mine, c - 3)
                    dve.tensor_scalar(kind, m.iota[:, 0:REL], m.edge_type[:, bass.ds(c, 1)], None, ALU.is_equal).then_inc(typed, 1)
                elif what == "count":
                    dve.wait_ge(mine, c + 1)
                    wait(dve, counted, c)
                    at = m.count[:, bass.ds(tile * REL, REL)]
                    dve.tensor_tensor(at, at, side[u % 2][:, 0:REL], ALU.add).then_inc(counted, 1)
                elif what == "find":
                    dve.wait_ge(looked, c + 1)
                    wait(dve, found, c - 3)
                    dve.scalar_tensor_tensor(kind, m.iota[:, 0:REL], m.edge_type[:, bass.ds(c, 1)], side[u % 2][:, 0:REL],
                                             ALU.is_equal, ALU.mult, accum_out=m.edge_norm[:, bass.ds(c, 1)]).then_inc(found, 1)
                else:
                    dve.wait_ge(product, c + 1)
                    wait(dve, added, c)
                    at = acc[:, bass.ds(tile * P, P)]
                    dve.tensor_tensor(at, at, sums[u % 2][:, 0:P], ALU.add).then_inc(added, 1)

            stages = [(0, "hot")] + [(0, "kind"), (3, "count")] * count + [(3, "add")] + [(4, "find")] * norm
            turns(nc, m, dve, stages, steps, ("count", "add"))


def linear(nc, m, w, x, out, func=ACT.Identity, bias=0.0, times=None):
    with Stage(nc) as cs:
        product, taken = cs.sems("product", "taken")
        block = cs.enter_context(nc.Block())

        @block.tensor
        def _(pe):
            pe.sem_inc(taken, 2)
            with pe.Fori(0, BLKS // 2) as j:
                for k in range(2):
                    pe.wait_ge(taken, 2 * j + k + 1)
                    pe.matmul(m.psum[k][:, 0:BLK], w, x[:, bass.ds((2 * j + k) * BLK, BLK)],
                              start=True, stop=True).then_inc(product, 1)

        @block.scalar
        def _(act):
            with act.Fori(0, BLKS // 2) as j:
                for k in range(2):
                    act.wait_ge(product, 2 * j + k + 1)
                    act.activation(out[:, bass.ds((2 * j + k) * BLK, BLK)], m.psum[k][:, 0:BLK], func,
                                   bias=bias).then_inc(taken, 1)

        if times is not None:
            @block.vector
            def _(dve):
                with dve.Fori(0, BLKS // 2) as j:
                    for k in range(2):
                        dve.wait_ge(taken, 2 * j + k + 3)
                        at = out[:, bass.ds((2 * j + k) * BLK, BLK)]
                        dve.tensor_tensor(at, at, times[:, bass.ds((2 * j + k) * BLK, BLK)], ALU.mult)



SETS = 4


def write_table(nc, m, x, width, stage, store, scale=None):
    step = min(width, 512)
    banks = width // step
    with Stage(nc) as cs:
        held, product, taken = cs.sems("held", "product", "taken")
        stored = [cs.sem(f"stored{k}") for k in range(SETS)]
        block = cs.enter_context(nc.Block())
        turns = TILES // SETS
        assert turns * SETS + 1 == TILES

        @block.vector
        def _(dve):
            def tile(j, k):
                dve.wait_ge(product, (j * SETS + k + 1) * banks)
                dve.tensor_copy(m.hot[:, k, :], x[:, bass.ds((j * SETS + k) * P, P)]).then_inc(held, 1)

            dve.sem_inc(product, SETS * banks)
            with dve.Fori(0, turns) as j:
                for k in range(SETS):
                    tile(j, k)
            tile(turns, 0)

        @block.tensor
        def _(pe):
            def tile(j, k):
                pe.wait_ge(held, j * SETS + k + 1)
                for h in range(banks):
                    pe.wait_ge(taken, (j * SETS + k) * banks + h + 1)
                    pe.matmul(m.psum[k * banks + h][:, 0:step], m.hot[:, k, :],
                              m.weights[:, h * step:(h + 1) * step], start=True, stop=True).then_inc(product, 1)

            pe.sem_inc(taken, SETS * banks)
            with pe.Fori(0, turns) as j:
                for k in range(SETS):
                    tile(j, k)
            tile(turns, 0)

        @block.scalar
        def _(act):
            def tile(j, k):
                for h in range(banks):
                    act.wait_ge(product, (SETS + j * SETS + k) * banks + h + 1)
                    act.activation(stage(k)[:, h * step:(h + 1) * step], m.psum[k * banks + h][:, 0:step], ACT.Copy,
                                   scale=1.0 if scale is None else scale[:, bass.ds(j * SETS + k, 1)]).then_inc(taken, 1)

            for k in range(SETS):
                tile(0, k)
            with act.Fori(1, turns) as j:
                for k in range(SETS):
                    act.wait_ge(stored[k], 16 * j)
                    tile(j, k)
            act.wait_ge(stored[0], 16 * turns)
            tile(turns, 0)

        @block.sync
        def _(sp):
            def tile(j, k):
                sp.wait_ge(taken, (SETS + j * SETS + k + 1) * banks)
                sp.dma_start(store(j * SETS + k), stage(k)).then_inc(stored[k], 16)

            with sp.Fori(0, turns) as j:
                for k in range(SETS):
                    tile(j, k)
            tile(turns, 0)
            sp.wait_ge(stored[0], 16 * (turns + 1))
            for k in range(1, SETS):
                sp.wait_ge(stored[k], 16 * turns)


def batch_norm(nc, m, x, out, gamma, beta, func=ACT.Identity):
    cut = 250
    parts = N // cut
    assert parts * cut == N
    stats = m.bnc[:, 0:6 * parts]
    mv, std, rstd, scale, shift = (m.bnc[:, 6 * parts + o:6 * parts + o + n] for o, n in ((0, 2), (2, 1), (3, 1), (4, 1), (5, 1)))
    with Stage(nc) as cs:
        step, rooted, ready = cs.sems("step", "rooted", "ready")
        block = cs.enter_context(nc.Block())

        @block.vector
        def _(dve):
            with dve.Fori(0, parts) as j:
                dve.bn_stats(stats[:, bass.ds(j * 6, 6)], x[:, bass.ds(j * cut, cut)]).then_inc(step, 1)
            dve.wait_ge(step, parts)
            dve.bn_aggr(mv, stats).then_inc(step, 1)
            dve.wait_ge(rooted, 1)
            dve.reciprocal(rstd, std).then_inc(step, 1)
            dve.wait_ge(step, parts + 2)
            dve.tensor_tensor(scale, gamma, rstd, ALU.mult).then_inc(step, 1)
            dve.wait_ge(step, parts + 3)
            dve.tensor_tensor(shift, scale, mv[:, 0:1], ALU.mult).then_inc(step, 1)
            dve.wait_ge(step, parts + 4)
            dve.tensor_tensor(shift, beta, shift, ALU.subtract).then_inc(ready, 1)

        @block.scalar
        def _(act):
            act.wait_ge(step, parts + 1)
            act.activation(std, mv[:, 1:2], ACT.Sqrt, bias=m.eps).then_inc(rooted, 1)
            act.wait_ge(ready, 1)
            act.activation(out[:, 0:NPAD], x[:, 0:NPAD], func, bias=shift, scale=scale)


def combine(nc, m, parts):
    with Stage(nc) as cs:
        step = cs.sem("step")
        block = cs.enter_context(nc.Block())

        @block.vector
        def _(dve):
            for n, (out, in0, scalar, in1, op0, op1) in enumerate(parts):
                if n:
                    dve.wait_ge(step, n)
                dve.scalar_tensor_tensor(out, in0, scalar, in1, op0, op1).then_inc(step, 1)


def layer_norm(nc, m, x, out, tmp):
    with Stage(nc) as cs:
        mean, centred, squared, var, rooted, inverse, done = cs.sems("mean", "centred", "squared", "var", "rooted", "inverse", "done")
        block = cs.enter_context(nc.Block())
        sq = [tmp[:, k * BLK:(k + 1) * BLK] for k in range(2)]
        std = [tmp[:, (2 + k) * BLK:(3 + k) * BLK] for k in range(2)]
        at = lambda a, j, k: a[:, bass.ds((2 * j + k) * BLK, BLK)]

        @block.tensor
        def _(pe):
            pe.sem_inc(centred, 2)
            pe.sem_inc(rooted, 2)
            with pe.Fori(0, BLKS // 2) as j:
                for k in range(2):
                    pe.wait_ge(centred, 2 * j + k + 1)
                    pe.matmul(m.psum[k][:, 0:BLK], m.mean[:, :], at(x, j, k), start=True, stop=True).then_inc(mean, 1)
                for k in range(2):
                    pe.wait_ge(squared, 2 * j + k + 1)
                    pe.wait_ge(rooted, 2 * j + k + 1)
                    pe.matmul(m.psum[2 + k][:, 0:BLK], m.mean[:, :], sq[k], start=True, stop=True).then_inc(var, 1)

        @block.vector
        def _(dve):
            with dve.Fori(0, BLKS // 2) as j:
                for k in range(2):
                    dve.wait_ge(mean, 2 * j + k + 1)
                    dve.tensor_tensor(at(x, j, k), at(x, j, k), m.psum[k][:, 0:BLK], ALU.subtract).then_inc(centred, 1)
                for k in range(2):
                    dve.wait_ge(rooted, 2 * j + k + 3)
                    dve.reciprocal(std[k], std[k]).then_inc(inverse, 1)
                    dve.wait_ge(inverse, 2 * j + k + 1)
                    dve.tensor_tensor(at(out, j, k), at(x, j, k), std[k], ALU.mult).then_inc(done, 1)

        @block.scalar
        def _(act):
            act.sem_inc(done, 2)
            with act.Fori(0, BLKS // 2) as j:
                for k in range(2):
                    act.wait_ge(centred, 2 * j + k + 3)
                    act.wait_ge(rooted, 2 * j + k + 1)
                    act.activation(sq[k], at(x, j, k), ACT.Square).then_inc(squared, 1)
                for k in range(2):
                    act.wait_ge(var, 2 * j + k + 1)
                    act.wait_ge(done, 2 * j + k + 1)
                    act.activation(std[k], m.psum[2 + k][:, 0:BLK], ACT.Sqrt, bias=m.eps).then_inc(rooted, 1)


def turn_tiles(nc, m, source, target):
    with Stage(nc) as cs:
        held, turned, taken = cs.sems("held", "turned", "taken")
        block = cs.enter_context(nc.Block())
        group = 7
        assert group * group == TILES

        @block.vector
        def _(dve):
            dve.sem_inc(turned, group)
            with dve.Fori(0, group) as j:
                for k in range(group):
                    dve.wait_ge(turned, j * group + k + 1)
                    dve.tensor_copy(m.hot[:, k, :], source[:, bass.ds((j * group + k) * P, P)]).then_inc(held, 1)

        @block.tensor
        def _(pe):
            pe.sem_inc(taken, group)
            with pe.Fori(0, group) as j:
                for k in range(group):
                    pe.wait_ge(held, j * group + k + 1)
                    pe.wait_ge(taken, j * group + k + 1)
                    pe.transpose(m.psum[k][:, 0:P], m.hot[:, k, :], m.ident[:, :]).then_inc(turned, 1)

        @block.scalar
        def _(act):
            with act.Fori(0, group) as j:
                for k in range(group):
                    act.wait_ge(turned, group + j * group + k + 1)
                    act.copy(target[:, bass.ds((j * group + k) * P, P)], m.psum[k][:, 0:P]).then_inc(taken, 1)


def load_vectors(nc, m, a):
    with Stage(nc) as cs:
        clear, loaded, done = cs.sems("clear", "loaded", "done")
        block = cs.enter_context(nc.Block())
        full = TILES - 1
        x_rows = m.big[4][:, 0:NPAD].rearrange("p (t d) -> p t d", d=D)
        w_nodes = m.big[3]

        @block.vector
        def _(dve):
            dve.memset(x_rows[:, full, :], 0.0).then_inc(clear, 1)
            dve.wait_ge(loaded, 16 * (len(VECTORS) + 1))
            dve.tensor_scalar(m.one_eps, m.one_eps, 1.0, None, ALU.add)

        @block.sync
        def _(sp):
            with nc.allow_non_contiguous_dma("a word to a partition"):
                for n, name in enumerate(VECTORS):
                    sp.dma_start(m.par[:, n:n + 1], a[name].rearrange("(p o) -> p o", o=1)).then_inc(loaded, 16)
                sp.dma_start(m.one_eps, a["L0_gnn_eps"].rearrange("(p o) -> p o", o=1).to_broadcast([P, 1])).then_inc(loaded, 16)
            sp.dma_start(x_rows[:, 0:full, :], a["x"][0:full * P, :].rearrange("(t p) d -> p t d", p=P)).then_inc(done, 16)
            sp.wait_ge(clear, 1)
            sp.dma_start(x_rows[0:LAST, full, :], a["x"][full * P:N, :]).then_inc(done, 16)
            sp.wait_ge(done, 32)


def load(nc, m, pairs, zero=()):
    with Stage(nc) as cs:
        loaded = cs.sem("loaded")
        block = cs.enter_context(nc.Block())

        @block.sync
        def _(sp):
            for out, in_ in pairs:
                sp.dma_start(out, in_).then_inc(loaded, 16)
            if pairs:
                sp.wait_ge(loaded, 16 * len(pairs))

        if zero:
            @block.vector
            def _(dve):
                for z in zero:
                    dve.memset(z, 0.0)


def degrees(nc, m, wide):
    with Stage(nc) as cs:
        step, rooted, spread, product, taken = cs.sems("step", "rooted", "spread", "product", "taken")
        block = cs.enter_context(nc.Block())
        group = 7
        assert group * group == TILES

        @block.vector
        def _(dve):
            dve.tensor_reduce(m.dinv[:, :], m.count[:, :].rearrange("p (t r) -> p t r", r=REL), AX.X, ALU.add).then_inc(step, 1)
            dve.wait_ge(step, 1)
            dve.tensor_scalar(m.count[:, :], m.count[:, :], 1.0, None, ALU.max).then_inc(step, 1)
            dve.wait_ge(step, 2)
            dve.reciprocal(m.count[:, :], m.count[:, :])
            dve.wait_ge(rooted, 1)
            dve.reciprocal(m.dinv[:, :], m.dinv[:, :]).then_inc(step, 1)
            dve.wait_ge(step, 3)
            dve.sem_inc(product, group)
            with dve.Fori(0, group) as j:
                for k in range(group):
                    dve.wait_ge(product, j * group + k + 1)
                    dve.tensor_scalar(m.hot[:, k, :], m.ident[:, :], m.dinv[:, bass.ds(j * group + k, 1)], None,
                                      ALU.mult).then_inc(spread, 1)

        @block.scalar
        def _(act):
            act.wait_ge(step, 1)
            act.activation(m.dinv[:, :], m.dinv[:, :], ACT.Sqrt, bias=1.0).then_inc(rooted, 1)
            with act.Fori(0, group) as j:
                for k in range(group):
                    act.wait_ge(product, group + j * group + k + 1)
                    act.copy(wide[:, bass.ds((j * group + k) * P, P)], m.psum[k][:, 0:P]).then_inc(taken, 1)

        @block.tensor
        def _(pe):
            pe.sem_inc(taken, group)
            with pe.Fori(0, group) as j:
                for k in range(group):
                    pe.wait_ge(spread, j * group + k + 1)
                    pe.wait_ge(taken, j * group + k + 1)
                    pe.matmul(m.psum[k][:, 0:P], m.ones[:, :], m.hot[:, k, :], start=True, stop=True).then_inc(product, 1)



def attention_table(nc, m, x, stage, target_score):
    turns = TILES // SETS
    a_source, a_target = m.weights[:, 2 * D:3 * D], m.weights[:, 3 * D:4 * D]
    with Stage(nc) as cs:
        held, product, taken, scored = cs.sems("held", "product", "taken", "scored")
        stored = [cs.sem(f"stored{k}") for k in range(SETS)]
        block = cs.enter_context(nc.Block())

        @block.vector
        def _(dve):
            def hold(j, k):
                dve.wait_ge(product, j * SETS + k + 1)
                dve.tensor_copy(m.hot[:, k, :], x[:, bass.ds((j * SETS + k) * P, P)]).then_inc(held, 1)

            def score(j, k):
                dve.wait_ge(taken, SETS + j * SETS + k + 1)
                dve.scalar_tensor_tensor(m.hot[:, SETS + k, :], stage(k)[:, 0:D], 1.0, a_source, ALU.mult, ALU.mult,
                                         accum_out=stage(k)[:, D:D + 1]).then_inc(scored, 1)
                dve.scalar_tensor_tensor(m.hot[:, 2 * SETS + k, :], stage(k)[:, 0:D], 1.0, a_target, ALU.mult, ALU.mult,
                                         accum_out=target_score[:, bass.ds(j * SETS + k, 1)]).then_inc(scored, 1)

            dve.sem_inc(product, SETS)
            with dve.Fori(0, turns) as j:
                for k in range(SETS):
                    hold(j, k)
                for k in range(SETS):
                    score(j, k)
                dve.wait_ge(scored, 2 * SETS * (j + 1))
            hold(turns, 0)
            score(turns, 0)

        @block.tensor
        def _(pe):
            def tile(j, k):
                pe.wait_ge(held, j * SETS + k + 1)
                pe.wait_ge(taken, j * SETS + k + 1)
                pe.matmul(m.psum[k][:, 0:D], m.hot[:, k, :], m.weights[:, D:2 * D], start=True, stop=True).then_inc(product, 1)

            pe.sem_inc(taken, SETS)
            with pe.Fori(0, turns) as j:
                for k in range(SETS):
                    tile(j, k)
            tile(turns, 0)

        @block.scalar
        def _(act):
            def tile(j, k):
                act.wait_ge(product, SETS + j * SETS + k + 1)
                act.copy(stage(k)[:, 0:D], m.psum[k][:, 0:D]).then_inc(taken, 1)

            for k in range(SETS):
                tile(0, k)
            with act.Fori(1, turns) as j:
                for k in range(SETS):
                    act.wait_ge(stored[k], 16 * j)
                    tile(j, k)
            act.wait_ge(stored[0], 16 * turns)
            tile(turns, 0)

        @block.sync
        def _(sp):
            def tile(j, k):
                sp.wait_ge(scored, 2 * (j * SETS + k + 1))
                sp.dma_start(m.att_table[bass.ds((j * SETS + k) * P, P), :], stage(k)).then_inc(stored[k], 16)

            with sp.Fori(0, turns) as j:
                for k in range(SETS):
                    tile(j, k)
            tile(turns, 0)
            sp.wait_ge(stored[0], 16 * (turns + 1))
            for k in range(1, SETS):
                sp.wait_ge(stored[k], 16 * turns)


def attend(nc, m, acc, neg_target, neg_max):
    with Stage(nc) as cs:
        (staged, begun, marked, turned, summed, scored, lowest, new_max, grown, powered, shrunk, back, weights,
         product, added, lower) = cs.sems("staged", "begun", "marked", "turned", "summed", "scored", "lowest", "new_max", "grown",
                                   "powered", "shrunk", "back", "weights", "product", "added", "lower")
        gathered, before = m.gathered, m.gathered_to
        m.gathered_to += 16 * TURNS
        block = cs.enter_context(nc.Block())
        mark = m.hot[:, 0:4, :]
        score = m.hot[:, 4:8, :]
        power = m.hot[:, 8:10, :]
        weight = m.hot[:, 10:14, :]
        lowered = m.hot[:, 14, :]
        turn_ps, back_ps, sums = m.psum[0:2], m.psum[2:4], m.psum[4:6]
        low = m.small[:, 480:484]
        neg = m.small[:, 484:488]
        drop = m.small[:, 488:492]
        factor = m.small[:, 492:496]
        one = lambda ring, u: ring[:, u % 4:u % 4 + 1]
        pair = lambda ring, u: ring[:, u % 4 - 1:u % 4 + 1]

        @block.gpsimd
        def _(pool):
            gather(pool, m, m.att_table, ROW, staged, begun, freed=product)

        @block.scalar
        def _(act):
            def stage(turn, q):
                act.copy(m.idx[:, q * QUARTER:(q + 1) * QUARTER],
                         m.edge_src[:, bass.ds(turn * UNROLL + q * QUARTER, QUARTER)]).then_inc(staged, 1)

            def steps(i, u, what, tile):
                c = i * UNROLL + u
                if what == "mark":
                    wait(act, turned, c - 3)
                    act.activation(mark[:, u % 4, :], m.iota[:, :], ACT.Abs, bias=m.edge_dst[:, bass.ds(c, 1)],
                                   scale=-1.0).then_inc(marked, 1)
                elif what == "sum":
                    act.wait_ge(turned, c + 1)
                    wait(act, powered, c - 3)
                    act.activation(score[:, u % 4, :], turn_ps[u % 2][:, 0:P], ACT.Identity,
                                   bias=m.target_score[:, bass.ds(tile, 1)]).then_inc(summed, 1)
                elif what == "stage" and u % QUARTER == 0:
                    q = (u // QUARTER + 2) % 4
                    ahead = i + 1 if q < 2 else i
                    if not isinstance(ahead, int) or 0 < ahead < TURNS:
                        act.wait_ge(turned, c - UNROLL // 2 + QUARTER)
                        stage(ahead, q)
                elif what == "power":
                    act.wait_ge(new_max, c + 1)
                    wait(act, back, c - 1)
                    act.activation(power[:, u % 2, :], score[:, u % 4, :], ACT.Exp, bias=one(neg, u)).then_inc(powered, 1)
                elif what == "pair back" and u % 2:
                    act.wait_ge(back, c + 1)
                    wait(act, product, c - 3)
                    act.copy(pair(weight, u), back_ps[u // 2 % 2][:, 0:2 * P].rearrange("p (k e) -> p k e", k=2)).then_inc(weights, 2)
                elif what == "pair shrink" and u % 2:
                    act.wait_ge(grown, c + 1)
                    wait(act, added, c - 3)
                    act.activation(pair(factor, u), pair(drop, u), ACT.Exp).then_inc(shrunk, 2)

            for q in range(4):
                stage(0, q)
            turns(nc, m, act, ((6, "power"), (0, "mark"), (1, "stage"), (7, "pair back"), (2, "sum"), (6, "pair shrink")), steps, ("sum",))

        @block.tensor
        def _(pe):
            def steps(i, u, what, tile):
                c = i * UNROLL + u
                if what == "turn":
                    pe.wait_ge(marked, c + 1)
                    wait(pe, summed, c - 1)
                    pe.matmul(turn_ps[u % 2][:, 0:P], mark[:, u % 4, :], lowered[:, :], start=True, stop=False)
                    pe.wait_ge(gathered[u % UNROLL], before + 16 * (i + 1 if u >= 0 else i))
                    pe.matmul(turn_ps[u % 2][:, 0:P], m.rows[:, u % UNROLL, D:D + 1].to_broadcast([P, P]), m.ident[:, :],
                              start=False, stop=True).then_inc(turned, 1)
                elif what == "back":
                    pe.wait_ge(powered, c + 1)
                    wait(pe, weights, c - 3)
                    half = u % 2 * P
                    pe.transpose(back_ps[u // 2 % 2][:, half:half + P], power[:, u % 2, :], m.ident[:, :]).then_inc(back, 1)
                else:
                    pe.wait_ge(weights, c + 1)
                    wait(pe, added, c - 1)
                    pe.matmul(sums[u % 2][:, 0:ROW], weight[:, u % 4, :], m.rows[:, u % UNROLL, :],
                              start=True, stop=True).then_inc(product, 1)

            pe.wait_ge(lower, 1)
            turns(nc, m, pe, ((1, "turn"), (6, "back"), (8, "sum")), steps)

        @block.vector
        def _(dve):
            def steps(i, u, what, tile):
                c = i * UNROLL + u
                if what == "add":
                    dve.wait_ge(product, c + 1)
                    dve.wait_ge(shrunk, c + 1)
                    wait(dve, added, c)
                    at = acc[:, bass.ds(tile * ROW, ROW)]
                    dve.scalar_tensor_tensor(at, at, one(factor, u), sums[u % 2][:, 0:ROW],
                                             ALU.mult, ALU.add).then_inc(added, 1)
                elif what == "pair score" and u % 2:
                    dve.wait_ge(summed, c + 1)
                    both = pair(score, u)
                    dve.scalar_tensor_tensor(both, both, LEAK, both, ALU.mult, ALU.max).then_inc(scored, 2)
                elif what == "pair lowest" and u % 2:
                    dve.wait_ge(scored, c + 1)
                    wait(dve, new_max, c - 3)
                    dve.tensor_reduce(pair(low, u), pair(score, u), AX.X, ALU.max, negate=True).then_inc(lowest, 2)
                elif what == "drop":
                    dve.wait_ge(lowest, c + 1)
                    wait(dve, new_max, c)
                    wait(dve, shrunk, c - 3)
                    dve.tensor_scalar(one(drop, u), one(low, u), neg_max[:, bass.ds(tile, 1)], 0.0,
                                      ALU.subtract, ALU.min).then_inc(grown, 1)
                elif what == "new":
                    wait(dve, powered, c - 3)
                    dve.wait_ge(grown, c + 1)
                    at = neg_max[:, bass.ds(tile, 1)]
                    dve.scalar_tensor_tensor(one(neg, u), one(low, u), at, one(low, u), ALU.min, ALU.min,
                                             accum_out=at).then_inc(new_max, 1)

            dve.tensor_scalar(lowered, m.ident[:, :], LOW, None, ALU.mult).then_inc(lower, 1)
            turns(nc, m, dve, ((3, "pair score"), (5, "drop"), (5, "new"), (3, "pair lowest"), (9, "add")), steps,
                  ("drop", "new", "add"))


def attention(nc, m, a, out):
    B = [b[:, 0:NPAD] for b in m.big]
    W = m.weights
    spread = lambda f, n: f.rearrange("(o d) -> o d", o=1).to_broadcast([P, n])
    target_score, neg_max = m.target_score, m.small[:, 64:64 + TILES + 1]
    load(nc, m, [(W[:, 0:D], a["L3_gnn_W_lin"]), (W[:, 2 * D:4 * D], spread(a["L3_gnn_a"], 2 * D)),
                 (W[:, 4 * D:5 * D], spread(a["L3_gnn_gamma"], D)), (W[:, 5 * D:6 * D], spread(a["L3_gnn_beta"], D))],
         zero=[m.big[1][:, 0:(TILES + 1) * ROW], target_score])

    with Stage(nc) as cs:
        turned = cs.sem("turned")
        block = cs.enter_context(nc.Block())

        @block.tensor
        def _(pe):
            pe.transpose(m.psum[0][:, 0:D], W[:, 0:D], m.ident[:, :]).then_inc(turned, 1)

        @block.scalar
        def _(act):
            act.wait_ge(turned, 1)
            act.copy(W[:, D:2 * D], m.psum[0][:, 0:D])

        @block.vector
        def _(dve):
            dve.memset(neg_max, -FLOOR)
            dve.memset(m.rows[:, 0:SETS, D + 1:D + 2], 1.0)

    attention_table(nc, m, B[0], lambda k: m.rows[:, k, :], target_score)
    attend(nc, m, m.big[1], target_score, neg_max)
    turn_tiles(nc, m, B[0], B[3])
    finish(nc, m, m.big[1], B[3], B[2], B[4], out)


def finish(nc, m, acc, x, y, tmp, out):
    shape = [P, TILES, D]
    view = lambda b: b.rearrange("p (t d) -> p t d", d=D)
    sums = acc[:, 0:TILES * ROW].rearrange("p (t r) -> p t r", r=ROW)
    x, y, tmp = view(x), view(y), view(tmp)
    z, mean, var = (m.small[:, 128 + 64 * n:128 + 64 * n + TILES] for n in range(3))
    gamma, beta = m.weights[:, 4 * D:5 * D], m.weights[:, 5 * D:6 * D]
    per_node = lambda v: v.unsqueeze(2).to_broadcast(shape)
    per_feature = lambda v: v.unsqueeze(1).to_broadcast(shape)
    with Stage(nc) as cs:
        step, asked, rooted, stored = cs.sems("step", "asked", "rooted", "stored")
        block = cs.enter_context(nc.Block())

        @block.vector
        def _(dve):
            steps = [0]

            def then(ins):
                steps[0] += 1
                ins.then_inc(step, 1)
                dve.wait_ge(step, steps[0])

            def norm(turn):
                then(dve.tensor_reduce(mean, y, AX.X, ALU.add))
                then(dve.tensor_scalar(mean, mean, 1.0 / D, None, ALU.mult))
                then(dve.tensor_tensor(y, y, per_node(mean), ALU.subtract))
                then(dve.tensor_tensor(tmp, y, y, ALU.mult))
                then(dve.tensor_reduce(var, tmp, AX.X, ALU.add))
                dve.tensor_scalar(var, var, 1.0 / D, None, ALU.mult).then_inc(asked, 1)
                dve.wait_ge(rooted, turn)
                then(dve.reciprocal(var, var))

            then(dve.tensor_scalar(z, sums[:, :, D + 1], 1e-30, None, ALU.max))
            then(dve.reciprocal(z, z))
            then(dve.tensor_tensor(y, sums[:, :, 0:D], per_node(z), ALU.mult))
            then(dve.tensor_tensor(y, y, x, ALU.add))
            norm(1)
            then(dve.tensor_tensor(y, y, per_node(var), ALU.mult))
            then(dve.tensor_tensor(y, y, per_feature(gamma), ALU.mult))
            then(dve.tensor_tensor(y, y, per_feature(beta), ALU.add))
            then(dve.tensor_tensor(y, y, x, ALU.add))
            norm(2)
            dve.tensor_tensor(y, y, per_node(var), ALU.mult).then_inc(asked, 1)

        @block.scalar
        def _(act):
            for turn in (1, 2):
                act.wait_ge(asked, turn)
                act.activation(var, var, ACT.Sqrt, bias=m.eps).then_inc(rooted, 1)

        @block.sync
        def _(sp):
            full = TILES - 1
            sp.wait_ge(asked, 3)
            sp.dma_start(out[0:full * P, :].rearrange("(t p) d -> p t d", p=P), y[:, 0:full, :]).then_inc(stored, 16)
            sp.dma_start(out[full * P:N, :], y[0:LAST, full, :]).then_inc(stored, 16)
            sp.wait_ge(stored, 32)


VECTORS = ["L0_gnn_b1", "L0_gnn_b2", "L0_gnn_gamma", "L0_gnn_beta", "L1_gnn_bn0_gamma", "L1_gnn_bn0_beta",
           "L1_gnn_b1", "L1_gnn_bn1_gamma", "L1_gnn_bn1_beta", "L1_gnn_b2", "L1_gnn_bn2_gamma", "L1_gnn_bn2_beta",
           "L2_gnn_b1", "L2_gnn_b2", "L2_gnn_b3", "L2_gnn_res_b"]


def build(nc, a, out):
    with ExitStack() as cs:
        m = Memory(nc, cs)
        vec = {name: m.par[:, n:n + 1] for n, name in enumerate(VECTORS)}
        B = [b[:, 0:NPAD] for b in m.big]
        acc_whole = m.big[1][:, 0:ACCW]
        W = m.weights

        make_constants(nc, m)
        edges = a["src"], a["dst"], a["edge_type_8"], a["edge_weight1"].rearrange("e o -> (e o)")
        load_columns(nc, m, *edges)
        pair_columns(nc, m)
        unsorted = nc.values_load(m.unsorted[0:1, 0:1], min_val=0, max_val=1)
        with nc.If(unsorted != 0):
            nc.all_engine_barrier()
            load_edges(nc, m, *edges)
            sort_edges(nc, m)
        with nc.Else():
            nc.all_engine_barrier()
            spread_columns(nc, m)
        edge_rows(nc, m)

        load_vectors(nc, m, a)
        turn_tiles(nc, m, B[4], B[0])
        load(nc, m, [(W[:, 0:D], a["L0_gnn_W1"]), (W[:, D:2 * D], a["L0_gnn_W2"]),
                     (B[4][:, 0:N], a["node_vec1"].rearrange("n o -> o n").to_broadcast([P, N]))],
             zero=[acc_whole, m.count[:, :], B[4][:, N:NPAD]])
        gather_sum(nc, m, a["x"], m.edge_src, m.big[1], scale_rows=m.edge_w, count=True)
        combine(nc, m, [(B[2], B[0], m.one_eps, B[1], ALU.mult, ALU.add)])
        linear(nc, m, W[:, 0:D], B[2], B[3], ACT.Relu, vec["L0_gnn_b1"])
        linear(nc, m, W[:, D:2 * D], B[3], B[2], ACT.Identity, vec["L0_gnn_b2"], times=B[4])
        batch_norm(nc, m, B[2], B[2], vec["L0_gnn_gamma"], vec["L0_gnn_beta"], ACT.Relu)
        combine(nc, m, [(B[2], B[0], 2.0, B[2], ALU.mult, ALU.add)])
        layer_norm(nc, m, B[2], B[0], B[3])

        degrees(nc, m, B[4])
        batch_norm(nc, m, B[0], B[2], vec["L1_gnn_bn0_gamma"], vec["L1_gnn_bn0_beta"])
        load(nc, m, [(W[:, 0:D], a["L1_gnn_W1"]), (W[:, D:2 * D], a["L1_gnn_W2"])])
        table = m.table[0:NPAD, :]
        for layer in (1, 2):
            x = B[2] if layer == 1 else B[3]
            if layer == 2:
                load(nc, m, [(W[:, 0:D], a["L1_gnn_W2"])])
            linear(nc, m, W[:, 0:D], x, B[1], times=B[4])
            write_table(nc, m, x, D, lambda k: m.rows[:, k, 0:D], lambda t: table[bass.ds(t * P, P), :], scale=m.dinv)
            gather_sum(nc, m, table, m.edge_src, m.big[1], norm=layer == 1)
            combine(nc, m, [(B[1], B[1], 1.0, B[4], ALU.mult, ALU.mult)])
            relu_bias(nc, m, B[1], B[3], vec[f"L1_gnn_b{layer}"])
            batch_norm(nc, m, B[3], B[3], vec[f"L1_gnn_bn{layer}_gamma"], vec[f"L1_gnn_bn{layer}_beta"])
        combine(nc, m, [(B[3], B[3], 1.0, B[2], ALU.mult, ALU.add), (B[3], B[3], 1.0, B[0], ALU.mult, ALU.add)])
        layer_norm(nc, m, B[3], B[0], B[2])

        load(nc, m, [(W[:, 0:D], a["L2_gnn_res_w"])])
        linear(nc, m, W[:, 0:D], B[0], B[2], bias=vec["L2_gnn_res_b"])
        for layer in (1, 2, 3):
            x = B[0] if layer == 1 else B[3]
            load(nc, m, [(W[:, 0:D], a[f"L2_gnn_root{layer}"])])
            linear(nc, m, W[:, 0:D], x, B[1])
            load(nc, m, [(W[:, :].rearrange("p (r d) -> p r d", d=D), a[f"L2_gnn_W{layer}"].rearrange("r p d -> p r d"))])
            by_tile = m.table.rearrange("(r n) d -> n r d", n=NPAD)
            write_table(nc, m, x, REL * D, lambda k: m.big[4][:, k * REL * D:(k + 1) * REL * D],
                        lambda t: by_tile[bass.ds(t * P, P), :, :])
            gather_sum(nc, m, m.table, m.edge_row, m.big[1], weight=m.edge_norm)
            relu_bias(nc, m, B[1], B[3], vec[f"L2_gnn_b{layer}"])
            combine(nc, m, [(B[3], B[3], 1.0, B[2], ALU.mult, ALU.add)])
        combine(nc, m, [(B[3], B[3], 1.0, B[0], ALU.mult, ALU.add)])
        layer_norm(nc, m, B[3], B[0], B[2])
        attention(nc, m, a, out)


def relu_bias(nc, m, x, out, bias):
    with Stage(nc) as cs:
        block = cs.enter_context(nc.Block())

        @block.scalar
        def _(act):
            act.activation(out, x, ACT.Relu, bias=bias)


def kernel(**inputs):
    import numpy as _np
    import concourse.bacc as _bacc
    from concourse import mybir as _mybir
    from concourse.bass_utils import run_bass_kernel_spmd as _run

    nc = _bacc.Bacc("TRN2", target_bir_lowering=False, num_devices=1)
    arrays, args = {}, {}
    for name, value in inputs.items():
        v = _np.ascontiguousarray(value)
        arrays[f"in_{name}"] = v
        args[name] = nc.dram_tensor(f"in_{name}", v.shape, _mybir.dt.from_np(v.dtype), kind="ExternalInput").ap()
    out = nc.dram_tensor("out", (N, D), F32, kind="ExternalOutput").ap()
    build(nc, args, out)
    r = _run(nc, [arrays], core_ids=[0])
    return r.results[0]["out"]
```
